# Optimizing a Trainium2 kernel written in Bass

```python
import numpy as np
import jax
import jax.numpy as jnp

def _softmax(x, axis=-1):
    return jax.nn.softmax(x, axis=axis)

def _gelu(x):
    return jax.nn.gelu(x, approximate=True)

def _silu(x):
    return jax.nn.silu(x)

def _sigmoid(x):
    return jax.nn.sigmoid(x)

def _layernorm(x, axis=-1, eps=1e-05):
    m = jnp.mean(x, axis=axis, keepdims=True)
    v = jnp.var(x, axis=axis, keepdims=True)
    return (x - m) / jnp.sqrt(v + eps)

def _scatter_add(tgt, idx, src, axis=0):
    return tgt.at[idx].add(src)

def _segment_sum(src, seg, n):
    return jax.ops.segment_sum(src, seg, n)
kernel_name = 'mk_vit_tower_d2_tok_img768_r4_0a89f5'

def setup_inputs(seed: int=0):
    np.random.seed(seed)
    _w = jnp.asarray

    def _rec_inputs():
        import jax
        import jax.numpy as jnp
        _rk = jax.random.key(seed)
        x = -0.000209053 + 0.999977 * jax.random.normal(jax.random.fold_in(_rk, 1), (8, 64, 112, 112), jnp.float32)
        return x
    x = _rec_inputs()

    def _L0_tok_setup():
        import jax, jax.numpy as jnp
        import numpy as np
        K = 3
        STRIDE = 2
        PAD = (K - 1) // 2
        key = jax.random.key(seed)
        k1, k2, k3 = jax.random.split(key, 3)
        B, C, H, W_ = (32, 64, 112, 112)
        DIM = 192
        x = jax.random.normal(k1, (B, C, H, W_), dtype=jnp.float32)
        W = jax.random.normal(k2, (DIM, C * K * K), dtype=jnp.float32) * 0.02
        b = jax.random.normal(k3, (DIM,), dtype=jnp.float32) * 0.02
        return {'x': x, 'W': W, 'b': b}
    _L0_tok_all = _L0_tok_setup()
    _L0_tok_in = {k: v for k, v in _L0_tok_all.items() if k in ('W', 'b')}
    del _L0_tok_all

    def _L0_attn_setup():
        import jax, jax.numpy as jnp
        import numpy as np
        B, N, C, H = (8, 1024, 192, 8)
        key = jax.random.key(seed)
        k1, k2, k3 = jax.random.split(key, 3)
        x = jax.random.normal(k1, (B, N, C), dtype=jnp.float32)
        W_qkv = jax.random.normal(k2, (C, 3 * C), dtype=jnp.float32) * 0.02
        W_proj = jax.random.normal(k3, (C, C), dtype=jnp.float32) * 0.02
        b_proj = jnp.zeros((C,), dtype=jnp.float32)
        temp = jnp.ones((H, 1, 1), dtype=jnp.float32)
        return {'x': x, 'W_qkv': W_qkv, 'W_proj': W_proj, 'b_proj': b_proj, 'temp': temp}
    _L0_attn_all = _L0_attn_setup()
    _L0_attn_in = {k: v for k, v in _L0_attn_all.items() if k in ('W_qkv', 'W_proj', 'b_proj', 'temp')}
    del _L0_attn_all

    def _L0_ffn_setup():
        import jax, jax.numpy as jnp
        import numpy as np
        ATOM = {'vm': 0, 'im': 1, 'cm': 2, 'sc': 3, 'cc': 4}
        TASK_PAIRS = [('vm', 'sc'), ('vm', 'cc'), ('im', 'sc'), ('im', 'cc'), ('cm', 'sc'), ('cm', 'cc')]
        SRC_IDX = np.array([[ATOM[l], ATOM[r]] for l, r in TASK_PAIRS], dtype=np.int32)
        DST_IDX = np.array([[ATOM[r], ATOM[l]] for l, r in TASK_PAIRS], dtype=np.int32)
        NCLS = 6
        NATOMS = 5

        def _l2norm(x, eps=1e-12):
            return x / jnp.clip(jnp.linalg.norm(x, axis=-1, keepdims=True), eps)
        key = jax.random.key(seed)
        ks = jax.random.split(key, 12)
        B, NPATCH, D, H = (64, 197, 192, 768)
        std = 0.02
        x = jax.random.normal(ks[0], (B, NCLS + NPATCH, D), dtype=jnp.float32)
        fc1_w = jax.random.normal(ks[1], (H, D), dtype=jnp.float32) * std
        fc1_b = jnp.zeros((H,), jnp.float32)
        fc2_w = jax.random.normal(ks[2], (D, H), dtype=jnp.float32) * std
        fc2_b = jnp.zeros((D,), jnp.float32)
        gate_pair = jax.random.normal(ks[3], (NCLS, 2, D), dtype=jnp.float32) * std
        atom_in_w = jax.random.normal(ks[4], (NATOMS, H, D), dtype=jnp.float32) * std
        atom_in_b = jax.random.normal(ks[5], (NATOMS, H), dtype=jnp.float32) * std
        atom_out_w = jax.random.normal(ks[6], (NATOMS, D, H), dtype=jnp.float32) * std
        atom_out_b = jax.random.normal(ks[7], (NATOMS, D), dtype=jnp.float32) * std
        balance_bias = jnp.zeros((NCLS, 2), jnp.float32)
        return {'x': x, 'fc1_w': fc1_w, 'fc1_b': fc1_b, 'fc2_w': fc2_w, 'fc2_b': fc2_b, 'gate_pair': gate_pair, 'atom_in_w': atom_in_w, 'atom_in_b': atom_in_b, 'atom_out_w': atom_out_w, 'atom_out_b': atom_out_b, 'balance_bias': balance_bias}
    _L0_ffn_all = _L0_ffn_setup()
    _L0_ffn_in = {k: v for k, v in _L0_ffn_all.items() if k in ('fc1_w', 'fc1_b', 'fc2_w', 'fc2_b', 'gate_pair', 'atom_in_w', 'atom_in_b', 'atom_out_w', 'atom_out_b', 'balance_bias')}
    del _L0_ffn_all

    def _L1_attn_setup():
        import jax, jax.numpy as jnp
        import numpy as np

        def _rotate_half(x):
            a, b = jnp.split(x, 2, axis=-1)
            return jnp.concatenate([-b, a], axis=-1)

        def _rope_tables(L, d, dtype):
            inv = 1.0 / 10000.0 ** (jnp.arange(0, d, 2, dtype=jnp.float32) / d)
            ang = jnp.arange(L, dtype=jnp.float32)[:, None] * inv[None, :]
            cos = jnp.repeat(jnp.cos(ang), 2, axis=-1)[None, :, None, :].astype(dtype)
            sin = jnp.repeat(jnp.sin(ang), 2, axis=-1)[None, :, None, :].astype(dtype)
            return (cos, sin)

        def _forward(X, Wq, Wk, Wv, Wu, Wg, Wo, prior_mu, prior_log_tau):
            B, L, D = X.shape
            h = prior_mu.shape[2]
            d = D // h
            eps = 1e-12
            q = (X @ Wq.T).reshape(B, L, h, d)
            k = (X @ Wk.T).reshape(B, L, h, d)
            v = (X @ Wv.T).reshape(B, L, h, d)
            u = (X @ Wu.T).reshape(B, L, h, d)
            gate = (X @ Wg.T).reshape(B, L, h, 3)
            t = jnp.arange(1, L + 1, dtype=X.dtype).reshape(1, L, 1, 1)
            log_tau = jnp.exp(jnp.clip(prior_log_tau, -50.0, 30.0))
            u_sum = jnp.cumsum(u, axis=1)
            bar_u = (log_tau * prior_mu + u_sum) / (log_tau + t)
            s_i = -jnp.sum(u * bar_u, axis=-1, keepdims=True) / np.float32(np.sqrt(d))
            cos, sin = _rope_tables(L, d, X.dtype)
            q = q * cos + _rotate_half(q) * sin
            k = k * cos + _rotate_half(k) * sin
            q = q / jnp.maximum(jnp.linalg.norm(q, axis=-1, keepdims=True), eps)
            k = k / jnp.maximum(jnp.linalg.norm(k, axis=-1, keepdims=True), eps)
            s_max = jax.lax.stop_gradient(jnp.max(s_i, axis=1, keepdims=True))
            exp_s = jnp.exp(s_i - s_max)
            E_t = jnp.cumsum(exp_s, axis=1)
            P_t = jnp.cumsum(s_i, axis=1)
            kv = jnp.einsum('blhd,blhe->blhde', k, v)
            F_t = jnp.cumsum(exp_s[..., None] * kv, axis=1)
            G_t = jnp.cumsum(s_i[..., None] * kv, axis=1)
            H_t = jnp.cumsum(kv, axis=1)
            sig1 = jax.nn.sigmoid(gate[..., 0:1])
            sigh = jax.nn.sigmoid(gate[..., 1:2])
            alpha = sigh / (E_t + eps)
            beta = (sig1 - sigh) / t
            gamma = -((beta * P_t + sigh) / t)
            M = alpha[..., None] * F_t + beta[..., None] * G_t + gamma[..., None] * H_t
            out = jnp.einsum('blhd,blhde->blhe', q, M)
            mu = jnp.mean(out, axis=-1, keepdims=True)
            var = jnp.mean(jnp.square(out - mu), axis=-1, keepdims=True)
            out = (out - mu) / jnp.sqrt(var + 1e-05)
            return out.reshape(B, L, D) @ Wo.T
        key = jax.random.key(seed)
        ks = jax.random.split(key, 7)
        B, L, D, h = (1, 256, 192, 12)
        d = D // h
        s = 0.02
        return {'X': jax.random.normal(ks[0], (B, L, D), jnp.float32), 'Wq': jax.random.normal(ks[1], (D, D), jnp.float32) * s, 'Wk': jax.random.normal(ks[2], (D, D), jnp.float32) * s, 'Wv': jax.random.normal(ks[3], (D, D), jnp.float32) * s, 'Wu': jax.random.normal(ks[4], (D, D), jnp.float32) * s, 'Wg': jax.random.normal(ks[5], (3 * h, D), jnp.float32) * s, 'Wo': jax.random.normal(ks[6], (D, D), jnp.float32) * s, 'prior_mu': jnp.zeros((1, 1, h, d), jnp.float32), 'prior_log_tau': jnp.zeros((1, 1, h, 1), jnp.float32)}
    _L1_attn_all = _L1_attn_setup()
    _L1_attn_in = {k: v for k, v in _L1_attn_all.items() if k in ('Wq', 'Wk', 'Wv', 'Wu', 'Wg', 'Wo', 'prior_mu', 'prior_log_tau')}
    del _L1_attn_all

    def _L1_ffn_setup():
        import jax, jax.numpy as jnp
        import numpy as np
        B, S, D, F, E = (8, 512, 192, 768, 16)
        CAP = 64
        EPS = 1e-06

        def _switch_moe_block(x, ln_w, w_router, wi, wo):
            var = jnp.mean(jnp.square(x.astype(jnp.float32)), axis=-1, keepdims=True)
            normed = (x * jax.lax.rsqrt(var + EPS)).astype(x.dtype) * ln_w
            logits = jnp.einsum('bsd,de->bse', normed.astype(jnp.float32), w_router.astype(jnp.float32))
            probs = jax.nn.softmax(logits, axis=-1)
            expert_idx = jnp.argmax(probs, axis=-1)
            onehot = jax.nn.one_hot(expert_idx, E, dtype=jnp.float32)
            priority = jnp.cumsum(onehot, axis=1)
            keep = onehot * (priority <= CAP)
            pos = (priority - 1.0).astype(jnp.int32)
            dispatch = keep[..., None] * jax.nn.one_hot(pos, CAP, dtype=jnp.float32)
            expert_in = jnp.einsum('bsec,bsd->becd', dispatch, normed)
            h = jax.nn.relu(jnp.einsum('becd,edf->becf', expert_in, wi))
            expert_out = jnp.einsum('becf,efd->becd', h, wo)
            combined = jnp.einsum('bsec,becd->bsd', dispatch, expert_out)
            routed = jnp.sum(dispatch, axis=(2, 3)) > 0
            next_states = jnp.where(routed[..., None], combined.astype(x.dtype), normed)
            router_prob = jnp.max(probs, axis=-1, keepdims=True).astype(x.dtype)
            return x + router_prob * next_states
        key = jax.random.key(seed)
        k_x, k_r, k_wi, k_wo = jax.random.split(key, 4)
        x = jax.random.normal(k_x, (B, S, D), dtype=jnp.float32)
        ln_w = jnp.ones((D,), dtype=jnp.float32)
        w_router = jax.random.normal(k_r, (D, E), dtype=jnp.float32) * 0.02
        wi = jax.random.normal(k_wi, (E, D, F), dtype=jnp.float32) * D ** (-0.5)
        wo = jax.random.normal(k_wo, (E, F, D), dtype=jnp.float32) * F ** (-0.5)
        return {'x': x, 'ln_w': ln_w, 'w_router': w_router, 'wi': wi, 'wo': wo}
    _L1_ffn_all = _L1_ffn_setup()
    _L1_ffn_in = {k: v for k, v in _L1_ffn_all.items() if k in ('ln_w', 'w_router', 'wi', 'wo')}
    del _L1_ffn_all
    return {'x': x, 'L0_tok_W': _L0_tok_in['W'], 'L0_tok_b': _L0_tok_in['b'], 'L0_attn_W_qkv': _L0_attn_in['W_qkv'], 'L0_attn_W_proj': _L0_attn_in['W_proj'], 'L0_attn_b_proj': _L0_attn_in['b_proj'], 'L0_attn_temp': _L0_attn_in['temp'], 'L0_ffn_fc1_w': _L0_ffn_in['fc1_w'], 'L0_ffn_fc1_b': _L0_ffn_in['fc1_b'], 'L0_ffn_fc2_w': _L0_ffn_in['fc2_w'], 'L0_ffn_fc2_b': _L0_ffn_in['fc2_b'], 'L0_ffn_gate_pair': _L0_ffn_in['gate_pair'], 'L0_ffn_atom_in_w': _L0_ffn_in['atom_in_w'], 'L0_ffn_atom_in_b': _L0_ffn_in['atom_in_b'], 'L0_ffn_atom_out_w': _L0_ffn_in['atom_out_w'], 'L0_ffn_atom_out_b': _L0_ffn_in['atom_out_b'], 'L0_ffn_balance_bias': _L0_ffn_in['balance_bias'], 'L1_attn_Wq': _L1_attn_in['Wq'], 'L1_attn_Wk': _L1_attn_in['Wk'], 'L1_attn_Wv': _L1_attn_in['Wv'], 'L1_attn_Wu': _L1_attn_in['Wu'], 'L1_attn_Wg': _L1_attn_in['Wg'], 'L1_attn_Wo': _L1_attn_in['Wo'], 'L1_attn_prior_mu': _L1_attn_in['prior_mu'], 'L1_attn_prior_log_tau': _L1_attn_in['prior_log_tau'], 'L1_ffn_ln_w': _L1_ffn_in['ln_w'], 'L1_ffn_w_router': _L1_ffn_in['w_router'], 'L1_ffn_wi': _L1_ffn_in['wi'], 'L1_ffn_wo': _L1_ffn_in['wo']}

def reference(x, L0_tok_W, L0_tok_b, L0_attn_W_qkv, L0_attn_W_proj, L0_attn_b_proj, L0_attn_temp, L0_ffn_fc1_w, L0_ffn_fc1_b, L0_ffn_fc2_w, L0_ffn_fc2_b, L0_ffn_gate_pair, L0_ffn_atom_in_w, L0_ffn_atom_in_b, L0_ffn_atom_out_w, L0_ffn_atom_out_b, L0_ffn_balance_bias, L1_attn_Wq, L1_attn_Wk, L1_attn_Wv, L1_attn_Wu, L1_attn_Wg, L1_attn_Wo, L1_attn_prior_mu, L1_attn_prior_log_tau, L1_ffn_ln_w, L1_ffn_w_router, L1_ffn_wi, L1_ffn_wo):
    import jax
    import jax.numpy as jnp

    def _L0_tok_ref(x, W, b):
        import jax, jax.numpy as jnp
        import numpy as np
        K = 3
        STRIDE = 2
        PAD = (K - 1) // 2
        dim = W.shape[0]
        C = x.shape[1]
        kernel = W.reshape(dim, C, K, K)
        y = jax.lax.conv_general_dilated(x, kernel, window_strides=(STRIDE, STRIDE), padding=[(PAD, PAD), (PAD, PAD)], dimension_numbers=('NCHW', 'OIHW', 'NCHW'))
        B, _, Hp, Wp = y.shape
        out = y.reshape(B, dim, Hp * Wp).transpose(0, 2, 1) + b
        return out

    def _L0_attn_ref(x, W_qkv, W_proj, b_proj, temp):
        import jax, jax.numpy as jnp
        import numpy as np
        B, N, C, H = (8, 1024, 192, 8)
        b, n, c = x.shape
        h = temp.shape[0]
        d = c // h
        qkv = (x @ W_qkv).reshape(b, n, h, d, 3)
        q, k, v = (qkv[..., 0], qkv[..., 1], qkv[..., 2])
        q = q / jnp.linalg.norm(q, axis=1, keepdims=True)
        k = k / jnp.linalg.norm(k, axis=1, keepdims=True)
        attn = jnp.einsum('bnhd,bnhe->bhde', q, k) * temp
        attn = jax.nn.softmax(attn, axis=-1)
        y = jnp.einsum('bhde,bnhe->bnhd', attn, v).reshape(b, n, c)
        return y @ W_proj + b_proj

    def _L0_ffn_ref(x, fc1_w, fc1_b, fc2_w, fc2_b, gate_pair, atom_in_w, atom_in_b, atom_out_w, atom_out_b, balance_bias):
        import jax, jax.numpy as jnp
        import numpy as np
        ATOM = {'vm': 0, 'im': 1, 'cm': 2, 'sc': 3, 'cc': 4}
        TASK_PAIRS = [('vm', 'sc'), ('vm', 'cc'), ('im', 'sc'), ('im', 'cc'), ('cm', 'sc'), ('cm', 'cc')]
        SRC_IDX = np.array([[ATOM[l], ATOM[r]] for l, r in TASK_PAIRS], dtype=np.int32)
        DST_IDX = np.array([[ATOM[r], ATOM[l]] for l, r in TASK_PAIRS], dtype=np.int32)
        NCLS = 6
        NATOMS = 5

        def _l2norm(x, eps=1e-12):
            return x / jnp.clip(jnp.linalg.norm(x, axis=-1, keepdims=True), eps)
        src = jnp.asarray(SRC_IDX)
        dst = jnp.asarray(DST_IDX)
        D = x.shape[-1]
        H = atom_in_w.shape[1]
        cls_tokens = x[:, :NCLS]
        patch_tokens = x[:, NCLS:]
        patch_out = jax.nn.gelu(patch_tokens @ fc1_w.T + fc1_b, approximate=False) @ fc2_w.T + fc2_b
        gate_in = _l2norm(cls_tokens.astype(jnp.float32))
        gate_w = _l2norm(gate_pair.astype(jnp.float32))
        gate_logits = jnp.einsum('bnd,nrd->bnr', gate_in, gate_w) + balance_bias[None]
        route_probs = jax.nn.softmax(gate_logits, axis=-1)
        chosen_route = jnp.argmax(route_probs, axis=-1)
        hid_all = jax.nn.gelu(jnp.einsum('bnd,ahd->bnah', cls_tokens, atom_in_w) + atom_in_b[None, None], approximate=False)
        sh_pair = hid_all[:, jnp.arange(NCLS)[:, None], src, :]
        route_out_w = atom_out_w[dst.reshape(-1)].reshape(NCLS, 2, D, H)
        route_candidates = jnp.einsum('bnrh,nrdh->bnrd', sh_pair, route_out_w) + atom_out_b[dst][None]
        chosen_w = jnp.take_along_axis(route_probs, chosen_route[..., None], axis=-1)
        chosen_cand = jnp.take_along_axis(route_candidates, chosen_route[:, :, None, None], axis=2)[:, :, 0]
        cls_out = chosen_cand * chosen_w.astype(chosen_cand.dtype)
        return jnp.concatenate([cls_out, patch_out], axis=1)

    def _L1_attn_ref(X, Wq, Wk, Wv, Wu, Wg, Wo, prior_mu, prior_log_tau):
        import jax, jax.numpy as jnp
        import numpy as np

        def _rotate_half(x):
            a, b = jnp.split(x, 2, axis=-1)
            return jnp.concatenate([-b, a], axis=-1)

        def _rope_tables(L, d, dtype):
            inv = 1.0 / 10000.0 ** (jnp.arange(0, d, 2, dtype=jnp.float32) / d)
            ang = jnp.arange(L, dtype=jnp.float32)[:, None] * inv[None, :]
            cos = jnp.repeat(jnp.cos(ang), 2, axis=-1)[None, :, None, :].astype(dtype)
            sin = jnp.repeat(jnp.sin(ang), 2, axis=-1)[None, :, None, :].astype(dtype)
            return (cos, sin)

        def _forward(X, Wq, Wk, Wv, Wu, Wg, Wo, prior_mu, prior_log_tau):
            B, L, D = X.shape
            h = prior_mu.shape[2]
            d = D // h
            eps = 1e-12
            q = (X @ Wq.T).reshape(B, L, h, d)
            k = (X @ Wk.T).reshape(B, L, h, d)
            v = (X @ Wv.T).reshape(B, L, h, d)
            u = (X @ Wu.T).reshape(B, L, h, d)
            gate = (X @ Wg.T).reshape(B, L, h, 3)
            t = jnp.arange(1, L + 1, dtype=X.dtype).reshape(1, L, 1, 1)
            log_tau = jnp.exp(jnp.clip(prior_log_tau, -50.0, 30.0))
            u_sum = jnp.cumsum(u, axis=1)
            bar_u = (log_tau * prior_mu + u_sum) / (log_tau + t)
            s_i = -jnp.sum(u * bar_u, axis=-1, keepdims=True) / np.float32(np.sqrt(d))
            cos, sin = _rope_tables(L, d, X.dtype)
            q = q * cos + _rotate_half(q) * sin
            k = k * cos + _rotate_half(k) * sin
            q = q / jnp.maximum(jnp.linalg.norm(q, axis=-1, keepdims=True), eps)
            k = k / jnp.maximum(jnp.linalg.norm(k, axis=-1, keepdims=True), eps)
            s_max = jax.lax.stop_gradient(jnp.max(s_i, axis=1, keepdims=True))
            exp_s = jnp.exp(s_i - s_max)
            E_t = jnp.cumsum(exp_s, axis=1)
            P_t = jnp.cumsum(s_i, axis=1)
            kv = jnp.einsum('blhd,blhe->blhde', k, v)
            F_t = jnp.cumsum(exp_s[..., None] * kv, axis=1)
            G_t = jnp.cumsum(s_i[..., None] * kv, axis=1)
            H_t = jnp.cumsum(kv, axis=1)
            sig1 = jax.nn.sigmoid(gate[..., 0:1])
            sigh = jax.nn.sigmoid(gate[..., 1:2])
            alpha = sigh / (E_t + eps)
            beta = (sig1 - sigh) / t
            gamma = -((beta * P_t + sigh) / t)
            M = alpha[..., None] * F_t + beta[..., None] * G_t + gamma[..., None] * H_t
            out = jnp.einsum('blhd,blhde->blhe', q, M)
            mu = jnp.mean(out, axis=-1, keepdims=True)
            var = jnp.mean(jnp.square(out - mu), axis=-1, keepdims=True)
            out = (out - mu) / jnp.sqrt(var + 1e-05)
            return out.reshape(B, L, D) @ Wo.T
        return _forward(X, Wq, Wk, Wv, Wu, Wg, Wo, prior_mu, prior_log_tau)

    def _L1_ffn_ref(x, ln_w, w_router, wi, wo):
        import jax, jax.numpy as jnp
        import numpy as np
        B, S, D, F, E = (8, 512, 192, 768, 16)
        CAP = 64
        EPS = 1e-06

        def _switch_moe_block(x, ln_w, w_router, wi, wo):
            var = jnp.mean(jnp.square(x.astype(jnp.float32)), axis=-1, keepdims=True)
            normed = (x * jax.lax.rsqrt(var + EPS)).astype(x.dtype) * ln_w
            logits = jnp.einsum('bsd,de->bse', normed.astype(jnp.float32), w_router.astype(jnp.float32))
            probs = jax.nn.softmax(logits, axis=-1)
            expert_idx = jnp.argmax(probs, axis=-1)
            onehot = jax.nn.one_hot(expert_idx, E, dtype=jnp.float32)
            priority = jnp.cumsum(onehot, axis=1)
            keep = onehot * (priority <= CAP)
            pos = (priority - 1.0).astype(jnp.int32)
            dispatch = keep[..., None] * jax.nn.one_hot(pos, CAP, dtype=jnp.float32)
            expert_in = jnp.einsum('bsec,bsd->becd', dispatch, normed)
            h = jax.nn.relu(jnp.einsum('becd,edf->becf', expert_in, wi))
            expert_out = jnp.einsum('becf,efd->becd', h, wo)
            combined = jnp.einsum('bsec,becd->bsd', dispatch, expert_out)
            routed = jnp.sum(dispatch, axis=(2, 3)) > 0
            next_states = jnp.where(routed[..., None], combined.astype(x.dtype), normed)
            router_prob = jnp.max(probs, axis=-1, keepdims=True).astype(x.dtype)
            return x + router_prob * next_states
        return _switch_moe_block(x, ln_w, w_router, wi, wo)
    h = _L0_tok_ref(x, L0_tok_W, L0_tok_b)
    h = h + _L0_attn_ref(_layernorm(h, axis=-1), L0_attn_W_qkv, L0_attn_W_proj, L0_attn_b_proj, L0_attn_temp)
    h = h + _L0_ffn_ref(_layernorm(h, axis=-1), L0_ffn_fc1_w, L0_ffn_fc1_b, L0_ffn_fc2_w, L0_ffn_fc2_b, L0_ffn_gate_pair, L0_ffn_atom_in_w, L0_ffn_atom_in_b, L0_ffn_atom_out_w, L0_ffn_atom_out_b, L0_ffn_balance_bias)
    h = h + _L1_attn_ref(_layernorm(h, axis=-1), L1_attn_Wq, L1_attn_Wk, L1_attn_Wv, L1_attn_Wu, L1_attn_Wg, L1_attn_Wo, L1_attn_prior_mu, L1_attn_prior_log_tau)
    h = h + _L1_ffn_ref(_layernorm(h, axis=-1), L1_ffn_ln_w, L1_ffn_w_router, L1_ffn_wi, L1_ffn_wo)
    return h

_drawn_inputs = setup_inputs


def setup_inputs(seed=0):
    import zlib

    import numpy as np

    out = dict(_drawn_inputs(seed))
    spreads = {'L0_attn_b_proj': (0.0, 0.1),
     'L0_attn_temp': (1.0, 0.6),
     'L0_ffn_fc1_b': (0.0, 0.1),
     'L0_ffn_fc2_b': (0.0, 0.1),
     'L0_ffn_balance_bias': (0.0, 0.8),
     'L1_attn_prior_mu': (0.0, 0.8),
     'L1_attn_prior_log_tau': (0.0, 0.8),
     'L1_ffn_ln_w': (1.0, 0.6)}
    factors = {'L0_ffn_gate_pair': 64.0,
     'L0_ffn_atom_in_w': 8.0,
     'L0_ffn_atom_in_b': 8.0,
     'L0_ffn_atom_out_w': 8.0,
     'L0_ffn_atom_out_b': 44.25,
     'L1_attn_Wq': 4.623,
     'L1_attn_Wk': 4.652,
     'L1_attn_Wv': 4.63,
     'L1_attn_Wu': 5.416,
     'L1_attn_Wg': 8.0,
     'L1_attn_Wo': 4.554}
    for name, (base, spread) in spreads.items():
        noise = np.random.default_rng([zlib.crc32(name.encode()), seed]).standard_normal(out[name].shape)
        drawn = base * np.exp(spread * noise) if base else spread * noise
        out[name] = jnp.asarray(drawn.astype(out[name].dtype))
    for name, factor in factors.items():
        out[name] = (out[name] * factor).astype(out[name].dtype)
    return out
```

```python
from contextlib import ExitStack

import numpy as np

import concourse.bass as bass
from concourse import mybir

ALU = mybir.AluOpType
ACT = mybir.ActivationFunctionType
AX = mybir.AxisListType
F32 = mybir.dt.float32
U32 = mybir.dt.uint32

B, CIN, IMG = 8, 64, 112
D = 192
DH = D // 2
OUTW = IMG // 2
T = 2 * OUTW
L = OUTW * OUTW
NC = L // T
NQ = NC // 4
SLAB = 5
HA = 8
F = 768
FT = F // 128
HL, HD = 12, 16
HP = 32
NCLS, NAT = 6, 5
E, CAP = 16, 64
RN, SD, MEAN, PROB = D, D + 1, D + 2, D + 3
ROW = D + 4
TPASS = 5
FAR = float(1 << 20)
NEG = -1.0e30
STAGE_COLUMNS = 10752
MIX_COLUMNS = 2692
GROUPS = {
    "attend": "att o3 vs v3 qkT",
    "mixing": "gram gk prodk prodq t1sb mix att0 norm0",
    "hidden": "hid",
    "class": "cpre chid cprod xc cbias cres",
    "others": "ug usum uprod lg onehot prio rtmp cum pick xo ob xg",
}


def pack_plan():
    return [
        ("conv01", 128, 3 * D), ("conv2", 64, 3 * D), ("tok_b", T, D),
        ("wq0", DH, 2 * D), ("wk0", DH, 2 * D), ("wvT", DH, 2 * D), ("wproj", DH, 2 * D), ("bproj", T, D),
        ("temp", DH, 2), ("offblock", DH, DH),
        ("fc1", DH, 2 * F), ("fc1_b", 128, FT), ("fc2", 128, FT * D), ("fc2_b", T, D),
        ("wqkv", DH, 2 * 3 * D), ("wug", DH, 2 * (D + 2 * HL)), ("wo", DH, 2 * D),
        ("mu", T, D), ("logtau", T, HL), ("lnw", 128, D), ("lnwT", DH, 2), ("router", DH, 2 * E),
        ("ident", 128, 128), ("tri", T, T), ("last", T, T), ("ones", 128, 128), ("zeros", 128, ROW),
        ("reset", T, E * NC), ("cos", T, NC * HD // 2), ("sin", T, NC * HD // 2), ("pos", T, NC),
        ("iotae", T, E), ("iota128", T, 128), ("tokid", T, B * NC), ("poff", T, B), ("eps", 128, 2),
        ("gate", NCLS, 2 * D), ("bal", NCLS, 2), ("out_b", NCLS, 2 * D), ("in_b", 128, NAT * FT),
        ("atom_in", DH, 2 * NAT * F), ("atom_out", 128, NAT * FT * D),
    ]


def pack_columns():
    at, where = 0, {}
    for name, p, n in pack_plan():
        where[name] = (p, at, n)
        at += n
    return where, at


class Steps:

    def __init__(self, sem, names):
        self.sem, self.names, self.at = sem, names.split(), 0

    def mark(self, instruction, name):
        assert self.names[self.at % len(self.names)] == name, (name, self.names, self.at)
        instruction.then_inc(self.sem, 1)
        self.at += 1

    def value(self, done, name):
        return done * len(self.names) + self.names.index(name) + 1


def build_tower(nc, xin, packed, out, rows, wi, wo_e, nb=B):
    where, total = pack_columns()
    ctx = ExitStack()
    with ctx:
        def sb(name, shape, dt=F32):
            return ctx.enter_context(nc.sbuf_tensor(name, shape, dt))

        def sem(name):
            return ctx.enter_context(nc.semaphore(name))

        W = sb("W", [128, total])
        PS = ctx.enter_context(nc.psum_tensor("PS", [128, 8, 512], F32))

        def w(name):
            p, at, n = where[name]
            return W[0:p, at:at + n]

        def bank(k, p, n):
            return PS[0:p, k, 0:n]

        def spread(ap, axis, n):
            ap = ap.unsqueeze(axis)
            shape = list(ap.shape)
            shape[axis] = n
            return ap.broadcast_to(shape)

        conv01 = w("conv01").rearrange("p (k n) -> p k n", k=3)
        conv2 = w("conv2").rearrange("p (k n) -> p k n", k=3)
        halves = {n: w(n).rearrange("p (k n) -> p k n", k=2)
                  for n in ("wq0", "wk0", "wvT", "wproj", "fc1", "wqkv", "wug", "wo", "router", "atom_in")}
        fc2 = w("fc2").rearrange("p (k n) -> p k n", k=FT)
        atom_out = w("atom_out").rearrange("p (a k n) -> p a k n", a=NAT, k=FT)
        ident, tri, last, ones, zeros = w("ident"), w("tri"), w("last"), w("ones"), w("zeros")
        cos = w("cos").rearrange("p (c d) -> p c d", d=HD // 2)
        sin = w("sin").rearrange("p (c d) -> p c d", d=HD // 2)
        eps_ln, eps_rms = w("eps")[:, 0:1], w("eps")[:, 1:2]

        U = sb("U", [128, STAGE_COLUMNS])
        top = {}

        def stage(name, shape):
            n = int(np.prod(shape[1:]))
            group = next(g for g, names in GROUPS.items() if name in names.split())
            at = top.setdefault(group, MIX_COLUMNS if group in ("others", "class") else 0)
            top[group] = at + n
            assert top[group] <= STAGE_COLUMNS, name
            flat = U[0:shape[0], at:at + n]
            letters = "abcd"[:len(shape) - 1]
            return flat.rearrange(f"p ({' '.join(letters)}) -> p {' '.join(letters)}",
                                  **dict(zip(letters, shape[1:])))

        h = sb("h", [T, NC, ROW])
        hx = h[:, :, 0:D]
        xs = sb("xs", [128, 2, 3, SLAB * OUTW])
        xg = stage("xg", [T, 4, D])
        xh = sb("xh", [T, 4, D])
        xT = sb("xT", [DH, 2, 4, T])
        bns = sb("bns", [T, 4, 6])
        bnv = sb("bnv", [T, 4, 2])
        mv = [sb(f"mv{n}", [T, NC, 2]) for n in range(4)]
        rs = [sb(f"rs{n}", [T, NC]) for n in range(4)]
        gram = stage("gram", [DH, 2, D])
        gk = stage("gk", [DH, 2, D])
        prodk = stage("prodk", [DH, 2, D])
        prodq = stage("prodq", [DH, 2, D])
        norm0 = stage("norm0", [DH, D + 2])
        att0 = stage("att0", [DH, 2, DH])
        rowm = sb("rowm", [DH, 2])
        rsum = sb("rsum", [DH, 2])
        t1sb = stage("t1sb", [DH, 2, D])
        mix = stage("mix", [DH, 2, D])
        hid = stage("hid", [128, FT, 4, T])

        gate = w("gate").rearrange("p (r n) -> p r n", r=2)
        gss = sb("gss", [NCLS, 2])
        xc = stage("xc", [NCLS, D])
        xcT = sb("xcT", [DH, 2, NCLS])
        cprod = stage("cprod", [NCLS, 3, D])
        csum = sb("csum", [NCLS, 3])
        clog = sb("clog", [NCLS, 2])
        cext = sb("cext", [NCLS, 2])
        cflag = sb("cflag", [NCLS, 2])
        cdiag = sb("cdiag", [NCLS, 2, NCLS])
        cflagb = sb("cflagb", [128, 2 * NCLS])
        cpre = stage("cpre", [128, NAT * FT, NCLS])
        chid = stage("chid", [128, NAT, FT, NCLS])
        csel = sb("csel", [128, NAT, FT, NCLS])
        cbias = stage("cbias", [NCLS, D])
        cres = stage("cres", [NCLS, D])

        GU = D + 2 * HL
        ug = stage("ug", [T, 4, GU])
        usum = stage("usum", [T, 4, D])
        uprod = stage("uprod", [T, 4, D])
        sraw = sb("sraw", [T, 4, HL])
        scoef = sb("scoef", [T, NC, HL])
        taumu = w("mu")
        tau = sb("tau", [T, HL])
        invt = sb("invt", [T, NC])
        gates = sb("gates", [T, NC, 2 * HL])
        es = sb("es", [T, 2 * HL, NC])
        cum = stage("cum", [T, 2 * HL, NC])
        smax = sb("smax", [T, HL])
        smaxT = sb("smaxT", [HL, 1])
        sdiag = sb("sdiag", [HL, HL])
        coef = sb("coef", [T, 3, HL, NC])
        qk = sb("qk", [T, 4, 2 * HL, HP])
        nrm = sb("nrm", [T, 4, 2 * HL])
        cq = sb("cq", [T, 4, HL, 3])
        ck = sb("ck", [T, 4, HL, 3])
        att = stage("att", [T, 2, 4, 3, T])
        rope1 = U[0:T, 0:4 * 2 * D].rearrange("p (c h d) -> p c h d", c=4, h=2 * HL)
        o3_at = top["attend"]
        o3 = stage("o3", [T, 4, HL, 3, HD])
        rope2 = U[0:T, o3_at:o3_at + 4 * 2 * D].rearrange("p (c h d) -> p c h d", c=4, h=2 * HL)
        vs = stage("vs", [T, 4, D])
        osum = vs
        v3 = stage("v3", [T, 4, HL, 3, HD])
        qkT = stage("qkT", [128, 4, 2, 3, T])
        state = sb("state", [128, 2, 3, 4, 3 * HD])
        ost = sb("ost", [T, 4, HL])
        oT = xT

        lg = stage("lg", [T, E, NC])
        onehot = stage("onehot", [T, E, NC])
        prio = stage("prio", [T, E, NC])
        rtmp = stage("rtmp", [T, E, NC])
        rmax = sb("rmax", [T, NC])
        prob = sb("prob", [T, NC])
        prs = sb("prs", [T, NC])
        rn = sb("rn", [T, NC])
        posx = sb("posx", [T, NC])
        pick = stage("pick", [T, 4, 128])
        slots = sb("slots", [128, B // 2, E])
        xo = stage("xo", [T, 4, D])
        ob = stage("ob", [T, 4, D])

        at_in, at_out = where["atom_in"][1], where["atom_out"][1]
        w1 = [W[0:DH, at_in + s * 2 * F:at_in + (s + 1) * 2 * F].rearrange("p (k n) -> p k n", k=2) for s in range(2)]
        w2 = [W[:, at_out + s * FT * D:at_out + (s + 1) * FT * D].rearrange("p (k n) -> p k n", k=FT) for s in range(2)]
        mh = W[:, at_out + 2 * FT * D:at_out + 2 * FT * D + FT * 512].rearrange("p (k n) -> p k n", k=FT)
        mrow_at = at_in + 4 * F
        mrow = [W[:, mrow_at + s * 4 * ROW:mrow_at + (s + 1) * 4 * ROW].rearrange("p (k n) -> p k n", k=4)
                for s in range(2)]
        mT_at = mrow_at + 8 * ROW
        mT = W[0:DH, mT_at:mT_at + 2 * 512].rearrange("p (k n) -> p k n", k=2)
        mx = W[:, mT_at + 2 * 512:mT_at + 2 * 512 + 4 * D].rearrange("p (k n) -> p k n", k=4)
        assert mT_at + 2 * 512 + 4 * D <= at_in + 2 * NAT * F and FT * (2 * D + 512) <= NAT * FT * D
        my = [U[:, s * 4 * D:(s + 1) * 4 * D].rearrange("p (k n) -> p k n", k=4) for s in range(2)]
        gidx = sb("gidx", [128, E + 2, B // 2], U32)
        sidx = sb("sidx", [128, E, B // 2], U32)
        gi = [sb(f"gi{s}", [128, B // 2], U32) for s in range(2)]
        si = [sb(f"si{s}", [128, B // 2], U32) for s in range(2)]
        empty = sb("empty", [128, B // 2, E])

        S = {n: sem(n) for n in (
            "held packed_in x_in0 x_in1 leads_given setup_done image_done "
            "conv_done conv_out xg_ready gram_read xh_ready turned xt_ready mix_done bias_in att_rsum h1_ready "
            "fc1_done gelu_done patches_done h2_ready ug_done ug_out gates_kept us_start us_done us_out uprod_done s_kept "
            "qk_done v_done rope_done qk_ready v_out squared rn_ready c_ready v3_ready qkt_done qkt_out "
            "s_done s_out st_done st_out o_done o_out osum_ready osum_used ctr_ready osq_out ovar osd_out orn oln_ready "
            "ot_done ot_out wo_done h3_ready lg_done lg_out pick_ready slots_done xn_ready xo_ready res_ready out_written "
            "rows_written x_kept gathered0 gathered1 w1_in0 w1_in1 w2_in0 w2_in1 index_ready gi_ready si_ready scattered0 scattered1 "
            "moe_x moe_h moe_turned moe_xt moe_f moe_ra moe_rd moe_o moe_y").split()}
        dA = Steps(sem("vector_conv"), "stat0 agg0 keep0 rstd0 stat1 agg1 keep1 rstd1")
        aA = Steps(sem("scalar_conv"), "sd0 sd1")
        dB = Steps(sem("vector_mix"), "g0 g1 g2 gk pk pq rnorm rqt l0 l1 l2 rowm rsum att t1 mix")
        pB = Steps(sem("tensor_mix"), "mirror gw qk t1 mix")
        aB = Steps(sem("scalar_mix"), "norm exp")
        dC = Steps(sem("vector_stats2"), "stat0 agg0 keep0 stat1 agg1 keep1")
        dR2 = Steps(sem("vector_rstd2"), "rstd")
        aR2 = Steps(sem("scalar_sd2"), "sd")
        dE = Steps(sem("vector_class"), "xc prod sq sum nmax nrec log flag0 flag1 max min diff p1 p "
                                        "diag0 diag1 flags pre sel bias0 bias res0 res")
        aE = Steps(sem("scalar_class"), "xcT norm exp gelu")
        pE = Steps(sem("tensor_class"), "turned hidden flags out")
        dD = Steps(sem("vector_stats3"), "stat0 agg0 keep0 stat1 agg1 keep1")
        dR3 = Steps(sem("vector_rstd3"), "class stat agg rstd")
        aR3 = Steps(sem("scalar_sd3"), "sd")
        dG = Steps(sem("vector_sums"), "max maxT diag shift scan0 scan1 excl sum eps einv al be0 be ga0 ga1 ga")
        pG = Steps(sem("tensor_sums"), "maxT max sums")
        aG = Steps(sem("scalar_sums"), "exp gates state0")
        dH = Steps(sem("vector_attend"), "ss nmax nrec pss0 pmean0 prn0 pss1 pmean1 prn1 stat0 agg0 keep0 stat1 agg1 keep1")
        lH = Steps(sem("pool_attend"), "k0 k1 k2 q0 q1 a0 a1")
        dI = Steps(sem("vector_rms"), "one_sd mean rstd sq ms rn keep")
        aI = Steps(sem("scalar_rms"), "sd rms")
        dR = Steps(sem("vector_route"), "scale max shift eq first lowest onehot psum prob prs keepp scan excl prio "
                                        "under keep pz pos posx")
        aR = Steps(sem("scalar_route"), "exp")
        pR = Steps(sem("tensor_route"), "sums")
        dS = Steps(sem("vector_setup"), "pad state sel slots gsq gss nmax nrec gate router tau taumu s0 s1 s2 invt")
        aS = Steps(sem("scalar_setup"), "gnorm tau")
        dM = Steps(sem("vector_indices"), "zero empty gather minus1")

        block = ctx.enter_context(nc.Block())
        LEADS = 5

        def ch(t, i, c, n=1):
            return t[:, bass.ds(4 * i + c, n)]

        def one(ap):
            return ap.rearrange("p a n -> p (a n)")

        def hold(eng):
            eng.sem_inc(S["held"], 1)

        def give_leads(eng, **leads):
            for name, n in leads.items():
                eng.sem_inc(S[name], n)
            eng.sem_inc(S["leads_given"], 1)
            eng.wait_ge(S["leads_given"], LEADS)

        @block.sync
        def _(sp):
            sp.dma_start(W[:, :], packed).then_inc(S["packed_in"], 16)
            give_leads(sp)
            sp.wait_ge(S["packed_in"], 16)
            sp.dma_start(rows[0:1, :], zeros[0:1, :]).then_inc(S["rows_written"], 16)
            with sp.Fori(0, nb) as b:
                with sp.Fori(0, NQ) as i:
                    g = b * NQ + i
                    for p in range(2):
                        sp.wait_ge(S["conv_done"], 2 * g + p + 1)
                        sp.dma_start(xs[:, p, :, :],
                                     xin[bass.ds(b, 1), :, :, bass.ds((8 * i + 4 * p) * OUTW, SLAB * OUTW)]
                                     .rearrange("b p v r -> p (b v) r")).then_inc(S[f"x_in{p}"], 16)
            sp.wait_ge(S["image_done"], nb + 1)
            with sp.Fori(0, E // 2) as k2:
                for s in range(2):
                    e = 2 * k2 + s
                    sp.wait_ge(S["moe_o"], 2 * e + 1)
                    sp.dma_start(w1[s], wi[bass.ds(e, 1)].rearrange("a p (k n) -> p (a k) n", k=2))\
                        .then_inc(S[f"w1_in{s}"], 16)
                    sp.dma_start(w2[s], wo_e[bass.ds(e, 1)].rearrange("a p (k n) -> p (a k) n", k=FT))\
                        .then_inc(S[f"w2_in{s}"], 16)

        @block.tensor
        def _(pe):
            mm, tr = nc.tensor.matmul, nc.tensor.transpose
            pe.wait_ge(S["packed_in"], 16)
            give_leads(pe, conv_done=2, gram_read=2, turned=2, mix_done=2, st_done=4, moe_turned=1, moe_f=6, moe_o=3)

            def turn(q):
                for p in range(2):
                    pe.wait_ge(S["xt_ready"], 2 * q + p + 1)
                    pe.wait_ge(S["xh_ready"], 2 * q + p + 1)
                    for j in range(2):
                        for k in range(2):
                            t = tr(PS[0:DH, p, (2 * k + j) * T:(2 * k + j + 1) * T],
                                   xh[:, 2 * p + j, k * DH:(k + 1) * DH], ident[0:T, 0:T])
                    t.then_inc(S["turned"], 1)

            def tile_pair(p, bk, x, weight, n, at=0):
                for j in range(2):
                    for k in range(2):
                        m = mm(PS[0:T, bk, j * n:(j + 1) * n], x[:, k, 2 * p + j, :], weight[:, k, at:at + n],
                               start=k == 0, stop=k == 1)
                return m

            with pe.Fori(0, nb) as b:
                pe.wait_ge(S["image_done"], b + 1)
                mm(bank(4, DH, D), zeros[0:T, 0:DH], zeros[0:T, 0:D], start=True, stop=False, skip_group_check=True)
                mm(bank(5, DH, DH), zeros[0:T, 0:DH], zeros[0:T, 0:DH], start=True, stop=False, skip_group_check=True)
                with pe.Fori(0, NQ) as i:
                    g = b * NQ + i
                    for p in range(2):
                        pe.wait_ge(S["conv_out"], 2 * g + p + 1)
                        pe.wait_ge(S[f"x_in{p}"], 16 * g + 16)
                        for j in range(2):
                            o = PS[0:T, 6 + p, j * D:(j + 1) * D]
                            for kx in range(3):
                                mm(o, xs[:, p, kx, 2 * j * OUTW:(2 * j + 2) * OUTW], conv01[:, kx, :],
                                   start=kx == 0, stop=False)
                            for kx in range(3):
                                m = mm(o, xs[0:CIN, p, kx, (2 * j + 1) * OUTW:(2 * j + 3) * OUTW], conv2[:, kx, :],
                                       start=False, stop=kx == 2)
                        m.then_inc(S["conv_done"], 1)
                    for p in range(2):
                        pe.wait_ge(S["xg_ready"], 2 * g + p + 1)
                        for j in range(2):
                            x = xg[:, 2 * p + j, :]
                            mm(bank(4, DH, D), x[:, 0:DH], x, start=False, stop=False, skip_group_check=True)
                            m = mm(bank(5, DH, DH), x[:, DH:D], x[:, DH:D], start=False, stop=False,
                                   skip_group_check=True)
                        m.then_inc(S["gram_read"], 1)

                pe.wait_ge(dB.sem, dB.value(b, "g1"))
                pB.mark(tr(bank(2, DH, DH), gram[:, 0, DH:D], ident[0:DH, 0:DH]), "mirror")
                pe.wait_ge(dB.sem, dB.value(b, "g2"))
                for bk, name in ((4, "wk0"), (5, "wq0")):
                    for n in range(2):
                        for k in range(2):
                            m = mm(PS[0:DH, bk, n * D:(n + 1) * D], gram[:, k, n * DH:(n + 1) * DH],
                                   halves[name][:, k, :], start=k == 0, stop=k == 1)
                pB.mark(m, "gw")
                pe.wait_ge(dB.sem, dB.value(b, "pq"))
                for n in range(2):
                    for k in range(2):
                        mm(PS[0:DH, 2, n * DH:(n + 1) * DH], halves["wq0"][:, k, n * DH:(n + 1) * DH],
                           gk[:, k, n * DH:(n + 1) * DH], start=k == 0, stop=k == 1)
                for k in range(2):
                    mm(bank(3, DH, D), ones[0:DH, 0:DH], prodk[:, k, :], start=k == 0, stop=k == 1)
                for n in range(2):
                    for k in range(2):
                        m = mm(PS[0:DH, 3, D + n:D + n + 1], prodq[:, k, n * DH:(n + 1) * DH], ones[0:DH, 0:1],
                               start=k == 0, stop=k == 1)
                pB.mark(m, "qk")
                pe.wait_ge(dB.sem, dB.value(b, "att"))
                for n in range(2):
                    m = mm(PS[0:DH, 2, n * D:(n + 1) * D], att0[:, n, :], halves["wproj"][:, n, :],
                           start=True, stop=True)
                pB.mark(m, "t1")
                pe.wait_ge(dB.sem, dB.value(b, "t1"))
                for n in range(2):
                    for k in range(2):
                        m = mm(PS[0:DH, 3, n * D:(n + 1) * D], halves["wvT"][:, k, n * DH:(n + 1) * DH],
                               t1sb[:, k, :], start=k == 0, stop=k == 1)
                pB.mark(m, "mix")
                pe.wait_ge(dB.sem, dB.value(b, "mix"))
                hold(pe)

                with pe.Fori(0, NQ) as i:
                    q = b * (TPASS * NQ) + i
                    g = b * NQ + i
                    turn(q)
                    for p in range(2):
                        pe.wait_ge(S["xt_ready"], 2 * q + p + 3)
                        pe.wait_ge(S["h1_ready"], 2 * g + p + 1)
                        tile_pair(p, 6 + p, xT, mix, D).then_inc(S["mix_done"], 1)

                pe.wait_ge(dE.sem, dE.value(b, "xc"))
                hold(pe)
                for k in range(2):
                    m = tr(PS[0:DH, 2, k * NCLS:(k + 1) * NCLS], xc[:, k * DH:(k + 1) * DH], ident[0:NCLS, 0:NCLS])
                pE.mark(m, "turned")
                pe.wait_ge(aE.sem, aE.value(b, "xcT"))
                for a in range(NAT * FT):
                    for k in range(2):
                        m = mm(PS[:, 3, a * NCLS:(a + 1) * NCLS], halves["atom_in"][:, k, a * 128:(a + 1) * 128],
                               xcT[:, k, :], start=k == 0, stop=k == 1)
                pE.mark(m, "hidden")
                pe.wait_ge(dE.sem, dE.value(b, "diag1"))
                pE.mark(mm(bank(4, 128, 2 * NCLS), ones[0:NCLS, :], cdiag[:, :, :].rearrange("p a n -> p (a n)"),
                           start=True, stop=True), "flags")
                pe.wait_ge(dE.sem, dE.value(b, "sel"))
                for a in range(NAT):
                    for k in range(FT):
                        m = mm(bank(5, NCLS, D), csel[:, a, k, :], atom_out[:, a, k, :],
                               start=a + k == 0, stop=(a == NAT - 1 and k == FT - 1))
                pE.mark(m, "out")

                pe.wait_ge(dE.sem, dE.value(b, "res"))
                hold(pe)
                with pe.Fori(0, NQ) as i:
                    q = b * (TPASS * NQ) + NQ + i
                    g = b * NQ + i
                    turn(q)
                    pe.wait_ge(S["xt_ready"], 2 * q + 4)
                    for f in range(FT):
                        if f >= 4:
                            pe.wait_ge(S["gelu_done"], FT * g + f - 3)
                        for k in range(2):
                            m = mm(PS[:, 2 + f % 4, 0:4 * T], halves["fc1"][:, k, f * 128:(f + 1) * 128],
                                   xT[:, k, :, :].rearrange("p c t -> p (c t)"), start=k == 0, stop=k == 1)
                        m.then_inc(S["fc1_done"], 1)
                    pe.wait_ge(S["gelu_done"], FT * g + FT)
                    for p in range(2):
                        pe.wait_ge(S["h2_ready"], 2 * g + p + 1)
                        if p == 0:
                            pe.wait_ge(S["h1_ready"], 2 * NQ * b + 2 * NQ + 2)
                        for j in range(2):
                            for k in range(FT):
                                m = mm(PS[0:T, 6 + p, j * D:(j + 1) * D], hid[:, k, 2 * p + j, :], fc2[:, k, :],
                                       start=k == 0, stop=k == FT - 1)
                        m.then_inc(S["patches_done"], 1)

                pe.wait_ge(S["us_start"], b + 1)
                hold(pe)
                with pe.Fori(0, NQ) as i:
                    q = b * (TPASS * NQ) + 2 * NQ + i
                    g = b * NQ + i
                    turn(q)
                    for p in range(2):
                        pe.wait_ge(S["xt_ready"], 2 * q + p + 3)
                        pe.wait_ge(S["ug_out"], 2 * g + p + 1)
                        tile_pair(p, 2 + p, xT, halves["wug"], GU).then_inc(S["ug_done"], 1)
                    for c in range(4):
                        pe.wait_ge(S["ug_out"], 2 * g + c // 2 + 3)
                        pe.wait_ge(S["us_out"], 4 * g + c + 1)
                        mm(bank(4 + c, T, D), last, usum[:, (c + 3) % 4, :], start=True, stop=False)
                        mm(bank(4 + c, T, D), tri, ug[:, c, 0:D], start=False, stop=True).then_inc(S["us_done"], 1)

                pe.wait_ge(dG.sem, dG.value(b, "max"))
                pG.mark(tr(bank(2, HL, T), smax[:, :], ident[0:T, 0:T]), "maxT")
                pe.wait_ge(dG.sem, dG.value(b, "diag"))
                pG.mark(mm(bank(3, T, HL), ones[0:HL, 0:T], sdiag[:, :], start=True, stop=True), "max")
                pe.wait_ge(aG.sem, aG.value(b, "exp"))
                for k in range(2):
                    part = es[:, k * HL:(k + 1) * HL, :].rearrange("p h c -> p (h c)")
                    mm(bank(4 + k, T, HL * NC), tri, part, start=True, stop=True)
                    m = mm(bank(6 + k, T, HL * NC), ones[0:T, 0:T], part, start=True, stop=True)
                pG.mark(m, "sums")

                pe.wait_ge(aG.sem, aG.value(b, "state0"))
                pe.wait_ge(dG.sem, dG.value(b, "ga"))
                mm(bank(7, 128, 9 * HD), zeros[0:T, 0:128], zeros[0:T, 0:9 * HD], start=True, stop=False,
                   skip_group_check=True)
                with pe.Fori(0, NQ) as i:
                    q = b * (TPASS * NQ) + 3 * NQ + i
                    g = b * NQ + i
                    pe.wait_ge(S["o_out"], 4 * g + 1)
                    turn(q)
                    pe.wait_ge(S["h3_ready"], 2 * g + 2)
                    pe.wait_ge(S["xt_ready"], 2 * q + 4)
                    for c in range(4):
                        for k in range(2):
                            m = mm(bank(2 + c, T, 2 * D), xT[:, k, c, :], halves["wqkv"][:, k, 0:2 * D],
                                   start=k == 0, stop=k == 1)
                        m.then_inc(S["qk_done"], 1)
                        for k in range(2):
                            m = mm(PS[0:T, (6, 0)[c // 2], (c % 2) * D:(c % 2 + 1) * D], xT[:, k, c, :],
                                   halves["wqkv"][:, k, 2 * D:3 * D], start=k == 0, stop=k == 1)
                        if c % 2 == 1:
                            m.then_inc(S["v_done"], 1)

                    def turn_qk(c):
                        pe.wait_ge(S["qk_ready"], 4 * g + c + 5)
                        if c < 2:
                            pe.wait_ge(S["v_out"], 2 * g + c + 1)
                        else:
                            pe.wait_ge(S["qkt_out"], 8 * g + 2 * c - 2)
                        for n, bk in enumerate(((1, 6), (0, 2))[c % 2]):
                            for k in range(3):
                                m = tr(PS[:, bk, k * T:(k + 1) * T],
                                       qk[:, c, n * HL + 4 * k:n * HL + 4 * k + 4, :].rearrange("p h d -> p (h d)"),
                                       ident[0:T, 0:T])
                            m.then_inc(S["qkt_done"], 1)

                    def scores(c):
                        for j in range(4):
                            if c == 0:
                                pe.wait_ge(S["qkt_out"], 8 * g + 8)
                            else:
                                pe.wait_ge(S["s_out"], 16 * g + 4 * (c - 1) + j + 1)
                            for k in range(3):
                                m = mm(PS[0:T, 2 + j, k * T:(k + 1) * T], qkT[32 * j:32 * j + 32, c, 1, k, :],
                                       qkT[32 * j:32 * j + 32, c, 0, k, :], start=True, stop=True)
                            m.then_inc(S["s_done"], 1)

                    def new_state(c):
                        pe.wait_ge(S["v3_ready"], 4 * g + c + 5)
                        pe.wait_ge(S["st_out"], 4 * g + c + 1)
                        for j in range(4):
                            for k in range(3):
                                m = mm(PS[32 * j:32 * j + 32, 7, k * 3 * HD:(k + 1) * 3 * HD],
                                       qk[:, c, HL + 4 * k + j, :],
                                       v3[:, c, 4 * k + j, :, :].rearrange("p j d -> p (j d)"),
                                       start=False, stop=False, skip_group_check=True)
                        m.then_inc(S["st_done"], 1)

                    def outputs(c):
                        pe.wait_ge(S["o_out"], 4 * g + c + 1)
                        pe.wait_ge(S["s_out"], 16 * g + 4 * c + 4)
                        for k in range(3):
                            mm(PS[0:T, k // 2, (k % 2) * 12 * HD:(k % 2 + 1) * 12 * HD], qkT[:, c, 0, k, :],
                               state[:, c % 2, k, :, :].rearrange("p j d -> p (j d)"),
                               start=True, stop=False, skip_group_check=True)
                            for n in range(4 * k, 4 * k + 4):
                                m = mm(PS[0:T, n // 8, (n % 8) * 3 * HD:(n % 8 + 1) * 3 * HD],
                                       att[:, c % 2, n % 4, k, :], v3[:, c, n, :, :].rearrange("p j d -> p (j d)"),
                                       start=False, stop=n % 4 == 3, skip_group_check=True)
                        m.then_inc(S["o_done"], 1)

                    for c in range(4):
                        turn_qk(c)
                    scores(0)
                    new_state(0)
                    for c in range(1, 4):
                        scores(c)
                        outputs(c - 1)
                        new_state(c)
                    outputs(3)
                    for p in range(2):
                        pe.wait_ge(S["oln_ready"], 2 * g + p + 1)
                        if p == 1:
                            pe.wait_ge(S["s_out"], 16 * g + 16)
                        for j in range(2):
                            for k in range(2):
                                m = tr(PS[0:DH, (6, 4)[p], (2 * k + j) * T:(2 * k + j + 1) * T],
                                       osum[:, 2 * p + j, k * DH:(k + 1) * DH], ident[0:T, 0:T])
                        m.then_inc(S["ot_done"], 1)
                    for p in range(2):
                        pe.wait_ge(S["ot_out"], 2 * g + p + 1)
                        m = tile_pair(p, 2 + p, oT, halves["wo"], D)
                        m.then_inc(S["wo_done"], 1)

                pe.wait_ge(S["h3_ready"], 2 * NQ * b + 2 * NQ + 2)
                hold(pe)
                with pe.Fori(0, NQ) as i:
                    q = b * (TPASS * NQ) + 4 * NQ + i
                    g = b * NQ + i
                    turn(q)
                    pe.wait_ge(S["lg_out"], g + 1)
                    pe.wait_ge(S["xt_ready"], 2 * q + 4)
                    for c in range(4):
                        for k in range(2):
                            m = mm(PS[0:T, 6, c * E:(c + 1) * E], xT[:, k, c, :], halves["router"][:, k, :],
                                   start=k == 0, stop=k == 1)
                    m.then_inc(S["lg_done"], 1)

                pe.wait_ge(dR.sem, dR.value(b, "onehot"))
                flat = onehot[:, :, :].rearrange("p e c -> p (e c)")
                mm(bank(2, T, E * NC), tri, flat, start=True, stop=True)
                pR.mark(mm(bank(3, T, E * NC), ones[0:T, 0:T], flat, start=True, stop=True), "sums")

                pe.wait_ge(dR.sem, dR.value(b, "posx"))
                mm(bank(4, 128, E), zeros[0:T, 0:128], zeros[0:T, 0:E], start=True, stop=False, skip_group_check=True)
                with pe.Fori(0, NQ) as i:
                    g = b * NQ + i
                    for c in range(4):
                        pe.wait_ge(S["pick_ready"], 4 * g + c + 1)
                        mm(bank(4, 128, E), pick[:, c, :], one(onehot[:, :, bass.ds(4 * i + c, 1)]
                                                            .rearrange("p e c -> p c e")),
                           start=False, stop=False, skip_group_check=True).then_inc(S["slots_done"], 1)

            pe.wait_ge(S["image_done"], nb + 1)
            with pe.Fori(0, E // 2) as k2:
                for s in range(2):
                    e = 2 * k2 + s
                    pe.wait_ge(S["moe_xt"], e + 1)
                    pe.wait_ge(S["moe_x"], e + 1)
                    for n in range(4):
                        for k in range(2):
                            m = tr(PS[0:DH, n // 2, (2 * k + n % 2) * 128:(2 * k + n % 2 + 1) * 128],
                                   mx[:, n, k * DH:(k + 1) * DH], ident)
                    m.then_inc(S["moe_turned"], 1)
                    pe.wait_ge(S["moe_xt"], e + 2)
                    pe.wait_ge(S[f"w1_in{s}"], 16 * k2 + 16)
                    for f in range(FT):
                        if f == 4:
                            pe.wait_ge(S["moe_ra"], 3 * e + 1)
                        if f == 5:
                            pe.wait_ge(S["moe_rd"], 3 * e + 1)
                        for k in range(2):
                            m = mm(PS[:, 2 + f % 4, :], w1[s][:, k, f * 128:(f + 1) * 128], mT[:, k, :],
                                   start=k == 0, stop=k == 1)
                        m.then_inc(S["moe_f"], 1)
                    pe.wait_ge(S["moe_ra"], 3 * e + 3)
                    pe.wait_ge(S["moe_rd"], 3 * e + 3)
                    pe.wait_ge(S[f"w2_in{s}"], 16 * k2 + 16)
                    for p in range(2):
                        pe.wait_ge(S["moe_y"], 2 * e + p + 1)
                        for j in range(2):
                            for k in range(FT):
                                m = mm(PS[:, 6 + p, j * D:(j + 1) * D],
                                       mh[:, k, (2 * p + j) * 128:(2 * p + j + 1) * 128], w2[s][:, k, :],
                                       start=k == 0, stop=k == FT - 1)
                        m.then_inc(S["moe_o"], 1)

        @block.scalar
        def _(act):
            A = nc.scalar.activation
            act.wait_ge(S["packed_in"], 16)
            give_leads(act, xt_ready=2, ug_out=2, us_out=1, st_out=1, lg_out=1, out_written=16, moe_xt=1)

            act.wait_ge(dS.sem, dS.value(0, "gss"))
            aS.mark(A(gss[:, :], gss[:, :], ACT.Sqrt), "gnorm")
            act.wait_ge(dS.sem, dS.value(0, "tau"))
            aS.mark(A(tau[:, :], tau[:, :], ACT.Exp), "tau")
            act.wait_ge(dS.sem, dS.value(0, "invt"))

            def xt_out(q):
                for p in range(2):
                    act.wait_ge(S["turned"], 2 * q + p + 3)
                    A(xT[:, :, 2 * p:2 * p + 2, :], bank(p, DH, 4 * T).rearrange("p (k c t) -> p k c t", k=2, c=2),
                      ACT.Copy).then_inc(S["xt_ready"], 1)

            with act.Fori(0, nb) as b:
                with act.Fori(0, NQ) as i:
                    g = b * NQ + i
                    for p in range(2):
                        act.wait_ge(dA.sem, dA.value(g, f"agg{p}"))
                        aA.mark(A(ch(rs[0], i, 2 * p, 2), bnv[:, 2 * p:2 * p + 2, 1], ACT.Sqrt,
                                  bias=eps_ln[0:T]), f"sd{p}")
                act.wait_ge(pB.sem, pB.value(b, "qk"))
                aB.mark(A(norm0[:, :], bank(3, DH, D + 2), ACT.Sqrt), "norm")
                act.wait_ge(dB.sem, dB.value(b, "rowm"))
                for n in range(2):
                    m = A(att0[:, n, :], att0[:, n, :], ACT.Exp, bias=rowm[:, n:n + 1])
                aB.mark(m, "exp")
                with act.Fori(0, NQ) as i:
                    act.wait_ge(S["mix_done"], 2 * (b * NQ + i) + 2)
                    xt_out(b * (TPASS * NQ) + i)
                act.wait_ge(dC.sem, dC.value(b * NQ + NQ - 1, "keep1"))
                aR2.mark(A(rs[1][:, :], mv[1][:, :, 1], ACT.Sqrt, bias=eps_ln[0:T]), "sd")
                act.wait_ge(pE.sem, pE.value(b, "turned"))
                aE.mark(A(xcT[:, :, :], bank(2, DH, 2 * NCLS).rearrange("p (k n) -> p k n", k=2), ACT.Copy), "xcT")
                act.wait_ge(dE.sem, dE.value(b, "sum"))
                aE.mark(A(csum[:, 2:3], csum[:, 2:3], ACT.Sqrt), "norm")
                act.wait_ge(dE.sem, dE.value(b, "diff"))
                aE.mark(A(cext[:, 1:2], cext[:, 1:2], ACT.Exp), "exp")
                act.wait_ge(dE.sem, dE.value(b, "pre"))
                aE.mark(A(chid[:, :, :, :].rearrange("p a k n -> p (a k n)"),
                          cpre[:, :, :].rearrange("p a n -> p (a n)"), ACT.Gelu), "gelu")
                act.wait_ge(S["mix_done"], 2 * NQ * b + 2 * NQ + 2)
                hold(act)
                with act.Fori(0, NQ) as i:
                    g = b * NQ + i
                    xt_out(b * (TPASS * NQ) + NQ + i)
                    act.wait_ge(S["patches_done"], 2 * g + 2)
                    for f in range(FT):
                        act.wait_ge(S["fc1_done"], FT * g + f + 1)
                        A(hid[:, f, :, :].rearrange("p c t -> p (c t)"), PS[:, 2 + f % 4, 0:4 * T], ACT.Gelu,
                          bias=w("fc1_b")[:, f:f + 1]).then_inc(S["gelu_done"], 1)
                act.wait_ge(dR3.sem, dR3.value(b, "agg"))
                aR3.mark(A(rs[2][:, :], mv[2][:, :, 1], ACT.Sqrt, bias=eps_ln[0:T]), "sd")
                act.wait_ge(S["uprod_done"], NQ * b + 1)
                A(usum[:, 3, :], taumu, ACT.Copy).then_inc(S["us_start"], 1)
                with act.Fori(0, NQ) as i:
                    g = b * NQ + i
                    xt_out(b * (TPASS * NQ) + 2 * NQ + i)
                    act.wait_ge(S["uprod_done"], g + 1)
                    act.wait_ge(S["gates_kept"], g + 1)
                    for p in range(2):
                        act.wait_ge(S["ug_done"], 2 * g + p + 1)
                        A(ug[:, 2 * p:2 * p + 2, :], bank(2 + p, T, 2 * GU).rearrange("p (c n) -> p c n", c=2),
                          ACT.Copy).then_inc(S["ug_out"], 1)
                    for c in range(4):
                        act.wait_ge(S["us_done"], 4 * g + c + 1)
                        A(usum[:, c, :], bank(4 + c, T, D), ACT.Copy).then_inc(S["us_out"], 1)
                act.wait_ge(dG.sem, dG.value(b, "shift"))
                aG.mark(A(es[:, 0:HL, :], es[:, 0:HL, :], ACT.Exp), "exp")
                act.wait_ge(S["gates_kept"], NQ * b + NQ + 1)
                aG.mark(A(gates[:, :, :], gates[:, :, :], ACT.Sigmoid), "gates")
                aG.mark(A(state[:, 0, :, :, :], spread(zeros[:, 0:9 * HD].rearrange("p (k d) -> p k d", k=3), 2, 4),
                          ACT.Copy),
                        "state0")
                with act.Fori(0, NQ) as i:
                    g = b * NQ + i
                    xt_out(b * (TPASS * NQ) + 3 * NQ + i)

                    def v_out(p):
                        act.wait_ge(S["v3_ready"], 4 * g + 4)
                        act.wait_ge(S["v_done"], 2 * g + p + 1)
                        A(vs[:, 2 * p:2 * p + 2, :], bank((6, 0)[p], T, 2 * D).rearrange("p (c n) -> p c n", c=2),
                          ACT.Copy).then_inc(S["v_out"], 1)

                    def square(c):
                        act.wait_ge(S["qk_ready"], 4 * g + c + 5)
                        A(rope1[:, c, :, :], qk[:, c, :, 0:HD], ACT.Square).then_inc(S["squared"], 1)

                    def qkt_out(c):
                        for n, bk in enumerate(((1, 6), (0, 2))[c % 2]):
                            act.wait_ge(S["qkt_done"], 8 * g + 2 * c + n + 1)
                            A(qkT[:, c, n, :, :], bank(bk, 128, 3 * T).rearrange("p (k t) -> p k t", k=3),
                              ACT.Copy).then_inc(S["qkt_out"], 1)

                    def state_out(c):
                        act.wait_ge(S["st_done"], 4 * g + c + 5)
                        for j in range(4):
                            lanes = slice(32 * j, 32 * j + 32)
                            m = A(state[lanes, (c + 1) % 2, :, j, :],
                                  PS[lanes, 7, 0:9 * HD].rearrange("p (k d) -> p k d", k=3), ACT.Copy)
                        m.then_inc(S["st_out"], 1)

                    def variance(p):
                        act.wait_ge(S["ctr_ready"], 2 * g + p + 1)
                        A(o3[:, 2 * p:2 * p + 2, 0:4, :, :].rearrange("p c h j d -> p c (h j d)"),
                          osum[:, 2 * p:2 * p + 2, :], ACT.Square).then_inc(S["osq_out"], 1)
                        act.wait_ge(S["ovar"], 2 * g + p + 1)
                        A(ost[:, 2 * p:2 * p + 2, :], ost[:, 2 * p:2 * p + 2, :], ACT.Sqrt, bias=eps_ln[0:T],
                          scale=1.0 / HD).then_inc(S["osd_out"], 1)

                    v_out(0)
                    square(0)
                    v_out(1)
                    square(1)
                    square(2)
                    square(3)
                    qkt_out(0)
                    qkt_out(1)
                    act.wait_ge(dH.sem, dH.value(g, "ss"))
                    A(nrm[:, :, :], nrm[:, :, :], ACT.Sqrt).then_inc(S["rn_ready"], 1)
                    qkt_out(2)
                    qkt_out(3)
                    for c in range(3):
                        state_out(c)
                    variance(0)
                    state_out(3)
                    variance(1)
                    for p in range(2):
                        act.wait_ge(S["ot_done"], 2 * g + p + 1)
                        A(oT[:, :, 2 * p:2 * p + 2, :],
                          bank((6, 4)[p], DH, 4 * T).rearrange("p (k c t) -> p k c t", k=2, c=2),
                          ACT.Copy).then_inc(S["ot_out"], 1)
                act.wait_ge(dH.sem, dH.value(b * NQ + NQ - 1, "keep1"))
                aI.mark(A(rs[3][:, :], mv[3][:, :, 1], ACT.Sqrt, bias=eps_ln[0:T]), "sd")
                act.wait_ge(dI.sem, dI.value(b, "ms"))
                aI.mark(A(rn[:, :], rn[:, :], ACT.Sqrt, bias=eps_rms[0:T]), "rms")
                with act.Fori(0, NQ) as i:
                    g = b * NQ + i
                    xt_out(b * (TPASS * NQ) + 4 * NQ + i)
                    act.wait_ge(S["lg_done"], g + 1)
                    A(lg[:, :, bass.ds(4 * i, 4)].rearrange("p e c -> p c e"),
                      bank(6, T, 4 * E).rearrange("p (c e) -> p c e", c=4), ACT.Copy).then_inc(S["lg_out"], 1)
                act.wait_ge(dR.sem, dR.value(b, "shift"))
                aR.mark(A(rtmp[:, :, :], rtmp[:, :, :], ACT.Exp), "exp")
                with act.Fori(0, NQ) as i:
                    g = b * NQ + i
                    token = b * L + i * (4 * T)
                    act.wait_ge(S["res_ready"], g + 5)
                    act.dma_start(out[bass.ds(token, 4 * T), :].rearrange("(c p) n -> p c n", p=T),
                                  ob[:, :, :]).then_inc(S["out_written"], 16)
                    act.dma_start(rows[bass.ds(token + 1, 4 * T), :].rearrange("(c p) n -> p c n", p=T),
                                  ch(h, i, 0, 4)).then_inc(S["rows_written"], 16)
            with act.Fori(0, E // 2) as k2:
                for s in range(2):
                    e = 2 * k2 + s
                    act.wait_ge(S["moe_f"], 6 * e + 6)
                    act.wait_ge(S["moe_turned"], e + 2)
                    for p in range(2):
                        m = A(mT[:, :, 256 * p:256 * (p + 1)], bank(p, DH, 512).rearrange("p (k n) -> p k n", k=2),
                              ACT.Copy)
                    m.then_inc(S["moe_xt"], 1)
                    act.wait_ge(S["moe_o"], 2 * e + 3)
                    for f in (0, 2, 4):
                        act.wait_ge(S["moe_f"], 6 * e + f + 7)
                        A(mh[:, f, :], PS[:, 2 + f % 4, :], ACT.Relu).then_inc(S["moe_ra"], 1)

        @block.vector
        def _(dve):
            tt, ts, stt = nc.vector.tensor_tensor, nc.vector.tensor_scalar, nc.vector.scalar_tensor_tensor
            red, cp = nc.vector.tensor_reduce, nc.vector.tensor_copy

            def settle(steps, done, name):
                dve.wait_ge(steps.sem, steps.value(done, name))

            dS.mark(nc.vector.memset(qk[:, :, :, :], 0.0), "pad")
            dS.mark(nc.vector.memset(state[:, :, :, :, :], 0.0), "state")
            dS.mark(nc.vector.memset(csel[:, :, :, :], 0.0), "sel")
            dS.mark(nc.vector.memset(slots[:, :, :], 0.0), "slots")
            dve.wait_ge(S["packed_in"], 16)
            give_leads(dve, conv_out=2, h1_ready=2, h2_ready=2, uprod_done=1, o_out=1, h3_ready=2,
                       image_done=1, patches_done=2, moe_y=2)
            dS.mark(tt(cprod[:, 0:2, :], gate, gate, ALU.mult), "gsq")
            settle(dS, 0, "gsq")
            dS.mark(red(gss[:, :], cprod[:, 0:2, :], AX.X, ALU.add), "gss")
            dve.wait_ge(aS.sem, aS.value(0, "gnorm"))
            dS.mark(ts(gss[:, :], gss[:, :], 1e-12, None, ALU.max), "nmax")
            settle(dS, 0, "nmax")
            dS.mark(nc.vector.reciprocal(gss[:, :], gss[:, :]), "nrec")
            settle(dS, 0, "nrec")
            dS.mark(tt(gate, gate, spread(gss[:, :], 2, D), ALU.mult), "gate")
            dS.mark(tt(halves["router"], halves["router"], spread(w("lnwT"), 2, E), ALU.mult), "router")
            dS.mark(ts(tau[:, :], w("logtau"), -50.0, 30.0, ALU.max, ALU.min), "tau")
            dve.wait_ge(aS.sem, aS.value(0, "tau"))
            dS.mark(tt(taumu.rearrange("p (h d) -> p h d", h=HL), w("mu").rearrange("p (h d) -> p h d", h=HL),
                       spread(tau[:, :], 2, HD), ALU.mult), "taumu")
            dS.mark(tt(scoef[:, :, :], spread(w("pos"), 2, HL), spread(tau[:, :], 1, NC), ALU.add), "s0")
            settle(dS, 0, "s0")
            dS.mark(nc.vector.reciprocal(scoef[:, :, :], scoef[:, :, :]), "s1")
            settle(dS, 0, "s1")
            dS.mark(ts(scoef[:, :, :], scoef[:, :, :], -1.0 / HD ** 0.5, None, ALU.mult), "s2")
            dS.mark(nc.vector.reciprocal(invt[:, :], w("pos")), "invt")
            settle(dS, 0, "invt")

            def normalise(q, i, n):
                for p in range(2):
                    dve.wait_ge(S["turned"], 2 * q + p + 1)
                    for c in (2 * p, 2 * p + 1):
                        m = ts(xh[:, c, :], one(ch(hx, i, c)), one(ch(mv[n], i, c)[:, :, 0:1]), ch(rs[n], i, c),
                               ALU.subtract, ALU.mult)
                    m.then_inc(S["xh_ready"], 1)

            def stats(steps, done, i, p, n):
                hold(dve)
                for j in range(2):
                    m = nc.vector.bn_stats(bns[:, 2 * p + j, :], one(ch(hx, i, 2 * p + j)))
                steps.mark(m, f"stat{p}")
                settle(steps, done, f"stat{p}")
                hold(dve)
                for j in range(2):
                    m = nc.vector.bn_aggr(bnv[:, 2 * p + j, :], bns[:, 2 * p + j, :])
                steps.mark(m, f"agg{p}")
                settle(steps, done, f"agg{p}")
                hold(dve)
                steps.mark(cp(ch(mv[n], i, 2 * p, 2), bnv[:, 2 * p:2 * p + 2, :]), f"keep{p}")

            def add_pair(i, p, bk):
                return tt(ch(hx, i, 2 * p, 2), ch(hx, i, 2 * p, 2), bank(bk, T, 2 * D).rearrange("p (c n) -> p c n", c=2),
                          ALU.add)

            with dve.Fori(0, nb) as b:
                dve.wait_ge(S["rows_written"], 16 * NQ * b + 16)
                dve.wait_ge(S["res_ready"], NQ * b + 4)
                dve.wait_ge(S["out_written"], 16 * NQ * b + 16)
                hold(dve)
                with dve.Fori(0, NQ) as i:
                    g = b * NQ + i
                    for p in range(2):
                        dve.wait_ge(S["conv_done"], 2 * g + p + 3)
                        tt(ch(hx, i, 2 * p, 2), bank(6 + p, T, 2 * D).rearrange("p (c n) -> p c n", c=2),
                           spread(w("tok_b"), 1, 2), ALU.add).then_inc(S["conv_out"], 1)
                        dve.wait_ge(S["conv_out"], 2 * g + p + 3)
                        stats(dA, g, i, p, 0)
                        dve.wait_ge(aA.sem, aA.value(g, f"sd{p}"))
                        dA.mark(nc.vector.reciprocal(ch(rs[0], i, 2 * p, 2), ch(rs[0], i, 2 * p, 2)), f"rstd{p}")
                        dve.wait_ge(S["gram_read"], 2 * g + p + 1)
                        settle(dA, g, f"rstd{p}")
                        for c in (2 * p, 2 * p + 1):
                            m = ts(xg[:, c, :], one(ch(hx, i, c)), bnv[:, c, 0:1], ch(rs[0], i, c),
                                   ALU.subtract, ALU.mult)
                        m.then_inc(S["xg_ready"], 1)

                dve.wait_ge(S["gram_read"], 2 * NQ * b + 2 * NQ + 2)
                dB.mark(cp(gram[:, 0, :], bank(4, DH, D)), "g0")
                dB.mark(cp(gram[:, 1, DH:D], bank(5, DH, DH)), "g1")
                dve.wait_ge(pB.sem, pB.value(b, "mirror"))
                dB.mark(cp(gram[:, 1, 0:DH], bank(2, DH, DH)), "g2")
                dve.wait_ge(pB.sem, pB.value(b, "gw"))
                gw = [bank(k, DH, 2 * D).rearrange("p (k n) -> p k n", k=2) for k in (4, 5)]
                dB.mark(cp(gk[:, :, :], gw[0]), "gk")
                dB.mark(tt(prodk[:, :, :], gw[0], halves["wk0"], ALU.mult), "pk")
                dB.mark(tt(prodq[:, :, :], gw[1], halves["wq0"], ALU.mult), "pq")
                dve.wait_ge(aB.sem, aB.value(b, "norm"))
                dB.mark(nc.vector.reciprocal(norm0[:, :], norm0[:, :]), "rnorm")
                settle(dB, b, "rnorm")
                dB.mark(tt(rsum[:, :], norm0[:, D:D + 2], w("temp"), ALU.mult), "rqt")
                dB.mark(tt(att0[:, :, :], bank(2, DH, D).rearrange("p (k n) -> p k n", k=2),
                           norm0[:, 0:D].rearrange("p (k n) -> p k n", k=2), ALU.mult), "l0")
                settle(dB, b, "l0")
                for n in range(2):
                    dB.mark(stt(att0[:, n, :], att0[:, n, :], rsum[:, n:n + 1], w("offblock"), ALU.mult, ALU.add),
                            f"l{n + 1}")
                settle(dB, b, "l2")
                dB.mark(red(rowm[:, :], att0[:, :, :], AX.X, ALU.max, negate=True), "rowm")
                dve.wait_ge(aB.sem, aB.value(b, "exp"))
                dB.mark(red(rsum[:, :], att0[:, :, :], AX.X, ALU.add), "rsum")
                settle(dB, b, "rsum")
                nc.vector.reciprocal(rsum[:, :], rsum[:, :]).then_inc(S["att_rsum"], 1)
                dve.wait_ge(S["att_rsum"], b + 1)
                dB.mark(tt(att0[:, :, :], att0[:, :, :], spread(rsum[:, :], 2, DH), ALU.mult), "att")
                dve.wait_ge(pB.sem, pB.value(b, "t1"))
                dB.mark(cp(t1sb[:, :, :], bank(2, DH, 2 * D).rearrange("p (k n) -> p k n", k=2)), "t1")
                dve.wait_ge(pB.sem, pB.value(b, "mix"))
                dB.mark(cp(mix[:, :, :], bank(3, DH, 2 * D).rearrange("p (k n) -> p k n", k=2)), "mix")

                with dve.Fori(0, NQ) as i:
                    g = b * NQ + i
                    q = b * (TPASS * NQ) + i
                    normalise(q, i, 0)
                    for p in range(2):
                        dve.wait_ge(S["bias_in"], 2 * NQ * b + i + 1)
                        dve.wait_ge(S["mix_done"], 2 * g + p + 3)
                        add_pair(i, p, 6 + p).then_inc(S["h1_ready"], 1)
                        dve.wait_ge(S["h1_ready"], 2 * g + p + 3)
                        stats(dC, g, i, p, 1)
                dve.wait_ge(aR2.sem, aR2.value(b, "sd"))
                dR2.mark(nc.vector.reciprocal(rs[1][:, :], rs[1][:, :]), "rstd")
                settle(dR2, b, "rstd")

                dE.mark(ts(xc[:, :], h[0:NCLS, 0, 0:D], mv[1][0:NCLS, 0, 0:1], rs[1][0:NCLS, 0:1],
                           ALU.subtract, ALU.mult), "xc")
                settle(dE, b, "xc")
                dE.mark(tt(cprod[:, 0:2, :], gate, spread(xc[:, :], 1, 2), ALU.mult), "prod")
                dE.mark(tt(cprod[:, 2, :], xc[:, :], xc[:, :], ALU.mult), "sq")
                settle(dE, b, "sq")
                dE.mark(red(csum[:, :], cprod[:, :, :], AX.X, ALU.add), "sum")
                dve.wait_ge(aE.sem, aE.value(b, "norm"))
                dE.mark(ts(csum[:, 2:3], csum[:, 2:3], 1e-12, None, ALU.max), "nmax")
                settle(dE, b, "nmax")
                dE.mark(nc.vector.reciprocal(csum[:, 2:3], csum[:, 2:3]), "nrec")
                settle(dE, b, "nrec")
                dE.mark(stt(clog[:, :], csum[:, 0:2], csum[:, 2:3], w("bal"), ALU.mult, ALU.add), "log")
                settle(dE, b, "log")
                dE.mark(tt(cflag[:, 0:1], clog[:, 0:1], clog[:, 1:2], ALU.is_ge), "flag0")
                dE.mark(tt(cflag[:, 1:2], clog[:, 0:1], clog[:, 1:2], ALU.is_lt), "flag1")
                dE.mark(tt(cext[:, 0:1], clog[:, 0:1], clog[:, 1:2], ALU.max), "max")
                dE.mark(tt(cext[:, 1:2], clog[:, 0:1], clog[:, 1:2], ALU.min), "min")
                settle(dE, b, "min")
                dE.mark(tt(cext[:, 1:2], cext[:, 1:2], cext[:, 0:1], ALU.subtract), "diff")
                dve.wait_ge(aE.sem, aE.value(b, "exp"))
                dE.mark(ts(cext[:, 0:1], cext[:, 1:2], 1.0, None, ALU.add), "p1")
                settle(dE, b, "p1")
                dE.mark(nc.vector.reciprocal(cext[:, 0:1], cext[:, 0:1]), "p")
                for n in range(2):
                    dE.mark(ts(cdiag[:, n, :], ident[0:NCLS, 0:NCLS], cflag[:, n:n + 1], None, ALU.mult), f"diag{n}")
                dve.wait_ge(pE.sem, pE.value(b, "flags"))
                dE.mark(cp(cflagb[:, :], bank(4, 128, 2 * NCLS)), "flags")
                dE.mark(tt(cpre[:, :, :], bank(3, 128, NAT * FT * NCLS).rearrange("p (a n) -> p a n", n=NCLS),
                           spread(w("in_b"), 2, NCLS), ALU.add), "pre")
                dve.wait_ge(aE.sem, aE.value(b, "gelu"))
                for a in range(3):
                    for t in range(2):
                        n = 2 * a + t
                        ts(csel[:, 3 + t, :, n], chid[:, a, :, n], cflagb[:, n:n + 1], None, ALU.mult)
                        m = ts(csel[:, a, :, n], chid[:, 3 + t, :, n], cflagb[:, NCLS + n:NCLS + n + 1], None, ALU.mult)
                dE.mark(m, "sel")
                out_b = w("out_b").rearrange("p (r n) -> p r n", r=2)
                dE.mark(ts(cbias[:, :], out_b[:, 0, :], cflag[:, 0:1], None, ALU.mult), "bias0")
                settle(dE, b, "bias0")
                dE.mark(stt(cbias[:, :], out_b[:, 1, :], cflag[:, 1:2], cbias[:, :], ALU.mult, ALU.add), "bias")
                dve.wait_ge(pE.sem, pE.value(b, "out"))
                settle(dE, b, "bias")
                dE.mark(tt(cres[:, :], cbias[:, :], bank(5, NCLS, D), ALU.add), "res0")
                settle(dE, b, "res0")
                dE.mark(stt(cres[:, :], cres[:, :], cext[:, 0:1], h[0:NCLS, 0, 0:D], ALU.mult, ALU.add), "res")

                with dve.Fori(0, NQ) as i:
                    g = b * NQ + i
                    q = b * (TPASS * NQ) + NQ + i
                    normalise(q, i, 1)
                    for p in range(2):
                        dve.wait_ge(S["bias_in"], 2 * NQ * b + NQ + i + 1)
                        dve.wait_ge(S["patches_done"], 2 * g + p + 3)
                        add_pair(i, p, 6 + p).then_inc(S["h2_ready"], 1)
                        dve.wait_ge(S["h2_ready"], 2 * g + p + 3)
                        stats(dD, g, i, p, 2)
                dve.wait_ge(dE.sem, dE.value(b, "res"))
                dR3.mark(cp(h[0:NCLS, 0, 0:D], cres[:, :]), "class")
                settle(dR3, b, "class")
                dR3.mark(nc.vector.bn_stats(bns[:, 0, :], h[:, 0, 0:D]), "stat")
                settle(dR3, b, "stat")
                hold(dve)
                dR3.mark(nc.vector.bn_aggr(mv[2][:, 0, :], bns[:, 0, :]), "agg")
                dve.wait_ge(aR3.sem, aR3.value(b, "sd"))
                dR3.mark(nc.vector.reciprocal(rs[2][:, :], rs[2][:, :]), "rstd")
                settle(dR3, b, "rstd")
                hold(dve)

                with dve.Fori(0, NQ) as i:
                    g = b * NQ + i
                    normalise(b * (TPASS * NQ) + 2 * NQ + i, i, 2)
                    dve.wait_ge(S["us_out"], 4 * g + 5)
                    tt(uprod[:, :, :], ug[:, :, 0:D], usum[:, :, :], ALU.mult).then_inc(S["uprod_done"], 1)
                    dve.wait_ge(S["uprod_done"], g + 2)
                    red(sraw[:, :, :], uprod[:, :, :].rearrange("p c (h d) -> p c h d", h=HL), AX.X, ALU.add)\
                        .then_inc(S["s_kept"], 1)
                    dve.wait_ge(S["s_kept"], 2 * g + 1)
                    tt(es[:, HL:2 * HL, bass.ds(4 * i, 4)].rearrange("p h c -> p c h"), sraw[:, :, :],
                       ch(scoef, i, 0, 4), ALU.mult).then_inc(S["s_kept"], 1)

                dve.wait_ge(S["s_kept"], 2 * NQ * b + 2 * NQ)
                dG.mark(red(smax[:, :], es[:, HL:2 * HL, :], AX.X, ALU.max), "max")
                dve.wait_ge(pG.sem, pG.value(b, "maxT"))
                dG.mark(red(smaxT[:, :], bank(2, HL, T), AX.X, ALU.max), "maxT")
                settle(dG, b, "maxT")
                dG.mark(ts(sdiag[:, :], ident[0:HL, 0:HL], smaxT[:, :], None, ALU.mult), "diag")
                dve.wait_ge(pG.sem, pG.value(b, "max"))
                dG.mark(tt(es[:, 0:HL, :], es[:, HL:2 * HL, :], spread(bank(3, T, HL), 2, NC), ALU.subtract), "shift")
                dve.wait_ge(pG.sem, pG.value(b, "sums"))
                cumf = cum[:, :, :].rearrange("p (k h) c -> p k (h c)", k=2)
                for k in range(2):
                    dG.mark(nc.vector.tensor_tensor_scan(cumf[:, k, :], w("reset")[:, 0:HL * NC], bank(6 + k, T, HL * NC),
                                                         0.0, ALU.mult, ALU.add), f"scan{k}")
                settle(dG, b, "scan1")
                dG.mark(tt(cumf, cumf, PS[0:T, 6:8, 0:HL * NC], ALU.subtract), "excl")
                settle(dG, b, "excl")
                dG.mark(tt(cumf, cumf, PS[0:T, 4:6, 0:HL * NC], ALU.add), "sum")
                settle(dG, b, "sum")
                dve.wait_ge(aG.sem, aG.value(b, "gates"))
                gt = gates[:, :, :].rearrange("p c h -> p h c")
                sig1, sigh = gt[:, 0:HL, :], gt[:, HL:2 * HL, :]
                dG.mark(ts(cum[:, 0:HL, :], cum[:, 0:HL, :], 1e-12, None, ALU.add), "eps")
                settle(dG, b, "eps")
                dG.mark(nc.vector.reciprocal(cum[:, 0:HL, :], cum[:, 0:HL, :]), "einv")
                settle(dG, b, "einv")
                dG.mark(tt(coef[:, 0, :, :], cum[:, 0:HL, :], sigh, ALU.mult), "al")
                dG.mark(tt(coef[:, 1, :, :], sig1, sigh, ALU.subtract), "be0")
                settle(dG, b, "be0")
                dG.mark(tt(coef[:, 1, :, :], coef[:, 1, :, :], spread(invt[:, :], 1, HL), ALU.mult), "be")
                settle(dG, b, "be")
                dG.mark(tt(coef[:, 2, :, :], coef[:, 1, :, :], cum[:, HL:2 * HL, :], ALU.mult), "ga0")
                settle(dG, b, "ga0")
                dG.mark(tt(coef[:, 2, :, :], coef[:, 2, :, :], sigh, ALU.add), "ga1")
                settle(dG, b, "ga1")
                dG.mark(stt(coef[:, 2, :, :], coef[:, 2, :, :], -1.0, spread(invt[:, :], 1, HL), ALU.mult, ALU.mult),
                        "ga")

                with dve.Fori(0, NQ) as i:
                    g = b * NQ + i
                    normalise(b * (TPASS * NQ) + 3 * NQ + i, i, 2)
                    for c in range(4):
                        dve.wait_ge(S["qk_done"], 4 * g + c + 1)
                        dve.wait_ge(S["qk_ready"], 4 * g + c + 1)
                        x = bank(2 + c, T, 2 * D).rearrange("p (h d e) -> p h d e", d=HD // 2, e=2)
                        r1, r2 = (r[:, c, :, :].rearrange("p h (d e) -> p h d e", e=2) for r in (rope1, rope2))
                        tt(r1, x, spread(spread(one(ch(cos, i, c)), 1, 2 * HL), 3, 2), ALU.mult)
                        lo, hi = slice(0, HD // 4), slice(HD // 4, HD // 2)
                        for to, frm in ((lo, hi), (hi, lo)):
                            m = tt(r2[:, :, to], x[:, :, frm],
                                   spread(spread(one(ch(sin, i, c)[:, :, to]), 1, 2 * HL), 3, 2), ALU.mult)
                        m.then_inc(S["rope_done"], 1)
                    dve.wait_ge(S["squared"], 4 * g + 4)
                    dH.mark(red(nrm[:, :, :], rope1[:, :, :, :], AX.X, ALU.add), "ss")
                    dve.wait_ge(S["rn_ready"], g + 1)
                    dH.mark(ts(nrm[:, :, :], nrm[:, :, :], 1e-12, None, ALU.max), "nmax")
                    settle(dH, g, "nmax")
                    dH.mark(nc.vector.reciprocal(nrm[:, :, :], nrm[:, :, :]), "nrec")

                    def masked(c):
                        if c >= 2:
                            dve.wait_ge(S["o_done"], 4 * g + c - 1)
                        for j in range(4):
                            dve.wait_ge(S["s_done"], 16 * g + 4 * c + j + 1)
                            tt(att[:, c % 2, j, :, :], bank(2 + j, T, 3 * T).rearrange("p (k t) -> p k t", k=3),
                               spread(tri, 1, 3), ALU.mult).then_inc(S["s_out"], 1)

                    def weigh(c):
                        dve.wait_ge(S["o_done"], 4 * g + c + 1)
                        if c == 0:
                            dve.wait_ge(S["c_ready"], g + 1)
                        for n, heads_of in enumerate((slice(0, 8), slice(8, HL))):
                            k = heads_of.stop - heads_of.start
                            m = tt(o3[:, c, heads_of, :, :],
                                   bank(n, T, k * 3 * HD).rearrange("p (h j d) -> p h j d", h=k, j=3),
                                   spread(cq[:, c, heads_of, :], 3, HD), ALU.mult)
                        m.then_inc(S["o_out"], 1)

                    def heads(t, p):
                        return t[:, 2 * p:2 * p + 2, :].rearrange("p c (h d) -> p c h d", h=HL)

                    def mean(p):
                        dve.wait_ge(S["osum_ready"], 2 * g + p + 1)
                        dH.mark(red(ost[:, 2 * p:2 * p + 2, :], heads(osum, p), AX.X, ALU.add), f"pss{p}")
                        settle(dH, g, f"pss{p}")
                        dH.mark(ts(ost[:, 2 * p:2 * p + 2, :], ost[:, 2 * p:2 * p + 2, :], -1.0 / HD, None, ALU.mult),
                                f"pmean{p}")

                    def variance(p):
                        dve.wait_ge(S["osq_out"], 2 * g + p + 1)
                        red(ost[:, 2 * p:2 * p + 2, :],
                            o3[:, 2 * p:2 * p + 2, 0:4, :, :].rearrange("p c h j d -> p c (h j d)")
                            .rearrange("p c (h d) -> p c h d", h=HL), AX.X, ALU.add).then_inc(S["ovar"], 1)
                        dve.wait_ge(S["osd_out"], 2 * g + p + 1)
                        dH.mark(nc.vector.reciprocal(ost[:, 2 * p:2 * p + 2, :], ost[:, 2 * p:2 * p + 2, :]),
                                f"prn{p}")

                    masked(0)
                    masked(1)
                    weigh(0)
                    masked(2)
                    weigh(1)
                    masked(3)
                    mean(0)
                    weigh(2)
                    variance(0)
                    weigh(3)
                    mean(1)
                    variance(1)
                    for p in range(2):
                        dve.wait_ge(S["wo_done"], 2 * g + p + 1)
                        add_pair(i, p, 2 + p).then_inc(S["h3_ready"], 1)
                        dve.wait_ge(S["h3_ready"], 2 * g + p + 3)
                        stats(dH, g, i, p, 3)

                dve.wait_ge(aI.sem, aI.value(b, "sd"))
                dI.mark(ts(h[:, :, SD], rs[3][:, :], 1.0, None, ALU.add), "one_sd")
                dI.mark(cp(h[:, :, MEAN], mv[3][:, :, 0]), "mean")
                dI.mark(nc.vector.reciprocal(rs[3][:, :], rs[3][:, :]), "rstd")
                settle(dI, b, "rstd")
                dI.mark(tt(rn[:, :], rs[3][:, :], rs[3][:, :], ALU.mult), "sq")
                settle(dI, b, "sq")
                dI.mark(tt(rn[:, :], rn[:, :], mv[3][:, :, 1], ALU.mult), "ms")
                dve.wait_ge(aI.sem, aI.value(b, "rms"))
                dI.mark(nc.vector.reciprocal(rn[:, :], rn[:, :]), "rn")
                settle(dI, b, "rn")
                dI.mark(cp(h[:, :, RN], rn[:, :]), "keep")
                with dve.Fori(0, NQ) as i:
                    g = b * NQ + i
                    q = b * (TPASS * NQ) + 4 * NQ + i
                    dve.wait_ge(S["x_kept"], g + 1)
                    normalise(q, i, 3)

                dve.wait_ge(S["lg_out"], NQ * b + NQ + 1)
                by_chunk = lg[:, :, :].rearrange("p e c -> p c e")
                dR.mark(tt(lg[:, :, :], lg[:, :, :], spread(rn[:, :], 1, E), ALU.mult), "scale")
                settle(dR, b, "scale")
                dR.mark(red(rmax[:, :], by_chunk, AX.X, ALU.max), "max")
                settle(dR, b, "max")
                dR.mark(tt(rtmp[:, :, :], lg[:, :, :], spread(rmax[:, :], 1, E), ALU.subtract), "shift")
                dR.mark(tt(prio[:, :, :], lg[:, :, :], spread(rmax[:, :], 1, E), ALU.is_equal), "eq")
                settle(dR, b, "eq")
                dR.mark(stt(prio[:, :, :], prio[:, :, :], -1000.0, spread(w("iotae"), 2, NC), ALU.mult, ALU.add),
                        "first")
                settle(dR, b, "first")
                dR.mark(red(posx[:, :], prio[:, :, :].rearrange("p e c -> p c e"), AX.X, ALU.min), "lowest")
                settle(dR, b, "lowest")
                dR.mark(tt(onehot[:, :, :], prio[:, :, :], spread(posx[:, :], 1, E), ALU.is_equal), "onehot")
                dve.wait_ge(aR.sem, aR.value(b, "exp"))
                dR.mark(red(prob[:, :], rtmp[:, :, :].rearrange("p e c -> p c e"), AX.X, ALU.add), "psum")
                settle(dR, b, "psum")
                dR.mark(nc.vector.reciprocal(prob[:, :], prob[:, :]), "prob")
                settle(dR, b, "prob")
                dR.mark(tt(prs[:, :], prob[:, :], rn[:, :], ALU.mult), "prs")
                dR.mark(cp(h[:, :, PROB], prob[:, :]), "keepp")
                dve.wait_ge(pR.sem, pR.value(b, "sums"))
                flat = [t[:, :, :].rearrange("p e c -> p (e c)") for t in (prio, rtmp, onehot)]
                dR.mark(nc.vector.tensor_tensor_scan(flat[0], w("reset")[:, 0:E * NC], bank(3, T, E * NC), 0.0,
                                                     ALU.mult, ALU.add), "scan")
                settle(dR, b, "scan")
                dR.mark(tt(flat[0], flat[0], bank(3, T, E * NC), ALU.subtract), "excl")
                settle(dR, b, "excl")
                dR.mark(tt(flat[0], flat[0], bank(2, T, E * NC), ALU.add), "prio")
                settle(dR, b, "prio")
                dR.mark(ts(flat[1], flat[0], CAP + 0.5, None, ALU.is_lt), "under")
                settle(dR, b, "under")
                dR.mark(tt(flat[2], flat[2], flat[1], ALU.mult), "keep")
                settle(dR, b, "keep")
                dR.mark(tt(flat[1], flat[0], flat[2], ALU.mult), "pz")
                settle(dR, b, "pz")
                dR.mark(red(posx[:, :], rtmp[:, :, :].rearrange("p e c -> p c e"), AX.X, ALU.add), "pos")
                settle(dR, b, "pos")
                dR.mark(ts(posx[:, :], posx[:, :], w("poff")[:, bass.ds(b, 1)], None, ALU.add), "posx")
                settle(dR, b, "posx")

                dve.wait_ge(S["x_kept"], NQ * b + NQ + 1)
                hold(dve)
                with dve.Fori(0, NQ) as i:
                    g = b * NQ + i
                    for c in range(4):
                        dve.wait_ge(S["slots_done"], 4 * g + c + 1)
                        ts(pick[:, c, :], w("iota128"), ch(posx, i, c),
                           w("tokid")[:, bass.ds(b * NC + 4 * i + c, 1)], ALU.is_equal, ALU.mult)\
                            .then_inc(S["pick_ready"], 1)
                    dve.wait_ge(S["res_ready"], g + 4)
                    for c in range(4):
                        stt(xo[:, c, :], w("lnw")[0:T], ch(prs, i, c), one(ch(hx, i, c)), ALU.mult, ALU.mult)\
                            .then_inc(S["xn_ready"], 1)
                    dve.wait_ge(S["xn_ready"], 4 * g + 4)
                    for c in range(4):
                        m = stt(xo[:, c, :], one(ch(hx, i, c)), one(ch(h, i, c)[:, :, SD:SD + 1]), xo[:, c, :],
                                ALU.mult, ALU.add)
                    m.then_inc(S["xo_ready"], 1)
                dve.wait_ge(S["slots_done"], 4 * NQ * b + 4 * NQ + 4)
                pair = slots[:, bass.ds(b // 2, 1), :].rearrange("p a e -> p (a e)")
                tt(pair, pair, bank(4, 128, E), ALU.add).then_inc(S["image_done"], 1)
            dve.wait_ge(S["image_done"], nb + 1)
            dM.mark(nc.vector.memset(gidx[:, :, :], 0), "zero")
            dM.mark(ts(empty[:, :, :], slots[:, :, :], 0.0, FAR, ALU.is_equal, ALU.mult), "empty")
            dve.wait_ge(dM.sem, dM.value(0, "empty"))
            dM.mark(cp(gidx[:, 0:E, :], slots[:, :, :].rearrange("p b e -> p e b")), "gather")
            dM.mark(stt(empty[:, :, :], slots[:, :, :], -1.0, empty[:, :, :], ALU.add, ALU.add), "minus1")
            dve.wait_ge(dM.sem, dM.value(0, "minus1"))
            cp(sidx[:, :, :], empty[:, :, :].rearrange("p b e -> p e b")).then_inc(S["index_ready"], 1)

            def expert(e, k2, s, first=False):
                dve.wait_ge(S["moe_turned"], e + 1)
                dve.wait_ge(S[f"gathered{s}"], 64 * k2 + 64)
                for n in range(4):
                    m = stt(mx[:, n, :], mrow[s][:, n, 0:D], mrow[s][:, n, RN:RN + 1], w("lnw"), ALU.mult, ALU.mult)
                m.then_inc(S["moe_x"], 1)
                dve.wait_ge(S["moe_o"], 2 * e + 3)
                for f in (1, 3, 5):
                    dve.wait_ge(S["moe_f"], 6 * e + f + 7)
                    ts(mh[:, f, :], PS[:, 2 + f % 4, :], 0.0, None, ALU.max).then_inc(S["moe_rd"], 1)
                if not first:
                    dve.wait_ge(S[f"scattered{s}"], 64 * k2)
                for n in range(4):
                    m = ts(my[s][:, n, :], mrow[s][:, n, 0:D], mrow[s][:, n, SD:SD + 1],
                           mrow[s][:, n, MEAN:MEAN + 1], ALU.mult, ALU.add)
                m.then_inc(S["moe_h"], 1)
                dve.wait_ge(S["moe_h"], e + 1)
                for p in range(2):
                    dve.wait_ge(S["moe_o"], 2 * e + p + 4)
                    for n in (2 * p, 2 * p + 1):
                        m = stt(my[s][:, n, :], PS[:, 6 + p, (n % 2) * D:(n % 2 + 1) * D],
                                mrow[s][:, n, PROB:PROB + 1], my[s][:, n, :], ALU.mult, ALU.add)
                    m.then_inc(S["moe_y"], 1)

            for s in range(2):
                expert(s, 0, s, first=True)
            with dve.Fori(0, E // 2 - 1) as k:
                for s in range(2):
                    expert(2 * k + 2 + s, k + 1, s)

        @block.gpsimd
        def _(pool):
            tt, ts, cp = nc.gpsimd.tensor_tensor, nc.gpsimd.tensor_scalar, nc.gpsimd.tensor_copy
            pool.wait_ge(S["packed_in"], 16)
            give_leads(pool, gates_kept=1, x_kept=1, v3_ready=4, qk_ready=4, res_ready=4, slots_done=4)

            def add_bias(b, i, after, name):
                pool.wait_ge(S["xh_ready"], after)
                tt(ch(hx, i, 0, 4), ch(hx, i, 0, 4), spread(w(name), 1, 4), ALU.add).then_inc(S["bias_in"], 1)

            with pool.Fori(0, nb) as b:
                with pool.Fori(0, NQ) as i:
                    add_bias(b, i, 2 * (b * (TPASS * NQ) + i) + 2, "bproj")
                with pool.Fori(0, NQ) as i:
                    add_bias(b, i, 2 * (b * (TPASS * NQ) + NQ + i) + 2, "fc2_b")
                with pool.Fori(0, NQ) as i:
                    g = b * NQ + i
                    pool.wait_ge(S["ug_out"], 2 * g + 4)
                    cp(ch(gates, i, 0, 4), ug[:, :, D:GU]).then_inc(S["gates_kept"], 1)
                with pool.Fori(0, NQ) as i:
                    g = b * NQ + i
                    for c in range(4):
                        pool.wait_ge(S["rope_done"], 4 * g + c + 1)
                        pool.wait_ge(S["st_done"], 4 * g + c + 1)
                        tt(qk[:, c, :, 0:HD], rope1[:, c, :, :], rope2[:, c, :, :], ALU.add)\
                            .then_inc(S["qk_ready"], 1)
                    pool.wait_ge(dH.sem, dH.value(g, "nrec"))
                    rk, rq = nrm[:, :, HL:2 * HL], nrm[:, :, 0:HL]
                    quad = bass.ds(4 * i, 4)
                    lH.mark(tt(ck[:, :, :, 0], es[:, 0:HL, quad].rearrange("p h c -> p c h"), rk, ALU.mult), "k0")
                    lH.mark(tt(ck[:, :, :, 1], es[:, HL:2 * HL, quad].rearrange("p h c -> p c h"), rk, ALU.mult), "k1")
                    lH.mark(cp(ck[:, :, :, 2], rk), "k2")
                    pool.wait_ge(lH.sem, lH.value(g, "k2"))
                    for c in range(4):
                        if c % 2 == 0:
                            pool.wait_ge(S["v_out"], 2 * g + c // 2 + 1)
                        tt(v3[:, c, :, :, :], spread(vs[:, c, :].rearrange("p (h d) -> p h d", h=HL), 2, 3),
                           spread(ck[:, c, :, :], 3, HD), ALU.mult).then_inc(S["v3_ready"], 1)
                    for j in range(3):
                        m = tt(cq[:, :, :, j], coef[:, j, :, quad].rearrange("p h c -> p c h"), rq, ALU.mult)
                        if j < 2:
                            lH.mark(m, f"q{j}")
                    m.then_inc(S["c_ready"], 1)
                    for p in range(2):
                        o = o3[:, 2 * p:2 * p + 2, :, :, :]
                        s = osum[:, 2 * p:2 * p + 2, :].rearrange("p c (h d) -> p c h d", h=HL)
                        mid = ost[:, 2 * p:2 * p + 2, :]
                        pool.wait_ge(S["o_out"], 4 * g + 2 * p + 3)
                        for c in range(2):
                            m = tt(s[:, c], o[:, c, :, 0, :], o[:, c, :, 1, :], ALU.add)
                        lH.mark(m, f"a{p}")
                        pool.wait_ge(lH.sem, lH.value(g, f"a{p}"))
                        for c in range(2):
                            m = tt(s[:, c], s[:, c], o[:, c, :, 2, :], ALU.add)
                        m.then_inc(S["osum_ready"], 1)
                        pool.wait_ge(dH.sem, dH.value(g, f"pmean{p}"))
                        tt(s, s, spread(mid, 3, HD), ALU.add).then_inc(S["ctr_ready"], 1)
                        pool.wait_ge(dH.sem, dH.value(g, f"prn{p}"))
                        pool.wait_ge(S["ctr_ready"], 2 * g + p + 1)
                        tt(s, s, spread(mid, 3, HD), ALU.mult).then_inc(S["oln_ready"], 1)
                with pool.Fori(0, NQ) as i:
                    pool.wait_ge(S["xh_ready"], 2 * (b * (TPASS * NQ) + 4 * NQ + i) + 2)
                    cp(ch(hx, i, 0, 4), xh[:, :, :]).then_inc(S["x_kept"], 1)
                with pool.Fori(0, NQ) as i:
                    g = b * NQ + i
                    pool.wait_ge(S["xo_ready"], g + 1)
                    pool.wait_ge(S["out_written"], 16 * g + 16)
                    mean = ch(h, i, 0, 4)[:, :, MEAN:MEAN + 1]
                    tt(ob[:, :, :], xo[:, :, :], mean.broadcast_to([T, 4, D]), ALU.add).then_inc(S["res_ready"], 1)
            pool.wait_ge(S["index_ready"], 1)
            pool.wait_ge(S["rows_written"], 16 * NQ * nb + 16)
            pool.wait_ge(S["out_written"], 16 * NQ * nb + 16)

            def gather(e, s, n):
                cp(gi[s][:, :], gidx[:, bass.ds(e, 1), :].rearrange("p a b -> p (a b)")).then_inc(S["gi_ready"], 1)
                pool.wait_ge(S["gi_ready"], n + 1)
                hold(pool)
                for t in range(B // 2):
                    pool.indirect_dma_start(mrow[s][:, t, :], None, rows, bass.IndirectOffsetOnAxis(ap=gi[s][:, t:t + 1], axis=0))\
                        .then_inc(S[f"gathered{s}"], 16)

            def scatter(e, k2, s, first=False):
                if not first:
                    pool.wait_ge(S[f"scattered{s}"], 64 * k2)
                cp(si[s][:, :], sidx[:, bass.ds(e, 1), :].rearrange("p a b -> p (a b)")).then_inc(S["si_ready"], 1)
                pool.wait_ge(S["si_ready"], e + 1)
                pool.wait_ge(S["moe_y"], 2 * e + 4)
                hold(pool)
                for t in range(B // 2):
                    pool.indirect_dma_start(out, bass.IndirectOffsetOnAxis(ap=si[s][:, t:t + 1], axis=0),
                                            my[s][:, t, :], None, bounds_check=nb * L - 1, oob_is_err=False)\
                        .then_inc(S[f"scattered{s}"], 16)

            for s in range(2):
                gather(s, s, s)
            for s in range(2):
                scatter(s, 0, s, first=True)
                gather(s + 2, s, s + 2)
            with pool.Fori(0, E // 2 - 1) as k:
                for s in range(2):
                    e = 2 * k + 2 + s
                    scatter(e, k + 1, s)
                    gather(e + 2, s, e + 2)
            for s in range(2):
                pool.wait_ge(S[f"gathered{s}"], 64 * (E // 2 + 1))
                pool.wait_ge(S[f"scattered{s}"], 64 * (E // 2))


def _planes(x):
    n = x.shape[0]
    planes = np.zeros((n, 2, CIN, 3, OUTW + 1, OUTW), x.dtype)
    for parity, rows in ((0, x[:, :, 1::2]), (1, x[:, :, 0::2])):
        at = slice(1, OUTW + 1) if parity == 0 else slice(0, OUTW)
        planes[:, parity, :, 0, at, 1:] = rows[..., 1:-1:2]
        planes[:, parity, :, 1, at] = rows[..., 0::2]
        planes[:, parity, :, 2, at] = rows[..., 1::2]
    return planes.reshape(n, 2 * CIN, 3, (OUTW + 1) * OUTW)


def _ktiles(m, size):
    k, n = m.shape
    return np.transpose(m.reshape(k // size, size, n), (1, 0, 2)).reshape(size, -1)


def _packed(a):
    conv = a["L0_tok_W"].reshape(D, CIN, 3, 3)
    taps = np.transpose(conv, (2, 3, 1, 0))
    qkv = a["L0_attn_W_qkv"].reshape(D, D, 3)
    gate = np.transpose(a["L1_attn_Wg"].reshape(HL, 3, D), (1, 0, 2))
    heads = np.arange(DH) // (D // HA)
    tok = np.arange(T, dtype=np.float32)
    inv = (1.0 / 10000.0 ** (np.arange(0, HD, 2, dtype=np.float32) / np.float32(HD))).astype(np.float32)
    ang = np.arange(L, dtype=np.float32)[:, None] * inv[None, :]
    sign = np.where(np.arange(HD // 2) < HD // 4, -1.0, 1.0).astype(np.float32)

    def table(f, sg):
        t = f(ang).astype(np.float32) * sg
        return np.transpose(t.reshape(NC, T, HD // 2), (1, 0, 2)).reshape(T, -1)

    def lanes(v, n=T):
        return np.broadcast_to(np.asarray(v).reshape(1, -1), (n, np.asarray(v).size))

    src = [(n // 2, 3 + n % 2) for n in range(NCLS)]
    out_b = np.stack([np.concatenate([a["L0_ffn_atom_out_b"][r], a["L0_ffn_atom_out_b"][l]]) for l, r in src])
    reset = np.ones((E, NC), np.float32)
    reset[:, 0] = 0.0
    last = np.zeros((T, T), np.float32)
    last[T - 1] = 1.0
    eps = np.zeros((128, 2), np.float32)
    eps[:, 0], eps[:, 1] = 1e-5, 1e-6
    chunk = np.arange(NC, dtype=np.float32)
    parts = {
        "conv01": np.transpose(taps[0:2], (0, 2, 1, 3)).reshape(128, 3 * D),
        "conv2": np.transpose(taps[2], (1, 0, 2)).reshape(CIN, 3 * D),
        "tok_b": lanes(a["L0_tok_b"]),
        "wq0": _ktiles(qkv[:, :, 0], DH), "wk0": _ktiles(qkv[:, :, 1], DH), "wvT": _ktiles(qkv[:, :, 2].T, DH),
        "wproj": _ktiles(a["L0_attn_W_proj"], DH), "bproj": lanes(a["L0_attn_b_proj"]),
        "temp": np.repeat(a["L0_attn_temp"].reshape(HA), D // HA).reshape(2, DH).T,
        "offblock": np.where(heads[:, None] == heads[None, :], 0.0, NEG).astype(np.float32),
        "fc1": _ktiles(a["L0_ffn_fc1_w"].T, DH), "fc1_b": a["L0_ffn_fc1_b"].reshape(FT, 128).T,
        "fc2": _ktiles(a["L0_ffn_fc2_w"].T, 128), "fc2_b": lanes(a["L0_ffn_fc2_b"]),
        "wqkv": _ktiles(np.concatenate([a["L1_attn_Wq"], a["L1_attn_Wk"], a["L1_attn_Wv"]]).T, DH),
        "wug": _ktiles(np.concatenate([a["L1_attn_Wu"], gate[0], gate[1]]).T, DH),
        "wo": _ktiles(a["L1_attn_Wo"].T, DH),
        "mu": lanes(a["L1_attn_prior_mu"]), "logtau": lanes(a["L1_attn_prior_log_tau"]),
        "lnw": lanes(a["L1_ffn_ln_w"], 128), "lnwT": a["L1_ffn_ln_w"].reshape(2, DH).T,
        "router": _ktiles(a["L1_ffn_w_router"], DH),
        "ident": np.eye(128, dtype=np.float32), "tri": np.triu(np.ones((T, T), np.float32)), "last": last,
        "ones": np.ones((128, 128), np.float32), "zeros": np.zeros((128, ROW), np.float32),
        "reset": lanes(reset), "cos": table(np.cos, 1.0), "sin": table(np.sin, sign),
        "pos": chunk[None, :] * T + tok[:, None] + 1, "iotae": lanes(np.arange(E, dtype=np.float32)),
        "iota128": lanes(np.arange(128, dtype=np.float32)),
        "tokid": np.arange(B * NC, dtype=np.float32)[None, :] * T + tok[:, None] + 1,
        "poff": lanes(CAP * (np.arange(B) % 2) - 1.0), "eps": eps,
        "gate": a["L0_ffn_gate_pair"].reshape(NCLS, 2 * D), "bal": a["L0_ffn_balance_bias"], "out_b": out_b,
        "in_b": np.transpose(a["L0_ffn_atom_in_b"].reshape(NAT, FT, 128), (2, 0, 1)).reshape(128, -1),
        "atom_in": _ktiles(a["L0_ffn_atom_in_w"].reshape(NAT * F, D).T, DH),
        "atom_out": np.transpose(a["L0_ffn_atom_out_w"].reshape(NAT, D, FT, 128), (3, 0, 2, 1)).reshape(128, -1),
    }
    where, total = pack_columns()
    packed = np.zeros((128, total), np.float32)
    for name, (p, at, n) in where.items():
        assert parts[name].shape == (p, n), (name, parts[name].shape)
        packed[:p, at:at + n] = parts[name]
    return packed


def arrays(inputs):
    a = {k: np.asarray(v) for k, v in inputs.items()}
    wi, wo_e = a["L1_ffn_wi"], a["L1_ffn_wo"]
    return {
        "xin": _planes(a["x"]), "packed": _packed(a),
        "wi": np.ascontiguousarray(np.transpose(wi.reshape(E, 2, DH, F), (0, 2, 1, 3)).reshape(E, DH, 2 * F)),
        "wo_e": np.ascontiguousarray(np.transpose(wo_e.reshape(E, FT, 128, D), (0, 2, 1, 3)).reshape(E, 128, FT * D)),
    }


def kernel(**inputs):
    import concourse.bacc as bacc
    from concourse.bass_utils import run_bass_kernel_spmd

    nc = bacc.Bacc("TRN2", target_bir_lowering=False, num_devices=1)
    data = arrays(inputs)
    args = [nc.dram_tensor(n, data[n].shape, F32, kind="ExternalInput").ap() for n in ("xin", "packed")]
    out = nc.dram_tensor("out", (B * L, D), F32, kind="ExternalOutput").ap()
    rows = nc.dram_tensor("rows", (B * L + 1, ROW), F32).ap()
    weights = [nc.dram_tensor(n, data[n].shape, F32, kind="ExternalInput").ap() for n in ("wi", "wo_e")]
    build_tower(nc, *args, out, rows, *weights)
    r = run_bass_kernel_spmd(nc, [data], core_ids=[0])
    return r.results[0]["out"].reshape(B, L, D)
```

```python
from contextlib import ExitStack

import numpy as np

import concourse.bass as bass
from concourse import mybir

ALU = mybir.AluOpType
ACT = mybir.ActivationFunctionType
AX = mybir.AxisListType
F32 = mybir.dt.float32
U32 = mybir.dt.uint32

B, CIN, IMG = 8, 64, 112
D = 192
DH = D // 2
OUTW = IMG // 2
T = 2 * OUTW
L = OUTW * OUTW
NC = L // T
NQ = NC // 4
SLAB = 5
HA = 8
F = 768
FT = F // 128
HL, HD = 12, 16
HP = 32
NCLS, NAT = 6, 5
E, CAP = 16, 64
RN, SD, MEAN, PROB = D, D + 1, D + 2, D + 3
ROW = D + 4
TPASS = 5
FAR = float(1 << 20)
NEG = -1.0e30
STAGE_COLUMNS = 11520
MIX_COLUMNS = 2692
GROUPS = {
    "attend": "att o3 vs osum v3 qT kT qd",
    "mixing": "gram gk prodk prodq t1sb mix att0 norm0",
    "hidden": "hid",
    "class": "cpre chid cprod xc cbias cres",
    "others": "gates ug usum uprod lg onehot prio rtmp cum pick xo ob xg",
}


def pack_plan():
    return [
        ("conv01", 128, 3 * D), ("conv2", 64, 3 * D), ("tok_b", T, D),
        ("wq0", DH, 2 * D), ("wk0", DH, 2 * D), ("wvT", DH, 2 * D), ("wproj", DH, 2 * D), ("bproj", T, D),
        ("temp", DH, 2), ("offblock", DH, DH),
        ("fc1", DH, 2 * F), ("fc1_b", 128, FT), ("fc2", 128, FT * D), ("fc2_b", T, D),
        ("wqkv", DH, 2 * 3 * D), ("wug", DH, 2 * (D + 2 * HL)), ("wo", DH, 2 * D),
        ("mu", T, D), ("logtau", T, HL), ("lnw", 128, D), ("lnwT", DH, 2), ("router", DH, 2 * E),
        ("ident", 128, 128), ("tri", T, T), ("ones", 128, 128), ("zeros", 128, ROW),
        ("reset", T, E * NC), ("cos", T, NC * HD // 2), ("sin", T, NC * HD // 2), ("pos", T, NC),
        ("iotae", T, E), ("iota128", T, 128), ("tokid", T, B * NC), ("poff", T, B), ("eps", 128, 2),
        ("gate", NCLS, 2 * D), ("bal", NCLS, 2), ("out_b", NCLS, 2 * D), ("in_b", 128, NAT * FT),
        ("atom_in", DH, 2 * NAT * F), ("atom_out", 128, NAT * FT * D),
    ]


def pack_columns():
    at, where = 0, {}
    for name, p, n in pack_plan():
        where[name] = (p, at, n)
        at += n
    return where, at


class Steps:

    def __init__(self, sem, names):
        self.sem, self.names, self.at = sem, names.split(), 0

    def mark(self, instruction, name):
        assert self.names[self.at % len(self.names)] == name, (name, self.names, self.at)
        instruction.then_inc(self.sem, 1)
        self.at += 1

    def value(self, done, name):
        return done * len(self.names) + self.names.index(name) + 1


def build_tower(nc, xin, packed, out, rows, wi, wo_e, nb=B):
    where, total = pack_columns()
    ctx = ExitStack()
    with ctx:
        def sb(name, shape, dt=F32):
            return ctx.enter_context(nc.sbuf_tensor(name, shape, dt))

        def sem(name):
            return ctx.enter_context(nc.semaphore(name))

        W = sb("W", [128, total])
        PS = ctx.enter_context(nc.psum_tensor("PS", [128, 8, 512], F32))

        def w(name):
            p, at, n = where[name]
            return W[0:p, at:at + n]

        def bank(k, p, n):
            return PS[0:p, k, 0:n]

        def spread(ap, axis, n):
            ap = ap.unsqueeze(axis)
            shape = list(ap.shape)
            shape[axis] = n
            return ap.broadcast_to(shape)

        conv01 = w("conv01").rearrange("p (k n) -> p k n", k=3)
        conv2 = w("conv2").rearrange("p (k n) -> p k n", k=3)
        halves = {n: w(n).rearrange("p (k n) -> p k n", k=2)
                  for n in ("wq0", "wk0", "wvT", "wproj", "fc1", "wqkv", "wug", "wo", "router", "atom_in")}
        fc2 = w("fc2").rearrange("p (k n) -> p k n", k=FT)
        atom_out = w("atom_out").rearrange("p (a k n) -> p a k n", a=NAT, k=FT)
        ident, tri, ones, zeros = w("ident"), w("tri"), w("ones"), w("zeros")
        cos = w("cos").rearrange("p (c d) -> p c d", d=HD // 2)
        sin = w("sin").rearrange("p (c d) -> p c d", d=HD // 2)
        eps_ln, eps_rms = w("eps")[:, 0:1], w("eps")[:, 1:2]

        U = sb("U", [128, STAGE_COLUMNS])
        top = {}

        def stage(name, shape):
            n = int(np.prod(shape[1:]))
            group = next(g for g, names in GROUPS.items() if name in names.split())
            at = top.setdefault(group, MIX_COLUMNS if group in ("others", "class") else 0)
            top[group] = at + n
            assert top[group] <= STAGE_COLUMNS, name
            flat = U[0:shape[0], at:at + n]
            letters = "abcd"[:len(shape) - 1]
            return flat.rearrange(f"p ({' '.join(letters)}) -> p {' '.join(letters)}",
                                  **dict(zip(letters, shape[1:])))

        h = sb("h", [T, NC, ROW])
        hx = h[:, :, 0:D]
        xs = sb("xs", [128, 2, 3, SLAB * OUTW])
        xg = stage("xg", [T, 4, D])
        xh = sb("xh", [T, 4, D])
        xT = sb("xT", [DH, 2, 4, T])
        bns = sb("bns", [T, 4, 6])
        bnv = sb("bnv", [T, 4, 2])
        mv = [sb(f"mv{n}", [T, NC, 2]) for n in range(4)]
        rs = [sb(f"rs{n}", [T, NC]) for n in range(4)]
        gram = stage("gram", [DH, 2, D])
        gk = stage("gk", [DH, 2, D])
        prodk = stage("prodk", [DH, 2, D])
        prodq = stage("prodq", [DH, 2, D])
        norm0 = stage("norm0", [DH, D + 2])
        att0 = stage("att0", [DH, 2, DH])
        rowm = sb("rowm", [DH, 2])
        rsum = sb("rsum", [DH, 2])
        t1sb = stage("t1sb", [DH, 2, D])
        mix = stage("mix", [DH, 2, D])
        hid = stage("hid", [128, FT, 4, T])

        gate = w("gate").rearrange("p (r n) -> p r n", r=2)
        gss = sb("gss", [NCLS, 2])
        xc = stage("xc", [NCLS, D])
        xcT = sb("xcT", [DH, 2, NCLS])
        cprod = stage("cprod", [NCLS, 3, D])
        csum = sb("csum", [NCLS, 3])
        clog = sb("clog", [NCLS, 2])
        cext = sb("cext", [NCLS, 2])
        cflag = sb("cflag", [NCLS, 2])
        cdiag = sb("cdiag", [NCLS, 2, NCLS])
        cflagb = sb("cflagb", [128, 2 * NCLS])
        cpre = stage("cpre", [128, NAT * FT, NCLS])
        chid = stage("chid", [128, NAT, FT, NCLS])
        csel = sb("csel", [128, NAT, FT, NCLS])
        cbias = stage("cbias", [NCLS, D])
        cres = stage("cres", [NCLS, D])

        GU = D + 2 * HL
        ug = stage("ug", [T, 4, GU])
        usum = stage("usum", [T, 4, D])
        uprod = stage("uprod", [T, 4, D])
        sraw = sb("sraw", [T, 4, HL])
        scoef = sb("scoef", [T, NC, HL])
        taumu = w("mu")
        tau = sb("tau", [T, HL])
        invt = sb("invt", [T, NC])
        gates = stage("gates", [T, NC, 2 * HL])
        es = sb("es", [T, 2 * HL, NC])
        cum = stage("cum", [T, 2 * HL, NC])
        smax = sb("smax", [T, HL])
        smaxT = sb("smaxT", [HL, 1])
        sdiag = sb("sdiag", [HL, HL])
        coef = sb("coef", [T, 3, HL, NC])
        qk = sb("qk", [T, 4, 2 * HL, HP])
        nrm = sb("nrm", [T, 4, 2 * HL])
        cq = sb("cq", [T, 4, HL, 3])
        ck = sb("ck", [T, 4, HL, 3])
        att = stage("att", [T, 2, 3, 4, T])
        rope1 = U[0:T, 0:4 * 2 * D].rearrange("p (c h d) -> p c h d", c=4, h=2 * HL)
        o3_at = top["attend"]
        o3 = stage("o3", [T, 4, HL, 3, HD])
        rope2 = U[0:T, o3_at:o3_at + 4 * 2 * D].rearrange("p (c h d) -> p c h d", c=4, h=2 * HL)
        vs = stage("vs", [T, 4, D])
        osum = stage("osum", [T, 4, D])
        v3 = stage("v3", [T, 4, HL, 3, HD])
        qT = stage("qT", [128, 3, 3, T])
        kT = stage("kT", [128, 3, T])
        qd = stage("qd", [128, 3, 4, T])
        state = sb("state", [128, 2, 3, 4, 3 * HD])
        ost = sb("ost", [T, 4, HL])
        oT = xT
        osq = U[0:T, o3_at + 3 * HL * 3 * HD:o3_at + 3 * HL * 3 * HD + 2 * D].rearrange("p (c n) -> p c n", c=2)

        lg = stage("lg", [T, E, NC])
        onehot = stage("onehot", [T, E, NC])
        prio = stage("prio", [T, E, NC])
        rtmp = stage("rtmp", [T, E, NC])
        rmax = sb("rmax", [T, NC])
        prob = sb("prob", [T, NC])
        prs = sb("prs", [T, NC])
        rn = sb("rn", [T, NC])
        posx = sb("posx", [T, NC])
        pick = stage("pick", [T, 4, 128])
        slots = sb("slots", [128, B // 2, E])
        xo = stage("xo", [T, 4, D])
        hs = xh
        ob = stage("ob", [T, 4, D])

        at_in, at_out = where["atom_in"][1], where["atom_out"][1]
        w1 = [W[0:DH, at_in + s * 2 * F:at_in + (s + 1) * 2 * F].rearrange("p (k n) -> p k n", k=2) for s in range(2)]
        w2 = [W[:, at_out + s * FT * D:at_out + (s + 1) * FT * D].rearrange("p (k n) -> p k n", k=FT) for s in range(2)]
        mh = W[:, at_out + 2 * FT * D:at_out + 2 * FT * D + FT * 512].rearrange("p (k n) -> p k n", k=FT)
        mrow_at = at_in + 4 * F
        mrow = [W[:, mrow_at + s * 4 * ROW:mrow_at + (s + 1) * 4 * ROW].rearrange("p (k n) -> p k n", k=4)
                for s in range(2)]
        mT_at = mrow_at + 8 * ROW
        mT = W[0:DH, mT_at:mT_at + 2 * 512].rearrange("p (k n) -> p k n", k=2)
        mx = W[:, mT_at + 2 * 512:mT_at + 2 * 512 + 4 * D].rearrange("p (k n) -> p k n", k=4)
        assert mT_at + 2 * 512 + 4 * D <= at_in + 2 * NAT * F and FT * (2 * D + 512) <= NAT * FT * D
        my = [U[:, s * 4 * D:(s + 1) * 4 * D].rearrange("p (k n) -> p k n", k=4) for s in range(2)]
        gidx = sb("gidx", [128, E + 2, B // 2], U32)
        sidx = sb("sidx", [128, E, B // 2], U32)
        gi = [sb(f"gi{s}", [128, B // 2], U32) for s in range(2)]
        si = [sb(f"si{s}", [128, B // 2], U32) for s in range(2)]
        empty = sb("empty", [128, B // 2, E])

        S = {n: sem(n) for n in (
            "held packed_in x_in0 x_in1 leads_given setup_done image_done "
            "conv_done conv_out xg_ready gram_read xh_ready turned xt_ready mix_done bias_in att_rsum h1_ready "
            "fc1_done gelu_done patches_done h2_ready ug_done ug_out gates_kept before_kept us_done uprod_done s_kept "
            "qk_done v_done rope_done qk_ready v_out squared rn_ready c_ready v3_ready qkt_done kq_out qt_out qd_zero "
            "s_done s_out st_done st_out o_done o_out osum_ready osum_used ctr_ready osq_out ovar osd_out orn oln_ready "
            "ot_done ot_out wo_done h3_ready lg_done lg_out pick_ready slots_done xs_ready xo_ready res_ready out_written "
            "rows_written x_kept gathered0 gathered1 w1_in0 w1_in1 w2_in0 w2_in1 index_ready gi_ready si_ready scattered0 scattered1 "
            "moe_x moe_h moe_turned moe_xt moe_f moe_ra moe_rd moe_o moe_y").split()}
        dA = Steps(sem("vector_conv"), "stat0 agg0 keep0 stat1 agg1 keep1 rstd")
        aA = Steps(sem("scalar_conv"), "sd")
        dB = Steps(sem("vector_mix"), "g0 g1 g2 gk pk pq rnorm rqt l0 l1 l2 rowm rsum att t1 mix")
        pB = Steps(sem("tensor_mix"), "mirror gw qk t1 mix")
        aB = Steps(sem("scalar_mix"), "norm exp")
        dC = Steps(sem("vector_stats2"), "stat0 agg0 keep0 stat1 agg1 keep1")
        dR2 = Steps(sem("vector_rstd2"), "rstd")
        aR2 = Steps(sem("scalar_sd2"), "sd")
        dE = Steps(sem("vector_class"), "xc prod sq sum nmax nrec log flag0 flag1 max min diff p1 p "
                                        "diag0 diag1 flags pre sel bias0 bias res0 res")
        aE = Steps(sem("scalar_class"), "xcT norm exp gelu")
        pE = Steps(sem("tensor_class"), "turned hidden flags out")
        dD = Steps(sem("vector_stats3"), "stat0 agg0 keep0 stat1 agg1 keep1")
        dR3 = Steps(sem("vector_rstd3"), "class stat agg rstd")
        aR3 = Steps(sem("scalar_sd3"), "sd")
        dG = Steps(sem("vector_sums"), "max maxT diag shift scan0 scan1 excl sum eps einv al be0 be ga0 ga1 ga")
        pG = Steps(sem("tensor_sums"), "maxT max sums")
        aG = Steps(sem("scalar_sums"), "exp gates state0")
        dH = Steps(sem("vector_squares"), "ss0 ss1")
        dN = Steps(sem("vector_norms"), "nmax0 nrec0 nmax1 nrec1")
        dL = Steps(sem("vector_head_norm"), "sum0 mean0 rec0 sum1 mean1 rec1")
        dT = Steps(sem("vector_stats4"), "stat0 agg0 keep0 stat1 agg1 keep1")
        lF = Steps(sem("pool_running"), "zero")
        lK = Steps(sem("pool_weights"), "k00 k10 k20 k01 k11 k21 q0 q1 q2")
        lA = Steps(sem("pool_sums"), "a0 a1")
        dI = Steps(sem("vector_rms"), "one_sd mean rstd sq ms rn keep")
        aI = Steps(sem("scalar_rms"), "sd rms")
        dR = Steps(sem("vector_route"), "scale max shift eq first lowest onehot psum prob prs keepp scan excl prio "
                                        "under keep pz pos posx")
        aR = Steps(sem("scalar_route"), "exp")
        pR = Steps(sem("tensor_route"), "sums")
        dS = Steps(sem("vector_setup"), "pad state sel slots gsq gss nmax nrec gate router tau taumu s0 s1 s2 invt")
        aS = Steps(sem("scalar_setup"), "gnorm tau")
        dM = Steps(sem("vector_indices"), "zero empty gather minus1")

        block = ctx.enter_context(nc.Block())
        LEADS = 5

        def ch(t, i, c, n=1):
            return t[:, bass.ds(4 * i + c, n)]

        def one(ap):
            return ap.rearrange("p a n -> p (a n)")

        def pipelined(eng, lead_in, body, lead_out):
            lead_in()
            with eng.Fori(0, NQ - 1) as i:
                body(i)
            lead_out(NQ - 1)

        def hold(eng):
            eng.sem_inc(S["held"], 1)

        def give_leads(eng, **leads):
            for name, n in leads.items():
                eng.sem_inc(S[name], n)
            eng.sem_inc(S["leads_given"], 1)
            eng.wait_ge(S["leads_given"], LEADS)

        @block.sync
        def _(sp):
            sp.dma_start(W[:, :], packed).then_inc(S["packed_in"], 16)
            give_leads(sp)
            sp.wait_ge(S["packed_in"], 16)
            sp.dma_start(rows[0:1, :], zeros[0:1, :]).then_inc(S["rows_written"], 16)

            def load(b, i):
                g = b * NQ + i
                for p in range(2):
                    sp.wait_ge(S["conv_done"], 2 * g + p + 1)
                    sp.dma_start(xs[:, p, :, :],
                                 xin[bass.ds(b, 1), :, :, bass.ds((8 * i + 4 * p) * OUTW, SLAB * OUTW)]
                                 .rearrange("b p v r -> p (b v) r")).then_inc(S[f"x_in{p}"], 16)

            def image(b, more):
                with sp.Fori(1, NQ) as i:
                    load(b, i)
                if more:
                    load(b + 1, 0)
                with sp.Fori(0, NQ) as i:
                    token = b * L + i * (4 * T)
                    sp.wait_ge(S["res_ready"], b * NQ + i + 5)
                    sp.dma_start(out[bass.ds(token, 4 * T), :].rearrange("(c p) n -> p c n", p=T),
                                 ob[:, :, :]).then_inc(S["out_written"], 16)
                    sp.dma_start(rows[bass.ds(token + 1, 4 * T), :].rearrange("(c p) n -> p c n", p=T),
                                 ch(h, i, 0, 4)).then_inc(S["rows_written"], 16)

            load(0, 0)
            with sp.Fori(0, nb - 1) as b:
                image(b, more=True)
            image(nb - 1, more=False)
            sp.wait_ge(S["image_done"], nb + 1)
            with sp.Fori(0, E // 2) as k2:
                for s in range(2):
                    e = 2 * k2 + s
                    sp.wait_ge(S["moe_o"], 2 * e + 1)
                    sp.dma_start(w1[s], wi[bass.ds(e, 1)].rearrange("a p (k n) -> p (a k) n", k=2))\
                        .then_inc(S[f"w1_in{s}"], 16)
                    sp.dma_start(w2[s], wo_e[bass.ds(e, 1)].rearrange("a p (k n) -> p (a k) n", k=FT))\
                        .then_inc(S[f"w2_in{s}"], 16)

        @block.tensor
        def _(pe):
            mm, tr = nc.tensor.matmul, nc.tensor.transpose
            pe.wait_ge(S["packed_in"], 16)
            give_leads(pe, conv_done=2, gram_read=1, turned=2, mix_done=2, st_done=4, us_done=4, moe_turned=1, moe_f=6, moe_o=3)

            def turn(q, p):
                pe.wait_ge(S["xt_ready"], 2 * q + p + 1)
                pe.wait_ge(S["xh_ready"], 2 * q + p + 1)
                for j in range(2):
                    for k in range(2):
                        t = tr(PS[0:DH, p, (2 * k + j) * T:(2 * k + j + 1) * T],
                               xh[:, 2 * p + j, k * DH:(k + 1) * DH], ident[0:T, 0:T])
                t.then_inc(S["turned"], 1)

            def tile_pair(p, bk, x, weight, n, at=0):
                for j in range(2):
                    for k in range(2):
                        m = mm(PS[0:T, bk, j * n:(j + 1) * n], x[:, k, 2 * p + j, :], weight[:, k, at:at + n],
                               start=k == 0, stop=k == 1)
                return m

            with pe.Fori(0, nb) as b:
                pe.wait_ge(S["image_done"], b + 1)
                mm(bank(4, DH, D), zeros[0:T, 0:DH], zeros[0:T, 0:D], start=True, stop=False, skip_group_check=True)
                mm(bank(5, DH, DH), zeros[0:T, 0:DH], zeros[0:T, 0:DH], start=True, stop=False, skip_group_check=True)
                def conv(i):
                    g = b * NQ + i
                    for p in range(2):
                        pe.wait_ge(S["conv_out"], 2 * g + p + 1)
                        pe.wait_ge(S[f"x_in{p}"], 16 * g + 16)
                        for j in range(2):
                            o = PS[0:T, 6 + p, j * D:(j + 1) * D]
                            for kx in range(3):
                                mm(o, xs[:, p, kx, 2 * j * OUTW:(2 * j + 2) * OUTW], conv01[:, kx, :],
                                   start=kx == 0, stop=False)
                            for kx in range(3):
                                m = mm(o, xs[0:CIN, p, kx, (2 * j + 1) * OUTW:(2 * j + 3) * OUTW], conv2[:, kx, :],
                                       start=False, stop=kx == 2)
                        m.then_inc(S["conv_done"], 1)

                def gram_of(i):
                    pe.wait_ge(S["xg_ready"], b * NQ + i + 1)
                    for c in range(4):
                        x = xg[:, c, :]
                        mm(bank(4, DH, D), x[:, 0:DH], x, start=False, stop=False, skip_group_check=True)
                        m = mm(bank(5, DH, DH), x[:, DH:D], x[:, DH:D], start=False, stop=False, skip_group_check=True)
                    m.then_inc(S["gram_read"], 1)

                def conv_next(i):
                    conv(i + 1)
                    gram_of(i)

                pipelined(pe, lambda: conv(0), conv_next, gram_of)

                pe.wait_ge(dB.sem, dB.value(b, "g1"))
                pB.mark(tr(bank(2, DH, DH), gram[:, 0, DH:D], ident[0:DH, 0:DH]), "mirror")
                pe.wait_ge(dB.sem, dB.value(b, "g2"))
                for bk, name in ((4, "wk0"), (5, "wq0")):
                    for n in range(2):
                        for k in range(2):
                            m = mm(PS[0:DH, bk, n * D:(n + 1) * D], gram[:, k, n * DH:(n + 1) * DH],
                                   halves[name][:, k, :], start=k == 0, stop=k == 1)
                pB.mark(m, "gw")
                pe.wait_ge(dB.sem, dB.value(b, "pq"))
                for n in range(2):
                    for k in range(2):
                        mm(PS[0:DH, 2, n * DH:(n + 1) * DH], halves["wq0"][:, k, n * DH:(n + 1) * DH],
                           gk[:, k, n * DH:(n + 1) * DH], start=k == 0, stop=k == 1)
                for k in range(2):
                    mm(bank(3, DH, D), ones[0:DH, 0:DH], prodk[:, k, :], start=k == 0, stop=k == 1)
                for n in range(2):
                    for k in range(2):
                        m = mm(PS[0:DH, 3, D + n:D + n + 1], prodq[:, k, n * DH:(n + 1) * DH], ones[0:DH, 0:1],
                               start=k == 0, stop=k == 1)
                pB.mark(m, "qk")
                pe.wait_ge(dB.sem, dB.value(b, "att"))
                for n in range(2):
                    m = mm(PS[0:DH, 2, n * D:(n + 1) * D], att0[:, n, :], halves["wproj"][:, n, :],
                           start=True, stop=True)
                pB.mark(m, "t1")
                pe.wait_ge(dB.sem, dB.value(b, "t1"))
                for n in range(2):
                    for k in range(2):
                        m = mm(PS[0:DH, 3, n * D:(n + 1) * D], halves["wvT"][:, k, n * DH:(n + 1) * DH],
                               t1sb[:, k, :], start=k == 0, stop=k == 1)
                pB.mark(m, "mix")
                pe.wait_ge(dB.sem, dB.value(b, "mix"))
                hold(pe)

                def stage_c(i, more):
                    q = b * (TPASS * NQ) + i
                    g = b * NQ + i
                    for p in range(2):
                        pe.wait_ge(S["xt_ready"], 2 * q + p + 3)
                        pe.wait_ge(S["h1_ready"], 2 * g + p + 1)
                        tile_pair(p, 6 + p, xT, mix, D).then_inc(S["mix_done"], 1)
                        if more:
                            turn(q + 1, p)

                pipelined(pe, lambda: [turn(b * (TPASS * NQ), p) for p in range(2)],
                          lambda i: stage_c(i, True), lambda i: stage_c(i, False))

                pe.wait_ge(dE.sem, dE.value(b, "xc"))
                hold(pe)
                for k in range(2):
                    m = tr(PS[0:DH, 2, k * NCLS:(k + 1) * NCLS], xc[:, k * DH:(k + 1) * DH], ident[0:NCLS, 0:NCLS])
                pE.mark(m, "turned")
                pe.wait_ge(aE.sem, aE.value(b, "xcT"))
                for a in range(NAT * FT):
                    for k in range(2):
                        m = mm(PS[:, 3, a * NCLS:(a + 1) * NCLS], halves["atom_in"][:, k, a * 128:(a + 1) * 128],
                               xcT[:, k, :], start=k == 0, stop=k == 1)
                pE.mark(m, "hidden")
                pe.wait_ge(dE.sem, dE.value(b, "diag1"))
                pE.mark(mm(bank(4, 128, 2 * NCLS), ones[0:NCLS, :], cdiag[:, :, :].rearrange("p a n -> p (a n)"),
                           start=True, stop=True), "flags")
                pe.wait_ge(dE.sem, dE.value(b, "sel"))
                for a in range(NAT):
                    for k in range(FT):
                        m = mm(bank(5, NCLS, D), csel[:, a, k, :], atom_out[:, a, k, :],
                               start=a + k == 0, stop=(a == NAT - 1 and k == FT - 1))
                pE.mark(m, "out")

                pe.wait_ge(dE.sem, dE.value(b, "res"))

                def stage_d(i, more):
                    q = b * (TPASS * NQ) + NQ + i
                    g = b * NQ + i
                    pe.wait_ge(S["xt_ready"], 2 * q + 4)
                    for f in range(FT):
                        if f >= 4:
                            pe.wait_ge(S["gelu_done"], FT * g + f - 3)
                        for k in range(2):
                            m = mm(PS[:, 2 + f % 4, 0:4 * T], halves["fc1"][:, k, f * 128:(f + 1) * 128],
                                   xT[:, k, :, :].rearrange("p c t -> p (c t)"), start=k == 0, stop=k == 1)
                        m.then_inc(S["fc1_done"], 1)
                    if more:
                        for p in range(2):
                            turn(q + 1, p)
                    pe.wait_ge(S["gelu_done"], FT * g + FT)
                    for p in range(2):
                        pe.wait_ge(S["h2_ready"], 2 * g + p + 1)
                        if p == 0:
                            pe.wait_ge(S["h1_ready"], 2 * NQ * b + 2 * NQ + 2)
                        for j in range(2):
                            for k in range(FT):
                                m = mm(PS[0:T, 6 + p, j * D:(j + 1) * D], hid[:, k, 2 * p + j, :], fc2[:, k, :],
                                       start=k == 0, stop=k == FT - 1)
                        m.then_inc(S["patches_done"], 1)

                pipelined(pe, lambda: [turn(b * (TPASS * NQ) + NQ, p) for p in range(2)],
                          lambda i: stage_d(i, True), lambda i: stage_d(i, False))

                def stage_f(i, more):
                    q = b * (TPASS * NQ) + 2 * NQ + i
                    g = b * NQ + i
                    for p in range(2):
                        pe.wait_ge(S["xt_ready"], 2 * q + p + 3)
                        pe.wait_ge(S["ug_out"], 2 * g + p + 1)
                        tile_pair(p, 2 + p, xT, halves["wug"], GU).then_inc(S["ug_done"], 1)
                        if more:
                            turn(q + 1, p)
                    pe.wait_ge(S["uprod_done"], g + 1)
                    for c in range(4):
                        pe.wait_ge(S["ug_out"], 2 * g + c // 2 + 3)
                        mm(bank(4 + c, T, D), tri, ug[:, c, 0:D], start=True, stop=False)
                        pe.wait_ge(S["before_kept"], b + 4 * g + c + 1)
                        mm(bank(4 + c, T, D), ones[0:T, 0:T], usum[:, c, :], start=False, stop=True)\
                            .then_inc(S["us_done"], 1)

                pipelined(pe, lambda: [turn(b * (TPASS * NQ) + 2 * NQ, p) for p in range(2)],
                          lambda i: stage_f(i, True), lambda i: stage_f(i, False))

                pe.wait_ge(dG.sem, dG.value(b, "max"))
                pG.mark(tr(bank(2, HL, T), smax[:, :], ident[0:T, 0:T]), "maxT")
                pe.wait_ge(dG.sem, dG.value(b, "diag"))
                pG.mark(mm(bank(3, T, HL), ones[0:HL, 0:T], sdiag[:, :], start=True, stop=True), "max")
                pe.wait_ge(aG.sem, aG.value(b, "exp"))
                for k in range(2):
                    part = es[:, k * HL:(k + 1) * HL, :].rearrange("p h c -> p (h c)")
                    mm(bank(4 + k, T, HL * NC), tri, part, start=True, stop=True)
                    m = mm(bank(6 + k, T, HL * NC), ones[0:T, 0:T], part, start=True, stop=True)
                pG.mark(m, "sums")

                pe.wait_ge(aG.sem, aG.value(b, "state0"))
                pe.wait_ge(dG.sem, dG.value(b, "ga"))
                mm(bank(7, 128, 9 * HD), zeros[0:T, 0:128], zeros[0:T, 0:9 * HD], start=True, stop=False,
                   skip_group_check=True)
                def head(i):
                    q = b * (TPASS * NQ) + 3 * NQ + i
                    g = b * NQ + i
                    pe.wait_ge(S["o_out"], 4 * g + 1)
                    for p in range(2):
                        turn(q, p)
                    for c in range(4):
                        pe.wait_ge(S["xt_ready"], 2 * q + c // 2 + 3)
                        if c == 2:
                            pe.wait_ge(S["xt_ready"], 2 * q + 4)
                        for k in range(2):
                            m = mm(bank(2 + c, T, 2 * D), xT[:, k, c, :], halves["wqkv"][:, k, 0:2 * D],
                                   start=k == 0, stop=k == 1)
                        m.then_inc(S["qk_done"], 1)
                        for k in range(2):
                            m = mm(PS[0:T, (6, 0)[c // 2], (c % 2) * D:(c % 2 + 1) * D], xT[:, k, c, :],
                                   halves["wqkv"][:, k, 2 * D:3 * D], start=k == 0, stop=k == 1)
                        if c % 2 == 1:
                            m.then_inc(S["v_done"], 1)

                def turn_qk(i, c):
                    g = b * NQ + i
                    pe.wait_ge(S["qk_ready"], 4 * g + (5 if c == 0 else 8))
                    if c == 0:
                        pe.wait_ge(S["v_out"], 2 * g + 1)
                    else:
                        pe.wait_ge(S["qt_out"], 4 * g + c)
                    for n, bk in enumerate((1 if c == 0 else 5, 6)):
                        for k in range(3):
                            m = tr(PS[:, bk, k * T:(k + 1) * T],
                                   qk[:, c, n * HL + 4 * k:n * HL + 4 * k + 4, :].rearrange("p h d -> p (h d)"),
                                   ident[0:T, 0:T])
                    m.then_inc(S["qkt_done"], 1)

                def turn_outputs(i, last=False):
                    g = b * NQ + i
                    if not last:
                        pe.wait_ge(S["qk_ready"], 4 * g + 11)
                    for p in range(2):
                        pe.wait_ge(S["oln_ready"], 2 * g + p + 1)
                        for j in range(2):
                            for k in range(2):
                                m = tr(PS[0:DH, 3 + p, (2 * k + j) * T:(2 * k + j + 1) * T],
                                       osum[:, 2 * p + j, k * DH:(k + 1) * DH], ident[0:T, 0:T])
                        m.then_inc(S["ot_done"], 1)

                def project_outputs(i, last=False):
                    g = b * NQ + i
                    for p in range(2):
                        pe.wait_ge(S["ot_out"], 2 * g + p + 1)
                        if not last:
                            pe.wait_ge(*((S["v_out"], 2 * g + 4) if p == 0 else (S["qt_out"], 4 * g + 5)))
                        tile_pair(p, p, oT, halves["wo"], D).then_inc(S["wo_done"], 1)

                def scores(i, c):
                    g = b * NQ + i
                    pe.wait_ge(S["kq_out"], 4 * g + c + 1)
                    if c == 0:
                        pe.wait_ge(S["qk_ready"], 4 * g + 7)
                    for k in range(3):
                        if c:
                            pe.wait_ge(S["s_out"], 12 * g + 3 * (c - 1) + k + 1)
                        mm(bank(2 + k, T, 4 * T), kT[:, k, :], qd[:, k, :, :].rearrange("p j t -> p (j t)"),
                           start=True, stop=True).then_inc(S["s_done"], 1)

                def new_state(i, c):
                    g = b * NQ + i
                    pe.wait_ge(S["v3_ready"], 4 * g + c + 5)
                    pe.wait_ge(S["st_out"], 4 * g + c + 1)
                    for k in range(3):
                        for j in range(4):
                            m = mm(PS[32 * j:32 * j + 32, 7, k * 3 * HD:(k + 1) * 3 * HD],
                                   qk[:, c, HL + 4 * k + j, :],
                                   v3[:, c, 4 * k + j, :, :].rearrange("p j d -> p (j d)"),
                                   start=False, stop=False, skip_group_check=True)
                    m.then_inc(S["st_done"], 1)

                def outputs(i, c):
                    g = b * NQ + i
                    pe.wait_ge(S["o_out"], 4 * g + c + 1)
                    pe.wait_ge(S["s_out"], 12 * g + 3 * c + 3)
                    pe.wait_ge(S["qt_out"], 4 * g + c + 1)
                    if c == 0:
                        pe.wait_ge(S["h3_ready"], 2 * g + 2)
                    for k in range(3):
                        mm(PS[0:T, k // 2, (k % 2) * 12 * HD:(k % 2 + 1) * 12 * HD], qT[:, c % 3, k, :],
                           state[:, c % 2, k, :, :].rearrange("p j d -> p (j d)"),
                           start=True, stop=False, skip_group_check=True)
                        for n in range(4 * k, 4 * k + 4):
                            m = mm(PS[0:T, n // 8, (n % 8) * 3 * HD:(n % 8 + 1) * 3 * HD],
                                   att[:, c % 2, k, n % 4, :], v3[:, c, n, :, :].rearrange("p j d -> p (j d)"),
                                   start=False, stop=n % 4 == 3, skip_group_check=True)
                    m.then_inc(S["o_done"], 1)

                def stage_h(i, first=False):
                    head(i)
                    turn_qk(i, 0)
                    if not first:
                        turn_outputs(i - 1)
                        project_outputs(i - 1)
                    scores(i, 0)
                    turn_qk(i, 1)
                    new_state(i, 0)
                    for c in range(1, 4):
                        scores(i, c)
                        if c < 3:
                            turn_qk(i, c + 1)
                        outputs(i, c - 1)
                        new_state(i, c)
                    outputs(i, 3)

                stage_h(0, first=True)
                with pe.Fori(1, NQ) as i:
                    stage_h(i)
                turn_outputs(NQ - 1, last=True)
                project_outputs(NQ - 1, last=True)

                pe.wait_ge(S["h3_ready"], 2 * NQ * b + 2 * NQ + 2)

                def stage_i(i, more):
                    q = b * (TPASS * NQ) + 4 * NQ + i
                    g = b * NQ + i
                    pe.wait_ge(S["lg_out"], g + 1)
                    for p in range(2):
                        pe.wait_ge(S["xt_ready"], 2 * q + p + 3)
                        for c in (2 * p, 2 * p + 1):
                            for k in range(2):
                                m = mm(PS[0:T, 6, c * E:(c + 1) * E], xT[:, k, c, :], halves["router"][:, k, :],
                                       start=k == 0, stop=k == 1)
                        if p == 1:
                            m.then_inc(S["lg_done"], 1)
                        if more:
                            turn(q + 1, p)

                pipelined(pe, lambda: [turn(b * (TPASS * NQ) + 4 * NQ, p) for p in range(2)],
                          lambda i: stage_i(i, True), lambda i: stage_i(i, False))

                pe.wait_ge(dR.sem, dR.value(b, "onehot"))
                flat = onehot[:, :, :].rearrange("p e c -> p (e c)")
                mm(bank(2, T, E * NC), tri, flat, start=True, stop=True)
                pR.mark(mm(bank(3, T, E * NC), ones[0:T, 0:T], flat, start=True, stop=True), "sums")

                pe.wait_ge(dR.sem, dR.value(b, "posx"))
                mm(bank(4, 128, E), zeros[0:T, 0:128], zeros[0:T, 0:E], start=True, stop=False, skip_group_check=True)
                with pe.Fori(0, NQ) as i:
                    g = b * NQ + i
                    for c in range(4):
                        pe.wait_ge(S["pick_ready"], 4 * g + c + 1)
                        mm(bank(4, 128, E), pick[:, c, :], one(onehot[:, :, bass.ds(4 * i + c, 1)]
                                                            .rearrange("p e c -> p c e")),
                           start=False, stop=False, skip_group_check=True).then_inc(S["slots_done"], 1)

            pe.wait_ge(S["image_done"], nb + 1)
            with pe.Fori(0, E // 2) as k2:
                for s in range(2):
                    e = 2 * k2 + s
                    pe.wait_ge(S["moe_xt"], e + 1)
                    pe.wait_ge(S["moe_x"], e + 1)
                    for n in range(4):
                        for k in range(2):
                            m = tr(PS[0:DH, n // 2, (2 * k + n % 2) * 128:(2 * k + n % 2 + 1) * 128],
                                   mx[:, n, k * DH:(k + 1) * DH], ident)
                    m.then_inc(S["moe_turned"], 1)
                    pe.wait_ge(S["moe_xt"], e + 2)
                    pe.wait_ge(S[f"w1_in{s}"], 16 * k2 + 16)
                    for f in range(FT):
                        if f == 4:
                            pe.wait_ge(S["moe_ra"], 3 * e + 1)
                        if f == 5:
                            pe.wait_ge(S["moe_rd"], 3 * e + 1)
                        for k in range(2):
                            m = mm(PS[:, 2 + f % 4, :], w1[s][:, k, f * 128:(f + 1) * 128], mT[:, k, :],
                                   start=k == 0, stop=k == 1)
                        m.then_inc(S["moe_f"], 1)
                    pe.wait_ge(S["moe_ra"], 3 * e + 3)
                    pe.wait_ge(S["moe_rd"], 3 * e + 3)
                    pe.wait_ge(S[f"w2_in{s}"], 16 * k2 + 16)
                    for p in range(2):
                        pe.wait_ge(S["moe_y"], 2 * e + p + 1)
                        for j in range(2):
                            for k in range(FT):
                                m = mm(PS[:, 6 + p, j * D:(j + 1) * D],
                                       mh[:, k, (2 * p + j) * 128:(2 * p + j + 1) * 128], w2[s][:, k, :],
                                       start=k == 0, stop=k == FT - 1)
                        m.then_inc(S["moe_o"], 1)

        @block.scalar
        def _(act):
            A = nc.scalar.activation
            act.wait_ge(S["packed_in"], 16)
            give_leads(act, xt_ready=2, ug_out=2, st_out=1, lg_out=1, x_kept=1, out_written=16, moe_xt=1)

            act.wait_ge(dS.sem, dS.value(0, "gss"))
            aS.mark(A(gss[:, :], gss[:, :], ACT.Sqrt), "gnorm")
            act.wait_ge(dS.sem, dS.value(0, "tau"))
            aS.mark(A(tau[:, :], tau[:, :], ACT.Exp), "tau")
            act.wait_ge(dS.sem, dS.value(0, "invt"))

            def xt_out(q):
                for p in range(2):
                    act.wait_ge(S["turned"], 2 * q + p + 3)
                    A(xT[:, :, 2 * p:2 * p + 2, :], bank(p, DH, 4 * T).rearrange("p (k c t) -> p k c t", k=2, c=2),
                      ACT.Copy).then_inc(S["xt_ready"], 1)

            with act.Fori(0, nb) as b:
                with act.Fori(0, NQ) as i:
                    g = b * NQ + i
                    act.wait_ge(dA.sem, dA.value(g, "agg1"))
                    aA.mark(A(ch(rs[0], i, 0, 4), bnv[:, :, 1], ACT.Sqrt, bias=eps_ln[0:T]), "sd")
                act.wait_ge(pB.sem, pB.value(b, "qk"))
                aB.mark(A(norm0[:, :], bank(3, DH, D + 2), ACT.Sqrt), "norm")
                act.wait_ge(dB.sem, dB.value(b, "rowm"))
                for n in range(2):
                    m = A(att0[:, n, :], att0[:, n, :], ACT.Exp, bias=rowm[:, n:n + 1])
                aB.mark(m, "exp")
                with act.Fori(0, NQ) as i:
                    xt_out(b * (TPASS * NQ) + i)
                act.wait_ge(dC.sem, dC.value(b * NQ + NQ - 1, "keep1"))
                aR2.mark(A(rs[1][:, :], mv[1][:, :, 1], ACT.Sqrt, bias=eps_ln[0:T]), "sd")
                act.wait_ge(pE.sem, pE.value(b, "turned"))
                aE.mark(A(xcT[:, :, :], bank(2, DH, 2 * NCLS).rearrange("p (k n) -> p k n", k=2), ACT.Copy), "xcT")
                act.wait_ge(dE.sem, dE.value(b, "sum"))
                aE.mark(A(csum[:, 2:3], csum[:, 2:3], ACT.Sqrt), "norm")
                act.wait_ge(dE.sem, dE.value(b, "diff"))
                aE.mark(A(cext[:, 1:2], cext[:, 1:2], ACT.Exp), "exp")
                act.wait_ge(dE.sem, dE.value(b, "pre"))
                aE.mark(A(chid[:, :, :, :].rearrange("p a k n -> p (a k n)"),
                          cpre[:, :, :].rearrange("p a n -> p (a n)"), ACT.Gelu), "gelu")
                def gelus(i):
                    g = b * NQ + i
                    act.wait_ge(S["patches_done"], 2 * g + 2)
                    for f in range(FT):
                        act.wait_ge(S["fc1_done"], FT * g + f + 1)
                        A(hid[:, f, :, :].rearrange("p c t -> p (c t)"), PS[:, 2 + f % 4, 0:4 * T], ACT.Gelu,
                          bias=w("fc1_b")[:, f:f + 1]).then_inc(S["gelu_done"], 1)

                def gelus_next(i):
                    gelus(i)
                    xt_out(b * (TPASS * NQ) + NQ + i + 1)

                pipelined(act, lambda: xt_out(b * (TPASS * NQ) + NQ), gelus_next, gelus)
                act.wait_ge(dR3.sem, dR3.value(b, "agg"))
                aR3.mark(A(rs[2][:, :], mv[2][:, :, 1], ACT.Sqrt, bias=eps_ln[0:T]), "sd")
                def ug_to_sbuf(i, more):
                    g = b * NQ + i
                    act.wait_ge(S["uprod_done"], g + 1)
                    act.wait_ge(S["gates_kept"], g + 1)
                    act.wait_ge(S["us_done"], 4 * g + 4)
                    for p in range(2):
                        act.wait_ge(S["ug_done"], 2 * g + p + 1)
                        A(ug[:, 2 * p:2 * p + 2, :], bank(2 + p, T, 2 * GU).rearrange("p (c n) -> p c n", c=2),
                          ACT.Copy).then_inc(S["ug_out"], 1)
                    if more:
                        xt_out(b * (TPASS * NQ) + 2 * NQ + i + 1)

                pipelined(act, lambda: xt_out(b * (TPASS * NQ) + 2 * NQ),
                          lambda i: ug_to_sbuf(i, True), lambda i: ug_to_sbuf(i, False))
                act.wait_ge(dG.sem, dG.value(b, "shift"))
                aG.mark(A(es[:, 0:HL, :], es[:, 0:HL, :], ACT.Exp), "exp")
                act.wait_ge(S["gates_kept"], NQ * b + NQ + 1)
                aG.mark(A(gates[:, :, :], gates[:, :, :], ACT.Sigmoid), "gates")
                aG.mark(A(state[:, 0, :, :, :], spread(zeros[:, 0:9 * HD].rearrange("p (k d) -> p k d", k=3), 2, 4),
                          ACT.Copy),
                        "state0")
                def v_out(i, p):
                    g = b * NQ + i
                    act.wait_ge(S["v3_ready"], 4 * g + 4)
                    act.wait_ge(S["v_done"], 2 * g + p + 1)
                    A(vs[:, 2 * p:2 * p + 2, :], bank((6, 0)[p], T, 2 * D).rearrange("p (c n) -> p c n", c=2),
                      ACT.Copy).then_inc(S["v_out"], 1)

                def square(i, c):
                    g = b * NQ + i
                    act.wait_ge(S["qk_ready"], 4 * g + c + 5)
                    A(rope1[:, c, :, :], qk[:, c, :, 0:HD], ACT.Square).then_inc(S["squared"], 1)

                def roots(i, p):
                    act.wait_ge(dH.sem, dH.value(b * NQ + i, f"ss{p}"))
                    A(nrm[:, 2 * p:2 * p + 2, :], nrm[:, 2 * p:2 * p + 2, :], ACT.Sqrt).then_inc(S["rn_ready"], 1)

                def qk_to_sbuf(i, c):
                    g = b * NQ + i
                    act.wait_ge(S["qkt_done"], 4 * g + c + 1)
                    if c == 0:
                        act.wait_ge(S["qd_zero"], b + 1)
                    else:
                        act.wait_ge(S["s_done"], 12 * g + 3 * c)
                    q, k = (bank(n, 128, 3 * T).rearrange("p (k t) -> p k t", k=3) for n in (1 if c == 0 else 5, 6))
                    A(kT[:, :, :], k, ACT.Copy)
                    for j in range(4):
                        lanes = slice(32 * j, 32 * j + 32)
                        m = A(qd[lanes, :, j, :], q[lanes], ACT.Copy)
                    m.then_inc(S["kq_out"], 1)
                    A(qT[:, c % 3, :, :], q, ACT.Copy).then_inc(S["qt_out"], 1)

                def state_out(i, c):
                    act.wait_ge(S["st_done"], 4 * (b * NQ + i) + c + 5)
                    for j in range(4):
                        lanes = slice(32 * j, 32 * j + 32)
                        m = A(state[lanes, (c + 1) % 2, :, j, :],
                              PS[lanes, 7, 0:9 * HD].rearrange("p (k d) -> p k d", k=3), ACT.Copy)
                    m.then_inc(S["st_out"], 1)

                def square_outputs(i, p):
                    act.wait_ge(S["ctr_ready"], 2 * (b * NQ + i) + p + 1)
                    A(osq, osum[:, 2 * p:2 * p + 2, :], ACT.Square).then_inc(S["osq_out"], 1)

                def deviation(i, p):
                    act.wait_ge(S["ovar"], 2 * (b * NQ + i) + p + 1)
                    A(ost[:, 2 * p:2 * p + 2, :], ost[:, 2 * p:2 * p + 2, :], ACT.Sqrt, bias=eps_ln[0:T],
                      scale=1.0 / HD).then_inc(S["osd_out"], 1)

                def outputs_turned(i):
                    for p in range(2):
                        act.wait_ge(S["ot_done"], 2 * (b * NQ + i) + p + 1)
                        A(oT[:, :, 2 * p:2 * p + 2, :],
                          bank(3 + p, DH, 4 * T).rearrange("p (k c t) -> p k c t", k=2, c=2),
                          ACT.Copy).then_inc(S["ot_out"], 1)

                def stage_h(i, first=False):
                    xt_out(b * (TPASS * NQ) + 3 * NQ + i)
                    v_out(i, 0)
                    square(i, 0)
                    if not first:
                        square_outputs(i - 1, 1)
                        deviation(i - 1, 1)
                    square(i, 1)
                    v_out(i, 1)
                    roots(i, 0)
                    if not first:
                        outputs_turned(i - 1)
                    qk_to_sbuf(i, 0)
                    square(i, 2)
                    square(i, 3)
                    roots(i, 1)
                    for c in range(3):
                        qk_to_sbuf(i, c + 1)
                        state_out(i, c)
                    square_outputs(i, 0)
                    deviation(i, 0)
                    state_out(i, 3)

                stage_h(0, first=True)
                with act.Fori(1, NQ) as i:
                    stage_h(i)
                square_outputs(NQ - 1, 1)
                deviation(NQ - 1, 1)
                outputs_turned(NQ - 1)
                act.wait_ge(dT.sem, dT.value(b * NQ + NQ - 1, "keep1"))
                aI.mark(A(rs[3][:, :], mv[3][:, :, 1], ACT.Sqrt, bias=eps_ln[0:T]), "sd")
                act.wait_ge(dI.sem, dI.value(b, "ms"))
                aI.mark(A(rn[:, :], rn[:, :], ACT.Sqrt, bias=eps_rms[0:T]), "rms")
                def x_out(i):
                    q = b * (TPASS * NQ) + 4 * NQ + i
                    act.wait_ge(S["xh_ready"], 2 * q + 2)
                    A(ch(hx, i, 0, 4), xh[:, :, :], ACT.Copy).then_inc(S["x_kept"], 1)
                    xt_out(q)

                def logits_out(i):
                    act.wait_ge(S["lg_done"], b * NQ + i + 1)
                    A(lg[:, :, bass.ds(4 * i, 4)].rearrange("p e c -> p c e"),
                      bank(6, T, 4 * E).rearrange("p (c e) -> p c e", c=4), ACT.Copy).then_inc(S["lg_out"], 1)

                def x_next(i):
                    x_out(i + 1)
                    logits_out(i)

                pipelined(act, lambda: x_out(0), x_next, logits_out)
                act.wait_ge(dR.sem, dR.value(b, "shift"))
                aR.mark(A(rtmp[:, :, :], rtmp[:, :, :], ACT.Exp), "exp")
                with act.Fori(0, NQ) as i:
                    g = b * NQ + i
                    act.wait_ge(S["res_ready"], g + 4)
                    for c in range(4):
                        row = one(ch(h, i, c))
                        m = A(hs[:, c, :], row[:, 0:D], ACT.Identity, scale=row[:, SD:SD + 1], bias=row[:, MEAN:MEAN + 1])
                    m.then_inc(S["xs_ready"], 1)
            with act.Fori(0, E // 2) as k2:
                for s in range(2):
                    e = 2 * k2 + s
                    act.wait_ge(S["moe_f"], 6 * e + 6)
                    act.wait_ge(S["moe_turned"], e + 2)
                    for p in range(2):
                        m = A(mT[:, :, 256 * p:256 * (p + 1)], bank(p, DH, 512).rearrange("p (k n) -> p k n", k=2),
                              ACT.Copy)
                    m.then_inc(S["moe_xt"], 1)
                    act.wait_ge(S["moe_o"], 2 * e + 3)
                    for f in (0, 2, 4):
                        act.wait_ge(S["moe_f"], 6 * e + f + 7)
                        A(mh[:, f, :], PS[:, 2 + f % 4, :], ACT.Relu).then_inc(S["moe_ra"], 1)

        @block.vector
        def _(dve):
            tt, ts, stt = nc.vector.tensor_tensor, nc.vector.tensor_scalar, nc.vector.scalar_tensor_tensor
            red, cp = nc.vector.tensor_reduce, nc.vector.tensor_copy

            def settle(steps, done, name):
                dve.wait_ge(steps.sem, steps.value(done, name))

            dS.mark(nc.vector.memset(qk[:, :, :, :], 0.0), "pad")
            dS.mark(nc.vector.memset(state[:, :, :, :, :], 0.0), "state")
            dS.mark(nc.vector.memset(csel[:, :, :, :], 0.0), "sel")
            dS.mark(nc.vector.memset(slots[:, :, :], 0.0), "slots")
            dve.wait_ge(S["packed_in"], 16)
            give_leads(dve, conv_out=2, h1_ready=2, h2_ready=2, uprod_done=1, o_out=1, h3_ready=2,
                       image_done=1, patches_done=2, moe_y=2)
            dS.mark(tt(cprod[:, 0:2, :], gate, gate, ALU.mult), "gsq")
            settle(dS, 0, "gsq")
            dS.mark(red(gss[:, :], cprod[:, 0:2, :], AX.X, ALU.add), "gss")
            dve.wait_ge(aS.sem, aS.value(0, "gnorm"))
            dS.mark(ts(gss[:, :], gss[:, :], 1e-12, None, ALU.max), "nmax")
            settle(dS, 0, "nmax")
            dS.mark(nc.vector.reciprocal(gss[:, :], gss[:, :]), "nrec")
            settle(dS, 0, "nrec")
            dS.mark(tt(gate, gate, spread(gss[:, :], 2, D), ALU.mult), "gate")
            dS.mark(tt(halves["router"], halves["router"], spread(w("lnwT"), 2, E), ALU.mult), "router")
            dS.mark(ts(tau[:, :], w("logtau"), -50.0, 30.0, ALU.max, ALU.min), "tau")
            dve.wait_ge(aS.sem, aS.value(0, "tau"))
            dS.mark(tt(taumu.rearrange("p (h d) -> p h d", h=HL), w("mu").rearrange("p (h d) -> p h d", h=HL),
                       spread(tau[:, :], 2, HD), ALU.mult), "taumu")
            dS.mark(tt(scoef[:, :, :], spread(w("pos"), 2, HL), spread(tau[:, :], 1, NC), ALU.add), "s0")
            settle(dS, 0, "s0")
            dS.mark(nc.vector.reciprocal(scoef[:, :, :], scoef[:, :, :]), "s1")
            settle(dS, 0, "s1")
            dS.mark(ts(scoef[:, :, :], scoef[:, :, :], -1.0 / HD ** 0.5, None, ALU.mult), "s2")
            dS.mark(nc.vector.reciprocal(invt[:, :], w("pos")), "invt")
            settle(dS, 0, "invt")

            def normalise(q, i, n):
                for p in range(2):
                    dve.wait_ge(S["turned"], 2 * q + p + 1)
                    for c in (2 * p, 2 * p + 1):
                        m = ts(xh[:, c, :], one(ch(hx, i, c)), one(ch(mv[n], i, c)[:, :, 0:1]), ch(rs[n], i, c),
                               ALU.subtract, ALU.mult)
                    m.then_inc(S["xh_ready"], 1)

            def stats(steps, done, i, p, n):
                hold(dve)
                for j in range(2):
                    m = nc.vector.bn_stats(bns[:, 2 * p + j, :], one(ch(hx, i, 2 * p + j)))
                steps.mark(m, f"stat{p}")
                settle(steps, done, f"stat{p}")
                hold(dve)
                for j in range(2):
                    m = nc.vector.bn_aggr(bnv[:, 2 * p + j, :], bns[:, 2 * p + j, :])
                steps.mark(m, f"agg{p}")
                settle(steps, done, f"agg{p}")
                hold(dve)
                steps.mark(cp(ch(mv[n], i, 2 * p, 2), bnv[:, 2 * p:2 * p + 2, :]), f"keep{p}")

            def add_pair(i, p, bk):
                return tt(ch(hx, i, 2 * p, 2), ch(hx, i, 2 * p, 2), bank(bk, T, 2 * D).rearrange("p (c n) -> p c n", c=2),
                          ALU.add)

            with dve.Fori(0, nb) as b:
                dve.wait_ge(S["rows_written"], 16 * NQ * b + 16)
                dve.wait_ge(S["res_ready"], NQ * b + 4)
                dve.wait_ge(S["out_written"], 16 * NQ * b + 16)
                hold(dve)
                with dve.Fori(0, NQ) as i:
                    g = b * NQ + i
                    for p in range(2):
                        dve.wait_ge(S["conv_done"], 2 * g + p + 3)
                        tt(ch(hx, i, 2 * p, 2), bank(6 + p, T, 2 * D).rearrange("p (c n) -> p c n", c=2),
                           spread(w("tok_b"), 1, 2), ALU.add).then_inc(S["conv_out"], 1)
                        dve.wait_ge(S["conv_out"], 2 * g + p + 3)
                        stats(dA, g, i, p, 0)
                    dve.wait_ge(aA.sem, aA.value(g, "sd"))
                    dA.mark(nc.vector.reciprocal(ch(rs[0], i, 0, 4), ch(rs[0], i, 0, 4)), "rstd")
                    dve.wait_ge(S["gram_read"], g + 1)
                    settle(dA, g, "rstd")
                    for c in range(4):
                        m = ts(xg[:, c, :], one(ch(hx, i, c)), bnv[:, c, 0:1], ch(rs[0], i, c),
                               ALU.subtract, ALU.mult)
                    m.then_inc(S["xg_ready"], 1)

                dve.wait_ge(S["gram_read"], NQ * b + NQ + 1)
                dB.mark(cp(gram[:, 0, :], bank(4, DH, D)), "g0")
                dB.mark(cp(gram[:, 1, DH:D], bank(5, DH, DH)), "g1")
                dve.wait_ge(pB.sem, pB.value(b, "mirror"))
                dB.mark(cp(gram[:, 1, 0:DH], bank(2, DH, DH)), "g2")
                dve.wait_ge(pB.sem, pB.value(b, "gw"))
                gw = [bank(k, DH, 2 * D).rearrange("p (k n) -> p k n", k=2) for k in (4, 5)]
                dB.mark(cp(gk[:, :, :], gw[0]), "gk")
                dB.mark(tt(prodk[:, :, :], gw[0], halves["wk0"], ALU.mult), "pk")
                dB.mark(tt(prodq[:, :, :], gw[1], halves["wq0"], ALU.mult), "pq")
                dve.wait_ge(aB.sem, aB.value(b, "norm"))
                dB.mark(nc.vector.reciprocal(norm0[:, :], norm0[:, :]), "rnorm")
                settle(dB, b, "rnorm")
                dB.mark(tt(rsum[:, :], norm0[:, D:D + 2], w("temp"), ALU.mult), "rqt")
                dB.mark(tt(att0[:, :, :], bank(2, DH, D).rearrange("p (k n) -> p k n", k=2),
                           norm0[:, 0:D].rearrange("p (k n) -> p k n", k=2), ALU.mult), "l0")
                settle(dB, b, "l0")
                for n in range(2):
                    dB.mark(stt(att0[:, n, :], att0[:, n, :], rsum[:, n:n + 1], w("offblock"), ALU.mult, ALU.add),
                            f"l{n + 1}")
                settle(dB, b, "l2")
                dB.mark(red(rowm[:, :], att0[:, :, :], AX.X, ALU.max, negate=True), "rowm")
                dve.wait_ge(aB.sem, aB.value(b, "exp"))
                dB.mark(red(rsum[:, :], att0[:, :, :], AX.X, ALU.add), "rsum")
                settle(dB, b, "rsum")
                nc.vector.reciprocal(rsum[:, :], rsum[:, :]).then_inc(S["att_rsum"], 1)
                dve.wait_ge(S["att_rsum"], b + 1)
                dB.mark(tt(att0[:, :, :], att0[:, :, :], spread(rsum[:, :], 2, DH), ALU.mult), "att")
                dve.wait_ge(pB.sem, pB.value(b, "t1"))
                dB.mark(cp(t1sb[:, :, :], bank(2, DH, 2 * D).rearrange("p (k n) -> p k n", k=2)), "t1")
                dve.wait_ge(pB.sem, pB.value(b, "mix"))
                dB.mark(cp(mix[:, :, :], bank(3, DH, 2 * D).rearrange("p (k n) -> p k n", k=2)), "mix")

                def mixed(i, more):
                    g = b * NQ + i
                    if more:
                        normalise(b * (TPASS * NQ) + i + 1, i + 1, 0)
                    for p in range(2):
                        dve.wait_ge(S["bias_in"], 2 * NQ * b + i + 1)
                        dve.wait_ge(S["mix_done"], 2 * g + p + 3)
                        add_pair(i, p, 6 + p).then_inc(S["h1_ready"], 1)
                        dve.wait_ge(S["h1_ready"], 2 * g + p + 3)
                        stats(dC, g, i, p, 1)

                pipelined(dve, lambda: normalise(b * (TPASS * NQ), 0, 0),
                          lambda i: mixed(i, True), lambda i: mixed(i, False))
                dve.wait_ge(aR2.sem, aR2.value(b, "sd"))
                dR2.mark(nc.vector.reciprocal(rs[1][:, :], rs[1][:, :]), "rstd")
                settle(dR2, b, "rstd")

                dE.mark(ts(xc[:, :], h[0:NCLS, 0, 0:D], mv[1][0:NCLS, 0, 0:1], rs[1][0:NCLS, 0:1],
                           ALU.subtract, ALU.mult), "xc")
                settle(dE, b, "xc")
                dE.mark(tt(cprod[:, 0:2, :], gate, spread(xc[:, :], 1, 2), ALU.mult), "prod")
                dE.mark(tt(cprod[:, 2, :], xc[:, :], xc[:, :], ALU.mult), "sq")
                settle(dE, b, "sq")
                dE.mark(red(csum[:, :], cprod[:, :, :], AX.X, ALU.add), "sum")
                dve.wait_ge(aE.sem, aE.value(b, "norm"))
                dE.mark(ts(csum[:, 2:3], csum[:, 2:3], 1e-12, None, ALU.max), "nmax")
                settle(dE, b, "nmax")
                dE.mark(nc.vector.reciprocal(csum[:, 2:3], csum[:, 2:3]), "nrec")
                settle(dE, b, "nrec")
                dE.mark(stt(clog[:, :], csum[:, 0:2], csum[:, 2:3], w("bal"), ALU.mult, ALU.add), "log")
                settle(dE, b, "log")
                dE.mark(tt(cflag[:, 0:1], clog[:, 0:1], clog[:, 1:2], ALU.is_ge), "flag0")
                dE.mark(tt(cflag[:, 1:2], clog[:, 0:1], clog[:, 1:2], ALU.is_lt), "flag1")
                dE.mark(tt(cext[:, 0:1], clog[:, 0:1], clog[:, 1:2], ALU.max), "max")
                dE.mark(tt(cext[:, 1:2], clog[:, 0:1], clog[:, 1:2], ALU.min), "min")
                settle(dE, b, "min")
                dE.mark(tt(cext[:, 1:2], cext[:, 1:2], cext[:, 0:1], ALU.subtract), "diff")
                dve.wait_ge(aE.sem, aE.value(b, "exp"))
                dE.mark(ts(cext[:, 0:1], cext[:, 1:2], 1.0, None, ALU.add), "p1")
                settle(dE, b, "p1")
                dE.mark(nc.vector.reciprocal(cext[:, 0:1], cext[:, 0:1]), "p")
                for n in range(2):
                    dE.mark(ts(cdiag[:, n, :], ident[0:NCLS, 0:NCLS], cflag[:, n:n + 1], None, ALU.mult), f"diag{n}")
                dve.wait_ge(pE.sem, pE.value(b, "flags"))
                dE.mark(cp(cflagb[:, :], bank(4, 128, 2 * NCLS)), "flags")
                dE.mark(tt(cpre[:, :, :], bank(3, 128, NAT * FT * NCLS).rearrange("p (a n) -> p a n", n=NCLS),
                           spread(w("in_b"), 2, NCLS), ALU.add), "pre")
                dve.wait_ge(aE.sem, aE.value(b, "gelu"))
                for a in range(3):
                    for t in range(2):
                        n = 2 * a + t
                        ts(csel[:, 3 + t, :, n], chid[:, a, :, n], cflagb[:, n:n + 1], None, ALU.mult)
                        m = ts(csel[:, a, :, n], chid[:, 3 + t, :, n], cflagb[:, NCLS + n:NCLS + n + 1], None, ALU.mult)
                dE.mark(m, "sel")
                out_b = w("out_b").rearrange("p (r n) -> p r n", r=2)
                dE.mark(ts(cbias[:, :], out_b[:, 0, :], cflag[:, 0:1], None, ALU.mult), "bias0")
                settle(dE, b, "bias0")
                dE.mark(stt(cbias[:, :], out_b[:, 1, :], cflag[:, 1:2], cbias[:, :], ALU.mult, ALU.add), "bias")
                dve.wait_ge(pE.sem, pE.value(b, "out"))
                settle(dE, b, "bias")
                dE.mark(tt(cres[:, :], cbias[:, :], bank(5, NCLS, D), ALU.add), "res0")
                settle(dE, b, "res0")
                dE.mark(stt(cres[:, :], cres[:, :], cext[:, 0:1], h[0:NCLS, 0, 0:D], ALU.mult, ALU.add), "res")

                def fed(i, more):
                    g = b * NQ + i
                    if more:
                        normalise(b * (TPASS * NQ) + NQ + i + 1, i + 1, 1)
                    for p in range(2):
                        dve.wait_ge(S["bias_in"], 2 * NQ * b + NQ + i + 1)
                        dve.wait_ge(S["patches_done"], 2 * g + p + 3)
                        add_pair(i, p, 6 + p).then_inc(S["h2_ready"], 1)
                        dve.wait_ge(S["h2_ready"], 2 * g + p + 3)
                        stats(dD, g, i, p, 2)

                pipelined(dve, lambda: normalise(b * (TPASS * NQ) + NQ, 0, 1),
                          lambda i: fed(i, True), lambda i: fed(i, False))
                dve.wait_ge(dE.sem, dE.value(b, "res"))
                dR3.mark(cp(h[0:NCLS, 0, 0:D], cres[:, :]), "class")
                settle(dR3, b, "class")
                dR3.mark(nc.vector.bn_stats(bns[:, 0, :], h[:, 0, 0:D]), "stat")
                settle(dR3, b, "stat")
                hold(dve)
                dR3.mark(nc.vector.bn_aggr(mv[2][:, 0, :], bns[:, 0, :]), "agg")
                dve.wait_ge(aR3.sem, aR3.value(b, "sd"))
                dR3.mark(nc.vector.reciprocal(rs[2][:, :], rs[2][:, :]), "rstd")
                settle(dR3, b, "rstd")
                hold(dve)

                def s_of(i, more):
                    g = b * NQ + i
                    if more:
                        normalise(b * (TPASS * NQ) + 2 * NQ + i + 1, i + 1, 2)
                    dve.wait_ge(S["us_done"], 4 * g + 8)
                    tt(uprod[:, :, :], ug[:, :, 0:D], PS[0:T, 4:8, 0:D], ALU.mult).then_inc(S["uprod_done"], 1)
                    dve.wait_ge(S["uprod_done"], g + 2)
                    red(sraw[:, :, :], uprod[:, :, :].rearrange("p c (h d) -> p c h d", h=HL), AX.X, ALU.add)\
                        .then_inc(S["s_kept"], 1)
                    dve.wait_ge(S["s_kept"], 2 * g + 1)
                    tt(es[:, HL:2 * HL, bass.ds(4 * i, 4)].rearrange("p h c -> p c h"), sraw[:, :, :],
                       ch(scoef, i, 0, 4), ALU.mult).then_inc(S["s_kept"], 1)

                pipelined(dve, lambda: normalise(b * (TPASS * NQ) + 2 * NQ, 0, 2),
                          lambda i: s_of(i, True), lambda i: s_of(i, False))

                dve.wait_ge(S["s_kept"], 2 * NQ * b + 2 * NQ)
                dG.mark(red(smax[:, :], es[:, HL:2 * HL, :], AX.X, ALU.max), "max")
                dve.wait_ge(pG.sem, pG.value(b, "maxT"))
                dG.mark(red(smaxT[:, :], bank(2, HL, T), AX.X, ALU.max), "maxT")
                settle(dG, b, "maxT")
                dG.mark(ts(sdiag[:, :], ident[0:HL, 0:HL], smaxT[:, :], None, ALU.mult), "diag")
                dve.wait_ge(pG.sem, pG.value(b, "max"))
                dG.mark(tt(es[:, 0:HL, :], es[:, HL:2 * HL, :], spread(bank(3, T, HL), 2, NC), ALU.subtract), "shift")
                dve.wait_ge(pG.sem, pG.value(b, "sums"))
                cumf = cum[:, :, :].rearrange("p (k h) c -> p k (h c)", k=2)
                for k in range(2):
                    dG.mark(nc.vector.tensor_tensor_scan(cumf[:, k, :], w("reset")[:, 0:HL * NC], bank(6 + k, T, HL * NC),
                                                         0.0, ALU.mult, ALU.add), f"scan{k}")
                settle(dG, b, "scan1")
                dG.mark(tt(cumf, cumf, PS[0:T, 6:8, 0:HL * NC], ALU.subtract), "excl")
                settle(dG, b, "excl")
                dG.mark(tt(cumf, cumf, PS[0:T, 4:6, 0:HL * NC], ALU.add), "sum")
                settle(dG, b, "sum")
                dve.wait_ge(aG.sem, aG.value(b, "gates"))
                gt = gates[:, :, :].rearrange("p c h -> p h c")
                sig1, sigh = gt[:, 0:HL, :], gt[:, HL:2 * HL, :]
                dG.mark(ts(cum[:, 0:HL, :], cum[:, 0:HL, :], 1e-12, None, ALU.add), "eps")
                settle(dG, b, "eps")
                dG.mark(nc.vector.reciprocal(cum[:, 0:HL, :], cum[:, 0:HL, :]), "einv")
                settle(dG, b, "einv")
                dG.mark(tt(coef[:, 0, :, :], cum[:, 0:HL, :], sigh, ALU.mult), "al")
                dG.mark(tt(coef[:, 1, :, :], sig1, sigh, ALU.subtract), "be0")
                settle(dG, b, "be0")
                dG.mark(tt(coef[:, 1, :, :], coef[:, 1, :, :], spread(invt[:, :], 1, HL), ALU.mult), "be")
                settle(dG, b, "be")
                dG.mark(tt(coef[:, 2, :, :], coef[:, 1, :, :], cum[:, HL:2 * HL, :], ALU.mult), "ga0")
                settle(dG, b, "ga0")
                dG.mark(tt(coef[:, 2, :, :], coef[:, 2, :, :], sigh, ALU.add), "ga1")
                settle(dG, b, "ga1")
                dG.mark(stt(coef[:, 2, :, :], coef[:, 2, :, :], -1.0, spread(invt[:, :], 1, HL), ALU.mult, ALU.mult),
                        "ga")

                def rope(i, c):
                    g = b * NQ + i
                    dve.wait_ge(S["qk_done"], 4 * g + c + 1)
                    dve.wait_ge(S["qk_ready"], 4 * g + c + 1)
                    x = bank(2 + c, T, 2 * D).rearrange("p (h d e) -> p h d e", d=HD // 2, e=2)
                    r1, r2 = (r[:, c, :, :].rearrange("p h (d e) -> p h d e", e=2) for r in (rope1, rope2))
                    tt(r1, x, spread(spread(one(ch(cos, i, c)), 1, 2 * HL), 3, 2), ALU.mult)
                    lo, hi = slice(0, HD // 4), slice(HD // 4, HD // 2)
                    for to, frm in ((lo, hi), (hi, lo)):
                        m = tt(r2[:, :, to], x[:, :, frm],
                               spread(spread(one(ch(sin, i, c)[:, :, to]), 1, 2 * HL), 3, 2), ALU.mult)
                    m.then_inc(S["rope_done"], 1)

                def squares_summed(i, p):
                    pair = slice(2 * p, 2 * p + 2)
                    dve.wait_ge(S["squared"], 4 * (b * NQ + i) + 2 * p + 2)
                    dH.mark(red(nrm[:, pair, :], rope1[:, pair, :, :], AX.X, ALU.add), f"ss{p}")

                def norms(i, p):
                    g = b * NQ + i
                    pair = slice(2 * p, 2 * p + 2)
                    dve.wait_ge(S["rn_ready"], 2 * g + p + 1)
                    dN.mark(ts(nrm[:, pair, :], nrm[:, pair, :], 1e-12, None, ALU.max), f"nmax{p}")
                    settle(dN, g, f"nmax{p}")
                    dN.mark(nc.vector.reciprocal(nrm[:, pair, :], nrm[:, pair, :]), f"nrec{p}")

                def masked(i, c):
                    g = b * NQ + i
                    if c >= 2:
                        dve.wait_ge(S["o_done"], 4 * g + c - 1)
                    for k in range(3):
                        dve.wait_ge(S["s_done"], 12 * g + 3 * c + k + 1)
                        tt(att[:, c % 2, k, :, :], bank(2 + k, T, 4 * T).rearrange("p (j t) -> p j t", j=4),
                           spread(tri, 1, 4), ALU.mult).then_inc(S["s_out"], 1)

                def weigh(i, c):
                    g = b * NQ + i
                    dve.wait_ge(S["o_done"], 4 * g + c + 1)
                    if c == 0:
                        dve.wait_ge(S["c_ready"], g + 1)
                    for n, heads_of in enumerate((slice(0, 8), slice(8, HL))):
                        k = heads_of.stop - heads_of.start
                        m = tt(o3[:, c, heads_of, :, :],
                               bank(n, T, k * 3 * HD).rearrange("p (h j d) -> p h j d", h=k, j=3),
                               spread(cq[:, c, heads_of, :], 3, HD), ALU.mult)
                    m.then_inc(S["o_out"], 1)

                def mean(i, p):
                    g = b * NQ + i
                    pair = slice(2 * p, 2 * p + 2)
                    dve.wait_ge(S["osum_ready"], 2 * g + p + 1)
                    dL.mark(red(ost[:, pair, :], osum[:, pair, :].rearrange("p c (h d) -> p c h d", h=HL), AX.X, ALU.add),
                            f"sum{p}")
                    settle(dL, g, f"sum{p}")
                    dL.mark(ts(ost[:, pair, :], ost[:, pair, :], -1.0 / HD, None, ALU.mult), f"mean{p}")

                def variance(i, p):
                    pair = slice(2 * p, 2 * p + 2)
                    dve.wait_ge(S["osq_out"], 2 * (b * NQ + i) + p + 1)
                    red(ost[:, pair, :], osq.rearrange("p c (h d) -> p c h d", h=HL), AX.X, ALU.add)\
                        .then_inc(S["ovar"], 1)

                def deviation(i, p):
                    pair = slice(2 * p, 2 * p + 2)
                    dve.wait_ge(S["osd_out"], 2 * (b * NQ + i) + p + 1)
                    dL.mark(nc.vector.reciprocal(ost[:, pair, :], ost[:, pair, :]), f"rec{p}")

                def projected(i, p):
                    g = b * NQ + i
                    dve.wait_ge(S["wo_done"], 2 * g + p + 1)
                    add_pair(i, p, p).then_inc(S["h3_ready"], 1)

                def h3_stats(i):
                    g = b * NQ + i
                    for p in range(2):
                        dve.wait_ge(S["h3_ready"], 2 * g + p + 3)
                        stats(dT, g, i, p, 3)

                def stage_h(i, first=False, more=True):
                    rope(i, 0)
                    if not first:
                        mean(i - 1, 1)
                    rope(i, 1)
                    if not first:
                        variance(i - 1, 1)
                    if not first:
                        deviation(i - 1, 1)
                    rope(i, 2)
                    squares_summed(i, 0)
                    rope(i, 3)
                    norms(i, 0)
                    squares_summed(i, 1)
                    if more:
                        normalise(b * (TPASS * NQ) + 3 * NQ + i + 1, i + 1, 2)
                    norms(i, 1)
                    if not first:
                        projected(i - 1, 0)
                        projected(i - 1, 1)
                    masked(i, 0)
                    masked(i, 1)
                    if not first:
                        h3_stats(i - 1)
                    weigh(i, 0)
                    masked(i, 2)
                    weigh(i, 1)
                    masked(i, 3)
                    mean(i, 0)
                    weigh(i, 2)
                    variance(i, 0)
                    deviation(i, 0)
                    weigh(i, 3)

                normalise(b * (TPASS * NQ) + 3 * NQ, 0, 2)
                stage_h(0, first=True)
                with dve.Fori(1, NQ - 1) as i:
                    stage_h(i)
                stage_h(NQ - 1, more=False)
                mean(NQ - 1, 1)
                variance(NQ - 1, 1)
                deviation(NQ - 1, 1)
                projected(NQ - 1, 0)
                projected(NQ - 1, 1)
                h3_stats(NQ - 1)

                dve.wait_ge(aI.sem, aI.value(b, "sd"))
                dI.mark(ts(h[:, :, SD], rs[3][:, :], 1.0, None, ALU.add), "one_sd")
                dI.mark(cp(h[:, :, MEAN], mv[3][:, :, 0]), "mean")
                dI.mark(nc.vector.reciprocal(rs[3][:, :], rs[3][:, :]), "rstd")
                settle(dI, b, "rstd")
                dI.mark(tt(rn[:, :], rs[3][:, :], rs[3][:, :], ALU.mult), "sq")
                settle(dI, b, "sq")
                dI.mark(tt(rn[:, :], rn[:, :], mv[3][:, :, 1], ALU.mult), "ms")
                dve.wait_ge(aI.sem, aI.value(b, "rms"))
                dI.mark(nc.vector.reciprocal(rn[:, :], rn[:, :]), "rn")
                settle(dI, b, "rn")
                dI.mark(cp(h[:, :, RN], rn[:, :]), "keep")
                with dve.Fori(0, NQ) as i:
                    dve.wait_ge(S["x_kept"], b * NQ + i + 1)
                    normalise(b * (TPASS * NQ) + 4 * NQ + i, i, 3)

                dve.wait_ge(S["lg_out"], NQ * b + NQ + 1)
                by_chunk = lg[:, :, :].rearrange("p e c -> p c e")
                dR.mark(tt(lg[:, :, :], lg[:, :, :], spread(rn[:, :], 1, E), ALU.mult), "scale")
                settle(dR, b, "scale")
                dR.mark(red(rmax[:, :], by_chunk, AX.X, ALU.max), "max")
                settle(dR, b, "max")
                dR.mark(tt(rtmp[:, :, :], lg[:, :, :], spread(rmax[:, :], 1, E), ALU.subtract), "shift")
                dR.mark(tt(prio[:, :, :], lg[:, :, :], spread(rmax[:, :], 1, E), ALU.is_equal), "eq")
                settle(dR, b, "eq")
                dR.mark(stt(prio[:, :, :], prio[:, :, :], -1000.0, spread(w("iotae"), 2, NC), ALU.mult, ALU.add),
                        "first")
                settle(dR, b, "first")
                dR.mark(red(posx[:, :], prio[:, :, :].rearrange("p e c -> p c e"), AX.X, ALU.min), "lowest")
                settle(dR, b, "lowest")
                dR.mark(tt(onehot[:, :, :], prio[:, :, :], spread(posx[:, :], 1, E), ALU.is_equal), "onehot")
                dve.wait_ge(aR.sem, aR.value(b, "exp"))
                dR.mark(red(prob[:, :], rtmp[:, :, :].rearrange("p e c -> p c e"), AX.X, ALU.add), "psum")
                settle(dR, b, "psum")
                dR.mark(nc.vector.reciprocal(prob[:, :], prob[:, :]), "prob")
                settle(dR, b, "prob")
                dR.mark(tt(prs[:, :], prob[:, :], rn[:, :], ALU.mult), "prs")
                dR.mark(cp(h[:, :, PROB], prob[:, :]), "keepp")
                dve.wait_ge(pR.sem, pR.value(b, "sums"))
                flat = [t[:, :, :].rearrange("p e c -> p (e c)") for t in (prio, rtmp, onehot)]
                dR.mark(nc.vector.tensor_tensor_scan(flat[0], w("reset")[:, 0:E * NC], bank(3, T, E * NC), 0.0,
                                                     ALU.mult, ALU.add), "scan")
                settle(dR, b, "scan")
                dR.mark(tt(flat[0], flat[0], bank(3, T, E * NC), ALU.subtract), "excl")
                settle(dR, b, "excl")
                dR.mark(tt(flat[0], flat[0], bank(2, T, E * NC), ALU.add), "prio")
                settle(dR, b, "prio")
                dR.mark(ts(flat[1], flat[0], CAP + 0.5, None, ALU.is_lt), "under")
                settle(dR, b, "under")
                dR.mark(tt(flat[2], flat[2], flat[1], ALU.mult), "keep")
                settle(dR, b, "keep")
                dR.mark(tt(flat[1], flat[0], flat[2], ALU.mult), "pz")
                settle(dR, b, "pz")
                dR.mark(red(posx[:, :], rtmp[:, :, :].rearrange("p e c -> p c e"), AX.X, ALU.add), "pos")
                settle(dR, b, "pos")
                dR.mark(ts(posx[:, :], posx[:, :], w("poff")[:, bass.ds(b, 1)], None, ALU.add), "posx")
                settle(dR, b, "posx")

                dve.wait_ge(S["x_kept"], NQ * b + NQ + 1)
                hold(dve)
                with dve.Fori(0, NQ) as i:
                    g = b * NQ + i
                    for c in range(4):
                        dve.wait_ge(S["slots_done"], 4 * g + c + 1)
                        ts(pick[:, c, :], w("iota128"), ch(posx, i, c),
                           w("tokid")[:, bass.ds(b * NC + 4 * i + c, 1)], ALU.is_equal, ALU.mult)\
                            .then_inc(S["pick_ready"], 1)
                    dve.wait_ge(S["res_ready"], g + 4)
                    for c in range(4):
                        m = stt(xo[:, c, :], w("lnw")[0:T], ch(prs, i, c), one(ch(hx, i, c)), ALU.mult, ALU.mult)
                    m.then_inc(S["xo_ready"], 1)
                dve.wait_ge(S["slots_done"], 4 * NQ * b + 4 * NQ + 4)
                pair = slots[:, bass.ds(b // 2, 1), :].rearrange("p a e -> p (a e)")
                tt(pair, pair, bank(4, 128, E), ALU.add).then_inc(S["image_done"], 1)
            dve.wait_ge(S["image_done"], nb + 1)
            dM.mark(nc.vector.memset(gidx[:, :, :], 0), "zero")
            dM.mark(ts(empty[:, :, :], slots[:, :, :], 0.0, FAR, ALU.is_equal, ALU.mult), "empty")
            dve.wait_ge(dM.sem, dM.value(0, "empty"))
            dM.mark(cp(gidx[:, 0:E, :], slots[:, :, :].rearrange("p b e -> p e b")), "gather")
            dM.mark(stt(empty[:, :, :], slots[:, :, :], -1.0, empty[:, :, :], ALU.add, ALU.add), "minus1")
            dve.wait_ge(dM.sem, dM.value(0, "minus1"))
            cp(sidx[:, :, :], empty[:, :, :].rearrange("p b e -> p e b")).then_inc(S["index_ready"], 1)

            def expert(e, k2, s, first=False):
                dve.wait_ge(S["moe_turned"], e + 1)
                dve.wait_ge(S[f"gathered{s}"], 64 * k2 + 64)
                for n in range(4):
                    m = stt(mx[:, n, :], mrow[s][:, n, 0:D], mrow[s][:, n, RN:RN + 1], w("lnw"), ALU.mult, ALU.mult)
                m.then_inc(S["moe_x"], 1)
                dve.wait_ge(S["moe_o"], 2 * e + 3)
                for f in (1, 3, 5):
                    dve.wait_ge(S["moe_f"], 6 * e + f + 7)
                    ts(mh[:, f, :], PS[:, 2 + f % 4, :], 0.0, None, ALU.max).then_inc(S["moe_rd"], 1)
                if not first:
                    dve.wait_ge(S[f"scattered{s}"], 64 * k2)
                for n in range(4):
                    m = ts(my[s][:, n, :], mrow[s][:, n, 0:D], mrow[s][:, n, SD:SD + 1],
                           mrow[s][:, n, MEAN:MEAN + 1], ALU.mult, ALU.add)
                m.then_inc(S["moe_h"], 1)
                dve.wait_ge(S["moe_h"], e + 1)
                for p in range(2):
                    dve.wait_ge(S["moe_o"], 2 * e + p + 4)
                    for n in (2 * p, 2 * p + 1):
                        m = stt(my[s][:, n, :], PS[:, 6 + p, (n % 2) * D:(n % 2 + 1) * D],
                                mrow[s][:, n, PROB:PROB + 1], my[s][:, n, :], ALU.mult, ALU.add)
                    m.then_inc(S["moe_y"], 1)

            for s in range(2):
                expert(s, 0, s, first=True)
            with dve.Fori(0, E // 2 - 1) as k:
                for s in range(2):
                    expert(2 * k + 2 + s, k + 1, s)

        @block.gpsimd
        def _(pool):
            tt, ts, cp = nc.gpsimd.tensor_tensor, nc.gpsimd.tensor_scalar, nc.gpsimd.tensor_copy
            pool.wait_ge(S["packed_in"], 16)
            give_leads(pool, gates_kept=1, v3_ready=4, qk_ready=4, res_ready=4, slots_done=4)

            def add_bias(b, i, after, name):
                pool.wait_ge(S["xh_ready"], after)
                tt(ch(hx, i, 0, 4), ch(hx, i, 0, 4), spread(w(name), 1, 4), ALU.add).then_inc(S["bias_in"], 1)

            with pool.Fori(0, nb) as b:
                with pool.Fori(0, NQ) as i:
                    add_bias(b, i, 2 * (b * (TPASS * NQ) + i) + 2, "bproj")
                with pool.Fori(0, NQ) as i:
                    add_bias(b, i, 2 * (b * (TPASS * NQ) + NQ + i) + 2, "fc2_b")
                pool.wait_ge(dR3.sem, dR3.value(b, "agg"))
                hold(pool)
                lF.mark(nc.gpsimd.memset(usum[:, 0, :], 0.0), "zero")
                pool.wait_ge(lF.sem, lF.value(b, "zero"))
                hold(pool)
                cp(usum[0:1, 0, :], taumu[0:1]).then_inc(S["before_kept"], 1)
                with pool.Fori(0, NQ) as i:
                    g = b * NQ + i
                    for c in range(4):
                        if c % 2 == 0:
                            pool.wait_ge(S["ug_out"], 2 * g + c // 2 + 3)
                        pool.wait_ge(S["us_done"], 4 * g + c + 2)
                        pool.wait_ge(S["before_kept"], b + 4 * g + c + 1)
                        tt(usum[:, (c + 1) % 4, :], usum[:, c, :], ug[:, c, 0:D], ALU.add)\
                            .then_inc(S["before_kept"], 1)
                    cp(ch(gates, i, 0, 4), ug[:, :, D:GU]).then_inc(S["gates_kept"], 1)

                nc.gpsimd.memset(qd[:, :, :, :], 0.0).then_inc(S["qd_zero"], 1)

                def rotated(i, c):
                    g = b * NQ + i
                    pool.wait_ge(S["rope_done"], 4 * g + c + 1)
                    pool.wait_ge(S["st_done"], 4 * g + c + 1)
                    tt(qk[:, c, :, 0:HD], rope1[:, c, :, :], rope2[:, c, :, :], ALU.add).then_inc(S["qk_ready"], 1)

                def value_weights(i, p):
                    g = b * NQ + i
                    pair = slice(2 * p, 2 * p + 2)
                    pool.wait_ge(dN.sem, dN.value(g, f"nrec{p}"))
                    at = bass.ds(4 * i + 2 * p, 2)
                    rk = nrm[:, pair, HL:2 * HL]
                    lK.mark(tt(ck[:, pair, :, 0], es[:, 0:HL, at].rearrange("p h c -> p c h"), rk, ALU.mult), f"k0{p}")
                    lK.mark(tt(ck[:, pair, :, 1], es[:, HL:2 * HL, at].rearrange("p h c -> p c h"), rk, ALU.mult),
                            f"k1{p}")
                    lK.mark(cp(ck[:, pair, :, 2], rk), f"k2{p}")

                def weighted(i, p):
                    g = b * NQ + i
                    pool.wait_ge(S["v_out"], 2 * g + p + 1)
                    pool.wait_ge(lK.sem, lK.value(g, f"k2{p}"))
                    for c in (2 * p, 2 * p + 1):
                        tt(v3[:, c, :, :, :], spread(vs[:, c, :].rearrange("p (h d) -> p h d", h=HL), 2, 3),
                           spread(ck[:, c, :, :], 3, HD), ALU.mult).then_inc(S["v3_ready"], 1)

                def output_weights(i):
                    for j in range(3):
                        lK.mark(tt(cq[:, :, :, j], coef[:, j, :, bass.ds(4 * i, 4)].rearrange("p h c -> p c h"),
                                   nrm[:, :, 0:HL], ALU.mult), f"q{j}")
                    pool.wait_ge(lK.sem, lK.value(b * NQ + i, "q2"))
                    pool.sem_inc(S["c_ready"], 1)

                def pair_of(p):
                    return (o3[:, 2 * p:2 * p + 2, :, :, :],
                            osum[:, 2 * p:2 * p + 2, :].rearrange("p c (h d) -> p c h d", h=HL),
                            ost[:, 2 * p:2 * p + 2, :])

                def summed(i, p):
                    g = b * NQ + i
                    o, s, _ = pair_of(p)
                    pool.wait_ge(S["o_out"], 4 * g + 2 * p + 3)
                    for c in range(2):
                        m = tt(s[:, c], o[:, c, :, 0, :], o[:, c, :, 1, :], ALU.add)
                    lA.mark(m, f"a{p}")
                    pool.wait_ge(lA.sem, lA.value(g, f"a{p}"))
                    for c in range(2):
                        m = tt(s[:, c], s[:, c], o[:, c, :, 2, :], ALU.add)
                    m.then_inc(S["osum_ready"], 1)

                def centred(i, p):
                    _, s, mid = pair_of(p)
                    pool.wait_ge(dL.sem, dL.value(b * NQ + i, f"mean{p}"))
                    tt(s, s, spread(mid, 3, HD), ALU.add).then_inc(S["ctr_ready"], 1)

                def normal(i, p):
                    g = b * NQ + i
                    _, s, mid = pair_of(p)
                    pool.wait_ge(dL.sem, dL.value(g, f"rec{p}"))
                    pool.wait_ge(S["ctr_ready"], 2 * g + p + 1)
                    tt(s, s, spread(mid, 3, HD), ALU.mult).then_inc(S["oln_ready"], 1)

                def stage_h(i, first=False):
                    if not first:
                        summed(i - 1, 1)
                    rotated(i, 0)
                    if not first:
                        centred(i - 1, 1)
                    rotated(i, 1)
                    if not first:
                        normal(i - 1, 1)
                    rotated(i, 2)
                    rotated(i, 3)
                    value_weights(i, 0)
                    weighted(i, 0)
                    value_weights(i, 1)
                    output_weights(i)
                    weighted(i, 1)
                    summed(i, 0)
                    centred(i, 0)
                    normal(i, 0)

                stage_h(0, first=True)
                with pool.Fori(1, NQ) as i:
                    stage_h(i)
                summed(NQ - 1, 1)
                centred(NQ - 1, 1)
                normal(NQ - 1, 1)
                with pool.Fori(0, NQ) as i:
                    g = b * NQ + i
                    pool.wait_ge(S["xo_ready"], g + 1)
                    pool.wait_ge(S["out_written"], 16 * g + 16)
                    pool.wait_ge(S["xs_ready"], g + 1)
                    tt(ob[:, :, :], xo[:, :, :], hs[:, :, :], ALU.add).then_inc(S["res_ready"], 1)
            pool.wait_ge(S["index_ready"], 1)
            pool.wait_ge(S["rows_written"], 16 * NQ * nb + 16)
            pool.wait_ge(S["out_written"], 16 * NQ * nb + 16)

            def gather(e, s, n):
                cp(gi[s][:, :], gidx[:, bass.ds(e, 1), :].rearrange("p a b -> p (a b)")).then_inc(S["gi_ready"], 1)
                pool.wait_ge(S["gi_ready"], n + 1)
                hold(pool)
                for t in range(B // 2):
                    pool.indirect_dma_start(mrow[s][:, t, :], None, rows, bass.IndirectOffsetOnAxis(ap=gi[s][:, t:t + 1], axis=0))\
                        .then_inc(S[f"gathered{s}"], 16)

            def scatter(e, k2, s, first=False):
                if not first:
                    pool.wait_ge(S[f"scattered{s}"], 64 * k2)
                cp(si[s][:, :], sidx[:, bass.ds(e, 1), :].rearrange("p a b -> p (a b)")).then_inc(S["si_ready"], 1)
                pool.wait_ge(S["si_ready"], e + 1)
                pool.wait_ge(S["moe_y"], 2 * e + 4)
                hold(pool)
                for t in range(B // 2):
                    pool.indirect_dma_start(out, bass.IndirectOffsetOnAxis(ap=si[s][:, t:t + 1], axis=0),
                                            my[s][:, t, :], None, bounds_check=nb * L - 1, oob_is_err=False)\
                        .then_inc(S[f"scattered{s}"], 16)

            for s in range(2):
                gather(s, s, s)
            for s in range(2):
                scatter(s, 0, s, first=True)
                gather(s + 2, s, s + 2)
            with pool.Fori(0, E // 2 - 1) as k:
                for s in range(2):
                    e = 2 * k + 2 + s
                    scatter(e, k + 1, s)
                    gather(e + 2, s, e + 2)
            for s in range(2):
                pool.wait_ge(S[f"gathered{s}"], 64 * (E // 2 + 1))
                pool.wait_ge(S[f"scattered{s}"], 64 * (E // 2))


def _planes(x):
    n = x.shape[0]
    planes = np.zeros((n, 2, CIN, 3, OUTW + 1, OUTW), x.dtype)
    for parity, rows in ((0, x[:, :, 1::2]), (1, x[:, :, 0::2])):
        at = slice(1, OUTW + 1) if parity == 0 else slice(0, OUTW)
        planes[:, parity, :, 0, at, 1:] = rows[..., 1:-1:2]
        planes[:, parity, :, 1, at] = rows[..., 0::2]
        planes[:, parity, :, 2, at] = rows[..., 1::2]
    return planes.reshape(n, 2 * CIN, 3, (OUTW + 1) * OUTW)


def _ktiles(m, size):
    k, n = m.shape
    return np.transpose(m.reshape(k // size, size, n), (1, 0, 2)).reshape(size, -1)


def _packed(a):
    conv = a["L0_tok_W"].reshape(D, CIN, 3, 3)
    taps = np.transpose(conv, (2, 3, 1, 0))
    qkv = a["L0_attn_W_qkv"].reshape(D, D, 3)
    gate = np.transpose(a["L1_attn_Wg"].reshape(HL, 3, D), (1, 0, 2))
    heads = np.arange(DH) // (D // HA)
    tok = np.arange(T, dtype=np.float32)
    inv = (1.0 / 10000.0 ** (np.arange(0, HD, 2, dtype=np.float32) / np.float32(HD))).astype(np.float32)
    ang = np.arange(L, dtype=np.float32)[:, None] * inv[None, :]
    sign = np.where(np.arange(HD // 2) < HD // 4, -1.0, 1.0).astype(np.float32)

    def table(f, sg):
        t = f(ang).astype(np.float32) * sg
        return np.transpose(t.reshape(NC, T, HD // 2), (1, 0, 2)).reshape(T, -1)

    def lanes(v, n=T):
        return np.broadcast_to(np.asarray(v).reshape(1, -1), (n, np.asarray(v).size))

    src = [(n // 2, 3 + n % 2) for n in range(NCLS)]
    out_b = np.stack([np.concatenate([a["L0_ffn_atom_out_b"][r], a["L0_ffn_atom_out_b"][l]]) for l, r in src])
    reset = np.ones((E, NC), np.float32)
    reset[:, 0] = 0.0
    eps = np.zeros((128, 2), np.float32)
    eps[:, 0], eps[:, 1] = 1e-5, 1e-6
    chunk = np.arange(NC, dtype=np.float32)
    parts = {
        "conv01": np.transpose(taps[0:2], (0, 2, 1, 3)).reshape(128, 3 * D),
        "conv2": np.transpose(taps[2], (1, 0, 2)).reshape(CIN, 3 * D),
        "tok_b": lanes(a["L0_tok_b"]),
        "wq0": _ktiles(qkv[:, :, 0], DH), "wk0": _ktiles(qkv[:, :, 1], DH), "wvT": _ktiles(qkv[:, :, 2].T, DH),
        "wproj": _ktiles(a["L0_attn_W_proj"], DH), "bproj": lanes(a["L0_attn_b_proj"]),
        "temp": np.repeat(a["L0_attn_temp"].reshape(HA), D // HA).reshape(2, DH).T,
        "offblock": np.where(heads[:, None] == heads[None, :], 0.0, NEG).astype(np.float32),
        "fc1": _ktiles(a["L0_ffn_fc1_w"].T, DH), "fc1_b": a["L0_ffn_fc1_b"].reshape(FT, 128).T,
        "fc2": _ktiles(a["L0_ffn_fc2_w"].T, 128), "fc2_b": lanes(a["L0_ffn_fc2_b"]),
        "wqkv": _ktiles(np.concatenate([a["L1_attn_Wq"], a["L1_attn_Wk"], a["L1_attn_Wv"]]).T, DH),
        "wug": _ktiles(np.concatenate([a["L1_attn_Wu"], gate[0], gate[1]]).T, DH),
        "wo": _ktiles(a["L1_attn_Wo"].T, DH),
        "mu": lanes(a["L1_attn_prior_mu"]), "logtau": lanes(a["L1_attn_prior_log_tau"]),
        "lnw": lanes(a["L1_ffn_ln_w"], 128), "lnwT": a["L1_ffn_ln_w"].reshape(2, DH).T,
        "router": _ktiles(a["L1_ffn_w_router"], DH),
        "ident": np.eye(128, dtype=np.float32), "tri": np.triu(np.ones((T, T), np.float32)),
        "ones": np.ones((128, 128), np.float32), "zeros": np.zeros((128, ROW), np.float32),
        "reset": lanes(reset), "cos": table(np.cos, 1.0), "sin": table(np.sin, sign),
        "pos": chunk[None, :] * T + tok[:, None] + 1, "iotae": lanes(np.arange(E, dtype=np.float32)),
        "iota128": lanes(np.arange(128, dtype=np.float32)),
        "tokid": np.arange(B * NC, dtype=np.float32)[None, :] * T + tok[:, None] + 1,
        "poff": lanes(CAP * (np.arange(B) % 2) - 1.0), "eps": eps,
        "gate": a["L0_ffn_gate_pair"].reshape(NCLS, 2 * D), "bal": a["L0_ffn_balance_bias"], "out_b": out_b,
        "in_b": np.transpose(a["L0_ffn_atom_in_b"].reshape(NAT, FT, 128), (2, 0, 1)).reshape(128, -1),
        "atom_in": _ktiles(a["L0_ffn_atom_in_w"].reshape(NAT * F, D).T, DH),
        "atom_out": np.transpose(a["L0_ffn_atom_out_w"].reshape(NAT, D, FT, 128), (3, 0, 2, 1)).reshape(128, -1),
    }
    where, total = pack_columns()
    packed = np.zeros((128, total), np.float32)
    for name, (p, at, n) in where.items():
        assert parts[name].shape == (p, n), (name, parts[name].shape)
        packed[:p, at:at + n] = parts[name]
    return packed


def arrays(inputs):
    a = {k: np.asarray(v) for k, v in inputs.items()}
    wi, wo_e = a["L1_ffn_wi"], a["L1_ffn_wo"]
    return {
        "xin": _planes(a["x"]), "packed": _packed(a),
        "wi": np.ascontiguousarray(np.transpose(wi.reshape(E, 2, DH, F), (0, 2, 1, 3)).reshape(E, DH, 2 * F)),
        "wo_e": np.ascontiguousarray(np.transpose(wo_e.reshape(E, FT, 128, D), (0, 2, 1, 3)).reshape(E, 128, FT * D)),
    }


def kernel(**inputs):
    import concourse.bacc as bacc
    from concourse.bass_utils import run_bass_kernel_spmd

    nc = bacc.Bacc("TRN2", target_bir_lowering=False, num_devices=1)
    data = arrays(inputs)
    args = [nc.dram_tensor(n, data[n].shape, F32, kind="ExternalInput").ap() for n in ("xin", "packed")]
    out = nc.dram_tensor("out", (B * L, D), F32, kind="ExternalOutput").ap()
    rows = nc.dram_tensor("rows", (B * L + 1, ROW), F32).ap()
    weights = [nc.dram_tensor(n, data[n].shape, F32, kind="ExternalInput").ap() for n in ("wi", "wo_e")]
    build_tower(nc, *args, out, rows, *weights)
    r = run_bass_kernel_spmd(nc, [data], core_ids=[0])
    return r.results[0]["out"].reshape(B, L, D)
```

```python
from contextlib import ExitStack

import numpy as np

import concourse.bass as bass
from concourse import mybir

ALU = mybir.AluOpType
ACT = mybir.ActivationFunctionType
AX = mybir.AxisListType
F32 = mybir.dt.float32
U32 = mybir.dt.uint32

B, CIN, IMG = 8, 64, 112
D = 192
DH = D // 2
OUTW = IMG // 2
T = 2 * OUTW
L = OUTW * OUTW
NC = L // T
NQ = NC // 4
SLAB = 5
HA = 8
F = 768
FT = F // 128
HL, HD = 12, 16
HP = 32
NCLS, NAT = 6, 5
E, CAP = 16, 64
RN, SD, MEAN, PROB = D, D + 1, D + 2, D + 3
ROW = D + 4
TPASS = 5
FAR = float(1 << 20)
NEG = -1.0e30
STAGE_COLUMNS = 11520
MIX_COLUMNS = 2692
GROUPS = {
    "attend": "att o3 vs osum v3 qT kT qd",
    "mixing": "gram gk prodk prodq t1sb mix att0 norm0",
    "hidden": "hid",
    "class": "cpre chid cprod xc cbias cres",
    "others": "gates ug usum uprod lg onehot prio rtmp cum pick xo ob xg lgT",
}


def pack_plan():
    return [
        ("conv01", 128, 3 * D), ("conv2", 64, 3 * D), ("tok_b", T, D),
        ("wq0", DH, 2 * D), ("wk0", DH, 2 * D), ("wvT", DH, 2 * D), ("wproj", DH, 2 * D), ("bproj", T, D),
        ("temp", DH, 2), ("offblock", DH, DH),
        ("fc1", DH, 2 * F), ("fc1_b", 128, FT), ("fc2", 128, FT * D), ("fc2_b", T, D),
        ("wqkv", DH, 2 * 3 * D), ("wug", DH, 2 * (D + 2 * HL)), ("wo", DH, 2 * D),
        ("mu", T, D), ("logtau", T, HL), ("lnw", 128, D), ("lnwT", DH, 2), ("router", DH, 2 * E),
        ("ident", 128, 128), ("tri", T, T), ("ones", 128, 128), ("zeros", 128, ROW),
        ("reset", T, E * NC), ("cos", T, NC * HD // 2), ("sin", T, NC * HD // 2), ("pos", T, NC),
        ("iotae", T, E), ("iota128", T, 128), ("tokid", T, B * NC), ("poff", T, B), ("eps", 128, 2),
        ("gate", NCLS, 2 * D), ("bal", NCLS, 2), ("out_b", NCLS, 2 * D), ("in_b", 128, NAT * FT),
        ("atom_in", DH, 2 * NAT * F), ("atom_out", 128, NAT * FT * D),
    ]


def pack_columns():
    at, where = 0, {}
    for name, p, n in pack_plan():
        where[name] = (p, at, n)
        at += n
    return where, at


class Steps:

    def __init__(self, sem, names):
        self.sem, self.names, self.at = sem, names.split(), 0

    def mark(self, instruction, name):
        assert self.names[self.at % len(self.names)] == name, (name, self.names, self.at)
        instruction.then_inc(self.sem, 1)
        self.at += 1

    def value(self, done, name):
        return done * len(self.names) + self.names.index(name) + 1


def build_tower(nc, xin, packed, out, rows, wi, wo_e, nb=B):
    where, total = pack_columns()
    ctx = ExitStack()
    with ctx:
        def sb(name, shape, dt=F32):
            return ctx.enter_context(nc.sbuf_tensor(name, shape, dt))

        def sem(name):
            return ctx.enter_context(nc.semaphore(name))

        W = sb("W", [128, total])
        PS = ctx.enter_context(nc.psum_tensor("PS", [128, 8, 512], F32))

        def w(name):
            p, at, n = where[name]
            return W[0:p, at:at + n]

        def bank(k, p, n):
            return PS[0:p, k, 0:n]

        def spread(ap, axis, n):
            ap = ap.unsqueeze(axis)
            shape = list(ap.shape)
            shape[axis] = n
            return ap.broadcast_to(shape)

        conv01 = w("conv01").rearrange("p (k n) -> p k n", k=3)
        conv2 = w("conv2").rearrange("p (k n) -> p k n", k=3)
        halves = {n: w(n).rearrange("p (k n) -> p k n", k=2)
                  for n in ("wq0", "wk0", "wvT", "wproj", "fc1", "wqkv", "wug", "wo", "router", "atom_in")}
        fc2 = w("fc2").rearrange("p (k n) -> p k n", k=FT)
        atom_out = w("atom_out").rearrange("p (a k n) -> p a k n", a=NAT, k=FT)
        ident, tri, ones, zeros = w("ident"), w("tri"), w("ones"), w("zeros")
        cos = w("cos").rearrange("p (c d) -> p c d", d=HD // 2)
        sin = w("sin").rearrange("p (c d) -> p c d", d=HD // 2)
        eps_ln, eps_rms = w("eps")[:, 0:1], w("eps")[:, 1:2]

        U = sb("U", [128, STAGE_COLUMNS])
        top = {}

        def stage(name, shape):
            n = int(np.prod(shape[1:]))
            group = next(g for g, names in GROUPS.items() if name in names.split())
            at = top.setdefault(group, MIX_COLUMNS if group in ("others", "class") else 0)
            top[group] = at + n
            assert top[group] <= STAGE_COLUMNS, name
            flat = U[0:shape[0], at:at + n]
            letters = "abcd"[:len(shape) - 1]
            return flat.rearrange(f"p ({' '.join(letters)}) -> p {' '.join(letters)}",
                                  **dict(zip(letters, shape[1:])))

        h = sb("h", [T, NC, ROW])
        hx = h[:, :, 0:D]
        xs = sb("xs", [128, 2, 3, SLAB * OUTW])
        xg = stage("xg", [T, 4, D])
        xh = sb("xh", [T, 4, D])
        xT = sb("xT", [DH, 2, 4, T])
        bns = sb("bns", [T, 4, 6])
        bnv = sb("bnv", [T, 4, 2])
        mv = [sb(f"mv{n}", [T, NC, 2]) for n in range(4)]
        rs = [sb(f"rs{n}", [T, NC]) for n in range(4)]
        gram = stage("gram", [DH, 2, D])
        gk = stage("gk", [DH, 2, D])
        prodk = stage("prodk", [DH, 2, D])
        prodq = stage("prodq", [DH, 2, D])
        norm0 = stage("norm0", [DH, D + 2])
        att0 = stage("att0", [DH, 2, DH])
        rowm = sb("rowm", [DH, 2])
        rsum = sb("rsum", [DH, 2])
        t1sb = stage("t1sb", [DH, 2, D])
        mix = stage("mix", [DH, 2, D])
        hid = stage("hid", [128, FT, 4, T])

        gate = w("gate").rearrange("p (r n) -> p r n", r=2)
        gss = sb("gss", [NCLS, 2])
        xc = stage("xc", [NCLS, D])
        xcT = sb("xcT", [DH, 2, NCLS])
        cprod = stage("cprod", [NCLS, 3, D])
        csum = sb("csum", [NCLS, 3])
        clog = sb("clog", [NCLS, 2])
        cext = sb("cext", [NCLS, 2])
        cflag = sb("cflag", [NCLS, 2])
        cdiag = sb("cdiag", [NCLS, 2, NCLS])
        cflagb = sb("cflagb", [128, 2 * NCLS])
        cpre = stage("cpre", [128, NAT * FT, NCLS])
        chid = stage("chid", [128, NAT, FT, NCLS])
        csel = sb("csel", [128, NAT, FT, NCLS])
        cbias = stage("cbias", [NCLS, D])
        cres = stage("cres", [NCLS, D])

        GU = D + 2 * HL
        ug = stage("ug", [T, 4, GU])
        usum = stage("usum", [T, 4, D])
        uprod = stage("uprod", [T, 4, D])
        sraw = sb("sraw", [T, 4, HL])
        scoef = sb("scoef", [T, NC, HL])
        taumu = w("mu")
        tau = sb("tau", [T, HL])
        invt = sb("invt", [T, NC])
        gates = stage("gates", [T, NC, 2 * HL])
        es = sb("es", [T, 2 * HL, NC])
        cum = stage("cum", [T, 2 * HL, NC])
        smax = sb("smax", [T, HL])
        smaxT = sb("smaxT", [HL, 1])
        sdiag = sb("sdiag", [HL, HL])
        coef = sb("coef", [T, 3, HL, NC])
        qk = sb("qk", [T, 4, 2 * HL, HP])
        nrm = sb("nrm", [T, 4, 2 * HL])
        cq = sb("cq", [T, 4, HL, 3])
        ck = sb("ck", [T, 4, HL, 3])
        att = stage("att", [T, 2, 3, 4, T])
        rope1 = U[0:T, 0:4 * 2 * D].rearrange("p (c h d) -> p c h d", c=4, h=2 * HL)
        o3_at = top["attend"]
        o3 = stage("o3", [T, 4, HL, 3, HD])
        rope2 = U[0:T, o3_at:o3_at + 4 * 2 * D].rearrange("p (c h d) -> p c h d", c=4, h=2 * HL)
        vs = stage("vs", [T, 4, D])
        osum = stage("osum", [T, 4, D])
        v3 = stage("v3", [T, 4, HL, 3, HD])
        qT = stage("qT", [128, 3, 3, T])
        kT = stage("kT", [128, 3, T])
        qd = stage("qd", [128, 3, 4, T])
        state = sb("state", [128, 2, 3, 4, 3 * HD])
        ost = sb("ost", [T, 4, HL])
        oT = xT
        osq = U[0:T, o3_at + 3 * HL * 3 * HD:o3_at + 3 * HL * 3 * HD + 2 * D].rearrange("p (c n) -> p c n", c=2)

        lg = stage("lg", [T, E, NC])
        onehot = stage("onehot", [T, E, NC])
        prio = stage("prio", [T, E, NC])
        rtmp = stage("rtmp", [T, E, NC])
        rmax = sb("rmax", [T, NC])
        prob = sb("prob", [T, NC])
        prs = sb("prs", [T, NC])
        rn = sb("rn", [T, NC])
        posx = sb("posx", [T, NC])
        pick = stage("pick", [T, 4, 128])
        slots = sb("slots", [128, B // 2, E])
        lgT = stage("lgT", [E, 4 * T])
        xo = stage("xo", [T, 4, D])
        hs = xh
        ob = stage("ob", [T, 4, D])

        at_in, at_out = where["atom_in"][1], where["atom_out"][1]
        w1 = [W[0:DH, at_in + s * 2 * F:at_in + (s + 1) * 2 * F].rearrange("p (k n) -> p k n", k=2) for s in range(2)]
        w2 = [W[:, at_out + s * FT * D:at_out + (s + 1) * FT * D].rearrange("p (k n) -> p k n", k=FT) for s in range(2)]
        mh = W[:, at_out + 2 * FT * D:at_out + 2 * FT * D + FT * 512].rearrange("p (k n) -> p k n", k=FT)
        mrow_at = at_in + 4 * F
        mrow = [W[:, mrow_at + s * 4 * ROW:mrow_at + (s + 1) * 4 * ROW].rearrange("p (k n) -> p k n", k=4)
                for s in range(2)]
        mT_at = mrow_at + 8 * ROW
        mT = W[0:DH, mT_at:mT_at + 2 * 512].rearrange("p (k n) -> p k n", k=2)
        mx = W[:, mT_at + 2 * 512:mT_at + 2 * 512 + 4 * D].rearrange("p (k n) -> p k n", k=4)
        assert mT_at + 2 * 512 + 4 * D <= at_in + 2 * NAT * F and FT * (2 * D + 512) <= NAT * FT * D
        my = [U[:, s * 4 * D:(s + 1) * 4 * D].rearrange("p (k n) -> p k n", k=4) for s in range(2)]
        gidx = sb("gidx", [128, E + 2, B // 2], U32)
        sidx = sb("sidx", [128, E, B // 2], U32)
        gi = [sb(f"gi{s}", [128, B // 2], U32) for s in range(2)]
        si = [sb(f"si{s}", [128, B // 2], U32) for s in range(2)]
        empty = sb("empty", [128, B // 2, E])

        S = {n: sem(n) for n in (
            "held packed_in atoms_in x_in0 x_in1 leads_given image_done "
            "conv_done conv_out xg_ready gram_read xh_ready turned xt_ready mix_done bias_in att_rsum h1_ready "
            "fc1_done gelu_done patches_done h2_ready ug_done ug_out gates_kept before_kept us_done uprod_done s_kept "
            "qk_done v_done rope_done qk_ready v_out squared rn_ready c_ready v3_ready qkt_done kq_out qt_out qd_zero "
            "s_done s_out st_done st_out o_done o_out osum_ready ctr_ready osq_out ovar osd_out oln_ready "
            "ot_done ot_out wo_done h3_ready lt_done lt_out lg_done lg_out pick_ready slots_done xs_ready xo_ready res_ready out_written "
            "rows_written x_kept gathered0 gathered1 w1_in0 w1_in1 w2_in0 w2_in1 index_ready gi_ready si_ready scattered0 scattered1 "
            "moe_x moe_h moe_turned moe_xt moe_f moe_ra moe_rd moe_o moe_y").split()}
        dA = Steps(sem("vector_conv"), "stat agg keep rstd")
        aA = Steps(sem("scalar_conv"), "sd")
        dB = Steps(sem("vector_mix"), "g0 g1 g2 gk pk pq rnorm rqt l0 l1 l2 rowm rsum att t1 mix")
        pB = Steps(sem("tensor_mix"), "mirror gw qk t1 mix")
        aB = Steps(sem("scalar_mix"), "norm exp")
        dC = Steps(sem("vector_stats2"), "stat agg keep")
        dR2 = Steps(sem("vector_rstd2"), "rstd0 rstd")
        aR2 = Steps(sem("scalar_sd2"), "sd0 sd")
        dE = Steps(sem("vector_class"), "h xc prod sq sum nmax nrec log max min diff flag0 flag1 p1 p "
                                        "diag0 diag1 pre flags sel bias0 bias res0 res")
        aE = Steps(sem("scalar_class"), "xcT norm exp gelu")
        pE = Steps(sem("tensor_class"), "turned hidden flags out")
        dD = Steps(sem("vector_stats3"), "stat agg keep")
        dR3 = Steps(sem("vector_rstd3"), "class stat agg rstd0 rstd")
        aR3 = Steps(sem("scalar_sd3"), "sd0 sd")
        dG = Steps(sem("vector_sums"), "max maxT diag shift scan0 scan1 excl sum eps einv al be0 be ga0 ga1 ga")
        pG = Steps(sem("tensor_sums"), "maxT max sums")
        aG = Steps(sem("scalar_sums"), "exp gates state0")
        dH = Steps(sem("vector_squares"), "ss0 ss1")
        dN = Steps(sem("vector_norms"), "nmax0 nrec0 nmax1 nrec1")
        dL = Steps(sem("vector_head_norm"), "sum0 mean0 rec0 sum1 mean1 rec1")
        dT = Steps(sem("vector_stats4"), "stat agg keep")
        lF = Steps(sem("pool_running"), "zero")
        lK = Steps(sem("pool_weights"), "k00 k10 k20 k01 k11 k21 q0 q1 q2")
        lA = Steps(sem("pool_sums"), "a0 a1")
        dI = Steps(sem("vector_rms"), "one_sd0 rstd0 one_sd mean rstd sq ms rn keep")
        aI = Steps(sem("scalar_rms"), "sd0 sd rms")
        dR = Steps(sem("vector_route"), "scale max shift eq first lowest onehot psum prob prs keepp scan excl prio "
                                        "under keep pz pos posx")
        aR = Steps(sem("scalar_route"), "exp")
        pR = Steps(sem("tensor_route"), "sums")
        dS = Steps(sem("vector_setup"), "pad state sel slots gsq gss nmax nrec gate router tau taumu s0 s1 s2 invt")
        aS = Steps(sem("scalar_setup"), "gnorm tau")
        dM = Steps(sem("vector_indices"), "zero empty gather minus1")

        block = ctx.enter_context(nc.Block())
        LEADS = 5

        def ch(t, i, c, n=1):
            return t[:, bass.ds(4 * i + c, n)]

        def one(ap):
            return ap.rearrange("p a n -> p (a n)")

        def pipelined(eng, lead_in, body, lead_out):
            lead_in()
            with eng.Fori(0, NQ - 1) as i:
                body(i)
            lead_out(NQ - 1)

        def hold(eng):
            eng.sem_inc(S["held"], 1)

        def give_leads(eng, **leads):
            for name, n in leads.items():
                eng.sem_inc(S[name], n)
            eng.sem_inc(S["leads_given"], 1)
            eng.wait_ge(S["leads_given"], LEADS)

        @block.sync
        def _(sp):
            atoms = where["atom_in"][1]
            sp.dma_start(W[:, 0:atoms], packed[:, 0:atoms]).then_inc(S["packed_in"], 16)
            give_leads(sp)
            sp.wait_ge(S["packed_in"], 16)
            sp.dma_start(rows[0:1, :], zeros[0:1, :]).then_inc(S["rows_written"], 16)

            def load(b, i):
                g = b * NQ + i
                for p in range(2):
                    sp.wait_ge(S["conv_done"], 2 * g + p + 1)
                    sp.dma_start(xs[:, p, :, :],
                                 xin[bass.ds(b, 1), :, :, bass.ds((8 * i + 4 * p) * OUTW, SLAB * OUTW)]
                                 .rearrange("b p v r -> p (b v) r")).then_inc(S[f"x_in{p}"], 16)

            def keep_rows(b, i):
                token = b * L + i * (4 * T)
                sp.wait_ge(S["rows_written"], 16 * (b * NQ + i) + 16)
                hold(sp)
                sp.dma_start(rows[bass.ds(token + 1, 4 * T), :].rearrange("(c p) n -> p c n", p=T),
                             ch(h, i, 0, 4)).then_inc(S["rows_written"], 16)

            def store(b, i):
                token = b * L + i * (4 * T)
                sp.wait_ge(S["res_ready"], 2 * (b * NQ + i) + 4)
                sp.dma_start(out[bass.ds(token, 4 * T), :].rearrange("(c p) n -> p c n", p=T),
                             ob[:, :, :]).then_inc(S["out_written"], 16)

            load(0, 0)
            sp.dma_start(W[:, atoms:total], packed[:, atoms:total]).then_inc(S["atoms_in"], 16)
            with sp.Fori(1, NQ) as i:
                load(0, i)
            with sp.Fori(1, nb) as b:
                load(b, 0)
                sp.wait_ge(dR.sem, dR.value(b - 1, "keepp"))
                hold(sp)
                sp.wait_ge(S["x_kept"], NQ * b + 1)
                hold(sp)
                keep_rows(b - 1, 0)
                load(b, 1)
                store(b - 1, 0)
                with sp.Fori(1, NQ - 1) as i:
                    keep_rows(b - 1, i)
                    store(b - 1, i)
                    load(b, i + 1)
                keep_rows(b - 1, NQ - 1)
                store(b - 1, NQ - 1)
            sp.wait_ge(dR.sem, dR.value(nb - 1, "keepp"))
            sp.wait_ge(S["x_kept"], NQ * nb + 1)
            with sp.Fori(0, NQ) as i:
                keep_rows(nb - 1, i)
                store(nb - 1, i)
            sp.wait_ge(S["image_done"], nb + 1)
            with sp.Fori(0, E // 2) as k2:
                for s in range(2):
                    e = 2 * k2 + s
                    sp.wait_ge(S["moe_o"], 2 * e + 1)
                    sp.dma_start(w1[s], wi[bass.ds(e, 1)].rearrange("a p (k n) -> p (a k) n", k=2))\
                        .then_inc(S[f"w1_in{s}"], 16)
                    sp.dma_start(w2[s], wo_e[bass.ds(e, 1)].rearrange("a p (k n) -> p (a k) n", k=FT))\
                        .then_inc(S[f"w2_in{s}"], 16)

        @block.tensor
        def _(pe):
            mm, tr = nc.tensor.matmul, nc.tensor.transpose
            pe.wait_ge(S["packed_in"], 16)
            give_leads(pe, conv_done=2, gram_read=1, turned=2, mix_done=2, st_done=4, us_done=4,
                       moe_turned=1, moe_f=6, moe_o=3)

            def turn(q, p, first=0):
                pe.wait_ge(S["xt_ready"], 2 * q + p + 1)
                pe.wait_ge(S["xh_ready"], 2 * q + p + 1)
                for j in range(2):
                    for k in range(2):
                        t = tr(PS[0:DH, first + p, (2 * k + j) * T:(2 * k + j + 1) * T],
                               xh[:, 2 * p + j, k * DH:(k + 1) * DH], ident[0:T, 0:T])
                t.then_inc(S["turned"], 1)

            def tile_pair(p, bk, x, weight, n, at=0):
                for j in range(2):
                    for k in range(2):
                        m = mm(PS[0:T, bk, j * n:(j + 1) * n], x[:, k, 2 * p + j, :], weight[:, k, at:at + n],
                               start=k == 0, stop=k == 1)
                return m

            def zero(bk, p, n):
                mm(bank(bk, p, n), zeros[0:T, 0:p], zeros[0:T, 0:n], start=True, stop=False, skip_group_check=True)

            def slots_open(b):
                pe.wait_ge(dR.sem, dR.value(b, "posx"))
                zero(3, 128, E)

            def fill(b, i):
                for c in range(4):
                    pe.wait_ge(S["pick_ready"], 4 * (b * NQ + i) + c + 1)
                    mm(bank(3, 128, E), pick[:, c, :], one(onehot[:, :, bass.ds(4 * i + c, 1)].rearrange("p e c -> p c e")),
                       start=False, stop=False, skip_group_check=True).then_inc(S["slots_done"], 1)

            def conv(b, i, p):
                g = b * NQ + i
                pe.wait_ge(S["conv_out"], 2 * g + p + 1)
                pe.wait_ge(S[f"x_in{p}"], 16 * g + 16)
                for j in range(2):
                    o = PS[0:T, 6 + p, j * D:(j + 1) * D]
                    for kx in range(3):
                        mm(o, xs[:, p, kx, 2 * j * OUTW:(2 * j + 2) * OUTW], conv01[:, kx, :],
                           start=kx == 0, stop=False)
                    for kx in range(3):
                        m = mm(o, xs[0:CIN, p, kx, (2 * j + 1) * OUTW:(2 * j + 3) * OUTW], conv2[:, kx, :],
                               start=False, stop=kx == 2)
                m.then_inc(S["conv_done"], 1)

            def conv_stage(b, after=None):
                zero(4, DH, D)
                zero(5, DH, DH)

                def gram_of(i):
                    pe.wait_ge(S["xg_ready"], b * NQ + i + 1)
                    for c in range(4):
                        x = xg[:, c, :]
                        mm(bank(4, DH, D), x[:, 0:DH], x, start=False, stop=False, skip_group_check=True)
                        m = mm(bank(5, DH, DH), x[:, DH:D], x[:, DH:D], start=False, stop=False, skip_group_check=True)
                    m.then_inc(S["gram_read"], 1)

                def conv_next(i):
                    if after is not None:
                        fill(after, i)
                    for p in range(2):
                        conv(b, i + 1, p)
                    gram_of(i)

                def conv_last(i):
                    if after is not None:
                        fill(after, i)
                    gram_of(i)

                pipelined(pe, lambda: slots_open(after) if after is not None else None, conv_next, conv_last)

            def image(b, more):
                pe.wait_ge(S["image_done"], b + 1)
                pe.wait_ge(dB.sem, dB.value(b, "g1"))
                pB.mark(tr(bank(2, DH, DH), gram[:, 0, DH:D], ident[0:DH, 0:DH]), "mirror")
                pe.wait_ge(dB.sem, dB.value(b, "g2"))
                for bk, name in ((4, "wk0"), (5, "wq0")):
                    for n in range(2):
                        for k in range(2):
                            m = mm(PS[0:DH, bk, n * D:(n + 1) * D], gram[:, k, n * DH:(n + 1) * DH],
                                   halves[name][:, k, :], start=k == 0, stop=k == 1)
                pB.mark(m, "gw")
                pe.wait_ge(dB.sem, dB.value(b, "pq"))
                for n in range(2):
                    for k in range(2):
                        mm(PS[0:DH, 2, n * DH:(n + 1) * DH], halves["wq0"][:, k, n * DH:(n + 1) * DH],
                           gk[:, k, n * DH:(n + 1) * DH], start=k == 0, stop=k == 1)
                for k in range(2):
                    mm(bank(3, DH, D), ones[0:DH, 0:DH], prodk[:, k, :], start=k == 0, stop=k == 1)
                for n in range(2):
                    for k in range(2):
                        m = mm(PS[0:DH, 3, D + n:D + n + 1], prodq[:, k, n * DH:(n + 1) * DH], ones[0:DH, 0:1],
                               start=k == 0, stop=k == 1)
                pB.mark(m, "qk")
                pe.wait_ge(dB.sem, dB.value(b, "att"))
                for n in range(2):
                    m = mm(PS[0:DH, 2, n * D:(n + 1) * D], att0[:, n, :], halves["wproj"][:, n, :],
                           start=True, stop=True)
                pB.mark(m, "t1")
                pe.wait_ge(dB.sem, dB.value(b, "t1"))
                for n in range(2):
                    for k in range(2):
                        m = mm(PS[0:DH, 3, n * D:(n + 1) * D], halves["wvT"][:, k, n * DH:(n + 1) * DH],
                               t1sb[:, k, :], start=k == 0, stop=k == 1)
                pB.mark(m, "mix")
                pe.wait_ge(dB.sem, dB.value(b, "mix"))
                hold(pe)

                def stage_c(i, more):
                    q = b * (TPASS * NQ) + i
                    g = b * NQ + i
                    for p in range(2):
                        pe.wait_ge(S["xt_ready"], 2 * q + p + 3)
                        pe.wait_ge(S["h1_ready"], 2 * g + p + 1)
                        tile_pair(p, 6 + p, xT, mix, D).then_inc(S["mix_done"], 1)
                        if more:
                            turn(q + 1, p)

                pipelined(pe, lambda: [turn(b * (TPASS * NQ), p) for p in range(2)],
                          lambda i: stage_c(i, True), lambda i: stage_c(i, False))

                def class_turned():
                    pe.wait_ge(dE.sem, dE.value(b, "xc"))
                    pe.wait_ge(S["gelu_done"], FT * NQ * b + 4)
                    hold(pe)
                    for k in range(2):
                        m = tr(PS[0:DH, 5, k * NCLS:(k + 1) * NCLS], xc[:, k * DH:(k + 1) * DH],
                               ident[0:NCLS, 0:NCLS])
                    pE.mark(m, "turned")

                def class_hidden():
                    pe.wait_ge(aE.sem, aE.value(b, "xcT"))
                    pe.wait_ge(S["atoms_in"], 16)
                    for a in range(NAT * FT):
                        for k in range(2):
                            m = mm(PS[:, 4, a * NCLS:(a + 1) * NCLS], halves["atom_in"][:, k, a * 128:(a + 1) * 128],
                                   xcT[:, k, :], start=k == 0, stop=k == 1)
                    pE.mark(m, "hidden")

                def class_flags():
                    pe.wait_ge(dE.sem, dE.value(b, "diag1"))
                    pe.wait_ge(S["gelu_done"], FT * (NQ * b + 1) + 3)
                    pE.mark(mm(bank(4, 128, 2 * NCLS), ones[0:NCLS, :], cdiag[:, :, :].rearrange("p a n -> p (a n)"),
                               start=True, stop=True), "flags")

                def class_out():
                    pe.wait_ge(dE.sem, dE.value(b, "sel"))
                    for a in range(NAT):
                        for k in range(FT):
                            m = mm(bank(5, NCLS, D), csel[:, a, k, :], atom_out[:, a, k, :],
                                   start=a + k == 0, stop=(a == NAT - 1 and k == FT - 1))
                    pE.mark(m, "out")

                def fc1_of(i):
                    q = b * (TPASS * NQ) + NQ + i
                    g = b * NQ + i
                    pe.wait_ge(S["xt_ready"], 2 * q + 4)
                    for f in range(FT):
                        if f >= 4:
                            pe.wait_ge(S["gelu_done"], FT * g + f - 3)
                        for k in range(2):
                            m = mm(PS[:, 2 + f % 4, 0:4 * T], halves["fc1"][:, k, f * 128:(f + 1) * 128],
                                   xT[:, k, :, :].rearrange("p c t -> p (c t)"), start=k == 0, stop=k == 1)
                        m.then_inc(S["fc1_done"], 1)

                def turn_next(i):
                    for p in range(2):
                        turn(b * (TPASS * NQ) + NQ + i + 1, p)

                def fc2_of(i):
                    g = b * NQ + i
                    pe.wait_ge(S["gelu_done"], FT * g + FT)
                    for p in range(2):
                        pe.wait_ge(S["h2_ready"], 2 * g + p + 1)
                        if p == 0:
                            pe.wait_ge(S["h1_ready"], 2 * NQ * b + 2 * NQ + 2)
                        for j in range(2):
                            for k in range(FT):
                                m = mm(PS[0:T, 6 + p, j * D:(j + 1) * D], hid[:, k, 2 * p + j, :], fc2[:, k, :],
                                       start=k == 0, stop=k == FT - 1)
                        m.then_inc(S["patches_done"], 1)

                turn_next(-1)
                fc1_of(0)
                turn_next(0)
                class_turned()
                fc2_of(0)
                class_hidden()
                pe.wait_ge(dE.sem, dE.value(b, "pre"))
                fc1_of(1)
                turn_next(1)
                class_flags()
                fc2_of(1)
                pe.wait_ge(dE.sem, dE.value(b, "flags"))
                fc1_of(2)
                turn_next(2)
                fc2_of(2)
                class_out()
                pe.wait_ge(dE.sem, dE.value(b, "res"))
                hold(pe)
                with pe.Fori(3, NQ - 1) as i:
                    fc1_of(i)
                    turn_next(i)
                    fc2_of(i)
                fc1_of(NQ - 1)
                fc2_of(NQ - 1)

                def stage_f(i, more):
                    q = b * (TPASS * NQ) + 2 * NQ + i
                    g = b * NQ + i
                    for p in range(2):
                        pe.wait_ge(S["xt_ready"], 2 * q + p + 3)
                        pe.wait_ge(S["ug_out"], 2 * g + p + 1)
                        tile_pair(p, 2 + p, xT, halves["wug"], GU).then_inc(S["ug_done"], 1)
                        if more:
                            turn(q + 1, p)
                    pe.wait_ge(S["uprod_done"], g + 1)
                    for c in range(4):
                        pe.wait_ge(S["ug_out"], 2 * g + c // 2 + 3)
                        mm(bank(4 + c, T, D), tri, ug[:, c, 0:D], start=True, stop=False)
                        pe.wait_ge(S["before_kept"], b + 4 * g + c + 1)
                        mm(bank(4 + c, T, D), ones[0:T, 0:T], usum[:, c, :], start=False, stop=True)\
                            .then_inc(S["us_done"], 1)

                pipelined(pe, lambda: [turn(b * (TPASS * NQ) + 2 * NQ, p) for p in range(2)],
                          lambda i: stage_f(i, True), lambda i: stage_f(i, False))

                pe.wait_ge(dG.sem, dG.value(b, "max"))
                pG.mark(tr(bank(2, HL, T), smax[:, :], ident[0:T, 0:T]), "maxT")
                pe.wait_ge(dG.sem, dG.value(b, "diag"))
                pG.mark(mm(bank(3, T, HL), ones[0:HL, 0:T], sdiag[:, :], start=True, stop=True), "max")
                pe.wait_ge(aG.sem, aG.value(b, "exp"))
                for k in range(2):
                    part = es[:, k * HL:(k + 1) * HL, :].rearrange("p h c -> p (h c)")
                    mm(bank(4 + k, T, HL * NC), tri, part, start=True, stop=True)
                    m = mm(bank(6 + k, T, HL * NC), ones[0:T, 0:T], part, start=True, stop=True)
                pG.mark(m, "sums")

                pe.wait_ge(aG.sem, aG.value(b, "state0"))
                pe.wait_ge(dG.sem, dG.value(b, "ga"))
                mm(bank(7, 128, 9 * HD), zeros[0:T, 0:128], zeros[0:T, 0:9 * HD], start=True, stop=False,
                   skip_group_check=True)
                def head(i):
                    q = b * (TPASS * NQ) + 3 * NQ + i
                    g = b * NQ + i
                    for c in range(4):
                        pe.wait_ge(S["xt_ready"], 2 * q + c // 2 + 3)
                        if c == 0:
                            pe.wait_ge(S["xt_ready"], 2 * q + 4)
                        if c == 2:
                            pe.wait_ge(S["o_out"], 4 * g + 1)
                        for k in range(2):
                            m = mm(bank(2 + c, T, 2 * D), xT[:, k, c, :], halves["wqkv"][:, k, 0:2 * D],
                                   start=k == 0, stop=k == 1)
                        m.then_inc(S["qk_done"], 1)
                        for k in range(2):
                            m = mm(PS[0:T, (6, 0)[c // 2], (c % 2) * D:(c % 2 + 1) * D], xT[:, k, c, :],
                                   halves["wqkv"][:, k, 2 * D:3 * D], start=k == 0, stop=k == 1)
                        if c % 2 == 1:
                            m.then_inc(S["v_done"], 1)

                def turn_qk(i, c):
                    g = b * NQ + i
                    pe.wait_ge(S["qk_ready"], 4 * g + (5 if c == 0 else 8))
                    if c == 0:
                        pe.wait_ge(S["v_out"], 2 * g + 1)
                    else:
                        pe.wait_ge(S["qt_out"], 4 * g + c)
                    for n, bk in enumerate((1 if c == 0 else 5, 6)):
                        for k in range(3):
                            m = tr(PS[:, bk, k * T:(k + 1) * T],
                                   qk[:, c, n * HL + 4 * k:n * HL + 4 * k + 4, :].rearrange("p h d -> p (h d)"),
                                   ident[0:T, 0:T])
                    m.then_inc(S["qkt_done"], 1)

                def turn_outputs(i, last=False):
                    g = b * NQ + i
                    if not last:
                        pe.wait_ge(S["qk_ready"], 4 * g + 11)
                    for p in range(2):
                        pe.wait_ge(S["oln_ready"], 2 * g + p + 1)
                        for j in range(2):
                            for k in range(2):
                                m = tr(PS[0:DH, 3 + p, (2 * k + j) * T:(2 * k + j + 1) * T],
                                       osum[:, 2 * p + j, k * DH:(k + 1) * DH], ident[0:T, 0:T])
                        m.then_inc(S["ot_done"], 1)

                def project_outputs(i, p, last=False):
                    g = b * NQ + i
                    pe.wait_ge(S["ot_out"], 2 * g + p + 1)
                    if not last:
                        pe.wait_ge(*((S["v_out"], 2 * g + 4) if p == 0 else (S["qt_out"], 4 * g + 5)))
                    tile_pair(p, p, oT, halves["wo"], D).then_inc(S["wo_done"], 1)

                def scores(i, c):
                    g = b * NQ + i
                    pe.wait_ge(S["kq_out"], 4 * g + c + 1)
                    if c == 0:
                        pe.wait_ge(S["qk_ready"], 4 * g + 7)
                    for k in range(3):
                        if c:
                            pe.wait_ge(S["s_out"], 12 * g + 3 * (c - 1) + k + 1)
                        mm(bank(2 + k, T, 4 * T), kT[:, k, :], qd[:, k, :, :].rearrange("p j t -> p (j t)"),
                           start=True, stop=True).then_inc(S["s_done"], 1)

                def new_state(i, c):
                    g = b * NQ + i
                    pe.wait_ge(S["v3_ready"], 4 * g + c + 5)
                    pe.wait_ge(S["st_out"], 4 * g + c + 1)
                    for k in range(3):
                        for j in range(4):
                            m = mm(PS[32 * j:32 * j + 32, 7, k * 3 * HD:(k + 1) * 3 * HD],
                                   qk[:, c, HL + 4 * k + j, :],
                                   v3[:, c, 4 * k + j, :, :].rearrange("p j d -> p (j d)"),
                                   start=False, stop=False, skip_group_check=True)
                    m.then_inc(S["st_done"], 1)

                def outputs(i, c):
                    g = b * NQ + i
                    pe.wait_ge(S["o_out"], 4 * g + c + 1)
                    pe.wait_ge(S["s_out"], 12 * g + 3 * c + 3)
                    pe.wait_ge(S["qt_out"], 4 * g + c + 1)
                    if c == 0:
                        pe.wait_ge(S["h3_ready"], 2 * g + 2)
                    for k in range(3):
                        mm(PS[0:T, k // 2, (k % 2) * 12 * HD:(k % 2 + 1) * 12 * HD], qT[:, c % 3, k, :],
                           state[:, c % 2, k, :, :].rearrange("p j d -> p (j d)"),
                           start=True, stop=False, skip_group_check=True)
                        for n in range(4 * k, 4 * k + 4):
                            m = mm(PS[0:T, n // 8, (n % 8) * 3 * HD:(n % 8 + 1) * 3 * HD],
                                   att[:, c % 2, k, n % 4, :], v3[:, c, n, :, :].rearrange("p j d -> p (j d)"),
                                   start=False, stop=n % 4 == 3, skip_group_check=True)
                    m.then_inc(S["o_done"], 1)

                def turn_quad(i):
                    for p in range(2):
                        turn(b * (TPASS * NQ) + 3 * NQ + i, p, first=5)

                def stage_h(i, first=False, more=True):
                    head(i)
                    turn_qk(i, 0)
                    if not first:
                        turn_outputs(i - 1)
                        project_outputs(i - 1, 0)
                        pe.wait_ge(S["ot_out"], 2 * (b * NQ + i))
                    scores(i, 0)
                    turn_qk(i, 1)
                    if not first:
                        project_outputs(i - 1, 1)
                    new_state(i, 0)
                    for c in range(1, 4):
                        scores(i, c)
                        if c < 3:
                            turn_qk(i, c + 1)
                        outputs(i, c - 1)
                        new_state(i, c)
                    if more:
                        pe.wait_ge(S["qt_out"], 4 * (b * NQ + i) + 4)
                        turn_quad(i + 1)
                    outputs(i, 3)

                turn_quad(0)
                stage_h(0, first=True)
                with pe.Fori(1, NQ - 1) as i:
                    stage_h(i)
                stage_h(NQ - 1, more=False)
                turn_outputs(NQ - 1, last=True)
                for p in range(2):
                    project_outputs(NQ - 1, p, last=True)

                pe.wait_ge(S["h3_ready"], 2 * NQ * b + 2 * NQ + 2)

                def stage_i(i, more):
                    q = b * (TPASS * NQ) + 4 * NQ + i
                    g = b * NQ + i
                    pe.wait_ge(S["xt_ready"], 2 * q + 4)
                    for k in range(2):
                        m = mm(bank(7, E, 4 * T), halves["router"][:, k, :], xT[:, k, :, :].rearrange("p c t -> p (c t)"),
                               start=k == 0, stop=k == 1)
                    m.then_inc(S["lt_done"], 1)
                    if more:
                        for p in range(2):
                            turn(q + 1, p)
                    pe.wait_ge(S["lt_out"], g + 1)
                    pe.wait_ge(S["lg_out"], g + 1)
                    hold(pe)
                    for c in range(4):
                        m = tr(PS[0:T, 6, c * E:(c + 1) * E], lgT[:, c * T:(c + 1) * T], ident[0:E, 0:E])
                    m.then_inc(S["lg_done"], 1)

                pipelined(pe, lambda: [turn(b * (TPASS * NQ) + 4 * NQ, p) for p in range(2)],
                          lambda i: stage_i(i, True), lambda i: stage_i(i, False))

                if more:
                    pe.wait_ge(S["lg_out"], NQ * b + NQ + 1)
                    conv(b + 1, 0, 0)
                pe.wait_ge(dR.sem, dR.value(b, "onehot"))
                flat = onehot[:, :, :].rearrange("p e c -> p (e c)")
                mm(bank(2, T, E * NC), tri, flat, start=True, stop=True)
                pR.mark(mm(bank(3, T, E * NC), ones[0:T, 0:T], flat, start=True, stop=True), "sums")
                if more:
                    conv(b + 1, 0, 1)

            for p in range(2):
                conv(0, 0, p)
            conv_stage(0)
            with pe.Fori(0, nb - 1) as b:
                image(b, more=True)
                conv_stage(b + 1, after=b)
            image(nb - 1, more=False)
            slots_open(nb - 1)
            hold(pe)
            with pe.Fori(0, NQ) as i:
                fill(nb - 1, i)

            pe.wait_ge(S["image_done"], nb + 1)
            with pe.Fori(0, E // 2) as k2:
                for s in range(2):
                    e = 2 * k2 + s
                    pe.wait_ge(S["moe_xt"], e + 1)
                    pe.wait_ge(S["moe_x"], e + 1)
                    for n in range(4):
                        for k in range(2):
                            m = tr(PS[0:DH, n // 2, (2 * k + n % 2) * 128:(2 * k + n % 2 + 1) * 128],
                                   mx[:, n, k * DH:(k + 1) * DH], ident)
                    m.then_inc(S["moe_turned"], 1)
                    pe.wait_ge(S["moe_xt"], e + 2)
                    pe.wait_ge(S[f"w1_in{s}"], 16 * k2 + 16)
                    for f in range(FT):
                        if f == 4:
                            pe.wait_ge(S["moe_ra"], 3 * e + 1)
                        if f == 5:
                            pe.wait_ge(S["moe_rd"], 3 * e + 1)
                        for k in range(2):
                            m = mm(PS[:, 2 + f % 4, :], w1[s][:, k, f * 128:(f + 1) * 128], mT[:, k, :],
                                   start=k == 0, stop=k == 1)
                        m.then_inc(S["moe_f"], 1)
                    pe.wait_ge(S["moe_ra"], 3 * e + 3)
                    pe.wait_ge(S["moe_rd"], 3 * e + 3)
                    pe.wait_ge(S[f"w2_in{s}"], 16 * k2 + 16)
                    for p in range(2):
                        pe.wait_ge(S["moe_y"], 2 * e + p + 1)
                        for j in range(2):
                            for k in range(FT):
                                m = mm(PS[:, 6 + p, j * D:(j + 1) * D],
                                       mh[:, k, (2 * p + j) * 128:(2 * p + j + 1) * 128], w2[s][:, k, :],
                                       start=k == 0, stop=k == FT - 1)
                        m.then_inc(S["moe_o"], 1)

        @block.scalar
        def _(act):
            A = nc.scalar.activation
            act.wait_ge(S["packed_in"], 16)
            give_leads(act, xt_ready=2, ug_out=2, st_out=1, lg_out=1, x_kept=1, out_written=16, moe_xt=1)

            act.wait_ge(dS.sem, dS.value(0, "gss"))
            aS.mark(A(gss[:, :], gss[:, :], ACT.Sqrt), "gnorm")
            act.wait_ge(dS.sem, dS.value(0, "tau"))
            aS.mark(A(tau[:, :], tau[:, :], ACT.Exp), "tau")
            act.wait_ge(dS.sem, dS.value(0, "invt"))

            def xt_out(q, first=0):
                for p in range(2):
                    act.wait_ge(S["turned"], 2 * q + p + 3)
                    A(xT[:, :, 2 * p:2 * p + 2, :], bank(first + p, DH, 4 * T).rearrange("p (k c t) -> p k c t", k=2, c=2),
                      ACT.Copy).then_inc(S["xt_ready"], 1)

            def residual(b, i):
                for p in range(2):
                    act.wait_ge(S["res_ready"], 2 * (b * NQ + i) + p + 1)
                    for c in (2 * p, 2 * p + 1):
                        row = one(ch(h, i, c))
                        m = A(hs[:, c, :], row[:, 0:D], ACT.Identity, scale=row[:, SD:SD + 1],
                              bias=row[:, MEAN:MEAN + 1])
                    m.then_inc(S["xs_ready"], 1)

            def conv_stage(b, after=None):
                def deviation(i):
                    act.wait_ge(dA.sem, dA.value(b * NQ + i, "agg"))
                    aA.mark(A(ch(rs[0], i, 0, 4), bnv[:, :, 1], ACT.Sqrt, bias=eps_ln[0:T]), "sd")

                def body(i):
                    if after is not None:
                        residual(after, i + 1)
                    deviation(i)

                pipelined(act, lambda: residual(after, 0) if after is not None else None, body, deviation)

            def image(b):
                act.wait_ge(pB.sem, pB.value(b, "qk"))
                aB.mark(A(norm0[:, :], bank(3, DH, D + 2), ACT.Sqrt), "norm")
                act.wait_ge(dB.sem, dB.value(b, "rowm"))
                for n in range(2):
                    m = A(att0[:, n, :], att0[:, n, :], ACT.Exp, bias=rowm[:, n:n + 1])
                aB.mark(m, "exp")
                with act.Fori(0, NQ) as i:
                    xt_out(b * (TPASS * NQ) + i)
                def deviations(n, steps, chunks, name):
                    steps.mark(A(rs[n][:, chunks], mv[n][:, chunks, 1], ACT.Sqrt, bias=eps_ln[0:T]), name)

                act.wait_ge(dC.sem, dC.value(b * NQ, "keep"))
                deviations(1, aR2, slice(0, 4), "sd0")
                xt_out(b * (TPASS * NQ) + NQ)
                act.wait_ge(dC.sem, dC.value(b * NQ + NQ - 1, "keep"))
                deviations(1, aR2, slice(4, NC), "sd")

                def gelus(i):
                    g = b * NQ + i
                    act.wait_ge(S["patches_done"], 2 * g + 2)
                    for f in range(FT):
                        act.wait_ge(S["fc1_done"], FT * g + f + 1)
                        A(hid[:, f, :, :].rearrange("p c t -> p (c t)"), PS[:, 2 + f % 4, 0:4 * T], ACT.Gelu,
                          bias=w("fc1_b")[:, f:f + 1]).then_inc(S["gelu_done"], 1)

                def turned_next(i):
                    xt_out(b * (TPASS * NQ) + NQ + i + 1)

                gelus(0)
                turned_next(0)
                act.wait_ge(pE.sem, pE.value(b, "turned"))
                aE.mark(A(xcT[:, :, :], bank(5, DH, 2 * NCLS).rearrange("p (k n) -> p k n", k=2), ACT.Copy), "xcT")
                act.wait_ge(dE.sem, dE.value(b, "sum"))
                aE.mark(A(csum[:, 2:3], csum[:, 2:3], ACT.Sqrt), "norm")
                act.wait_ge(dE.sem, dE.value(b, "diff"))
                aE.mark(A(cext[:, 1:2], cext[:, 1:2], ACT.Exp), "exp")
                gelus(1)
                turned_next(1)
                act.wait_ge(dE.sem, dE.value(b, "pre"))
                aE.mark(A(chid[:, :, :, :].rearrange("p a k n -> p (a k n)"),
                          cpre[:, :, :].rearrange("p a n -> p (a n)"), ACT.Gelu), "gelu")
                with act.Fori(2, NQ - 1) as i:
                    gelus(i)
                    turned_next(i)
                gelus(NQ - 1)
                act.wait_ge(dR3.sem, dR3.value(b, "agg"))
                deviations(2, aR3, slice(0, 4), "sd0")
                xt_out(b * (TPASS * NQ) + 2 * NQ)
                act.wait_ge(dD.sem, dD.value(b * NQ + NQ - 1, "keep"))
                deviations(2, aR3, slice(4, NC), "sd")
                def ug_to_sbuf(i, more):
                    g = b * NQ + i
                    act.wait_ge(S["uprod_done"], g + 1)
                    act.wait_ge(S["gates_kept"], g + 1)
                    act.wait_ge(S["us_done"], 4 * g + 4)
                    for p in range(2):
                        act.wait_ge(S["ug_done"], 2 * g + p + 1)
                        A(ug[:, 2 * p:2 * p + 2, :], bank(2 + p, T, 2 * GU).rearrange("p (c n) -> p c n", c=2),
                          ACT.Copy).then_inc(S["ug_out"], 1)
                    if more:
                        xt_out(b * (TPASS * NQ) + 2 * NQ + i + 1)

                pipelined(act, lambda: hold(act),
                          lambda i: ug_to_sbuf(i, True), lambda i: ug_to_sbuf(i, False))
                act.wait_ge(dG.sem, dG.value(b, "shift"))
                aG.mark(A(es[:, 0:HL, :], es[:, 0:HL, :], ACT.Exp), "exp")
                act.wait_ge(S["gates_kept"], NQ * b + NQ + 1)
                aG.mark(A(gates[:, :, :], gates[:, :, :], ACT.Sigmoid), "gates")
                aG.mark(A(state[:, 0, :, :, :], spread(zeros[:, 0:9 * HD].rearrange("p (k d) -> p k d", k=3), 2, 4),
                          ACT.Copy),
                        "state0")
                def v_out(i, p):
                    g = b * NQ + i
                    act.wait_ge(S["v3_ready"], 4 * g + 4)
                    act.wait_ge(S["v_done"], 2 * g + p + 1)
                    A(vs[:, 2 * p:2 * p + 2, :], bank((6, 0)[p], T, 2 * D).rearrange("p (c n) -> p c n", c=2),
                      ACT.Copy).then_inc(S["v_out"], 1)

                def square(i, c):
                    g = b * NQ + i
                    act.wait_ge(S["qk_ready"], 4 * g + c + 5)
                    A(rope1[:, c, :, :], qk[:, c, :, 0:HD], ACT.Square).then_inc(S["squared"], 1)

                def roots(i, p):
                    act.wait_ge(dH.sem, dH.value(b * NQ + i, f"ss{p}"))
                    A(nrm[:, 2 * p:2 * p + 2, :], nrm[:, 2 * p:2 * p + 2, :], ACT.Sqrt).then_inc(S["rn_ready"], 1)

                def qk_to_sbuf(i, c):
                    g = b * NQ + i
                    act.wait_ge(S["qkt_done"], 4 * g + c + 1)
                    if c == 0:
                        act.wait_ge(S["qd_zero"], b + 1)
                    else:
                        act.wait_ge(S["s_done"], 12 * g + 3 * c)
                    q, k = (bank(n, 128, 3 * T).rearrange("p (k t) -> p k t", k=3) for n in (1 if c == 0 else 5, 6))
                    A(kT[:, :, :], k, ACT.Copy)
                    for j in range(4):
                        lanes = slice(32 * j, 32 * j + 32)
                        m = A(qd[lanes, :, j, :], q[lanes], ACT.Copy)
                    m.then_inc(S["kq_out"], 1)
                    A(qT[:, c % 3, :, :], q, ACT.Copy).then_inc(S["qt_out"], 1)

                def state_out(i, c):
                    act.wait_ge(S["st_done"], 4 * (b * NQ + i) + c + 5)
                    for j in range(4):
                        lanes = slice(32 * j, 32 * j + 32)
                        m = A(state[lanes, (c + 1) % 2, :, j, :],
                              PS[lanes, 7, 0:9 * HD].rearrange("p (k d) -> p k d", k=3), ACT.Copy)
                    m.then_inc(S["st_out"], 1)

                def square_outputs(i, p):
                    act.wait_ge(S["ctr_ready"], 2 * (b * NQ + i) + p + 1)
                    A(osq, osum[:, 2 * p:2 * p + 2, :], ACT.Square).then_inc(S["osq_out"], 1)

                def deviation(i, p):
                    act.wait_ge(S["ovar"], 2 * (b * NQ + i) + p + 1)
                    A(ost[:, 2 * p:2 * p + 2, :], ost[:, 2 * p:2 * p + 2, :], ACT.Sqrt, bias=eps_ln[0:T],
                      scale=1.0 / HD).then_inc(S["osd_out"], 1)

                def outputs_turned(i):
                    for p in range(2):
                        act.wait_ge(S["ot_done"], 2 * (b * NQ + i) + p + 1)
                        A(oT[:, :, 2 * p:2 * p + 2, :],
                          bank(3 + p, DH, 4 * T).rearrange("p (k c t) -> p k c t", k=2, c=2),
                          ACT.Copy).then_inc(S["ot_out"], 1)

                def stage_h(i, first=False, more=True):
                    v_out(i, 0)
                    square(i, 0)
                    if not first:
                        square_outputs(i - 1, 1)
                        deviation(i - 1, 1)
                    square(i, 1)
                    v_out(i, 1)
                    roots(i, 0)
                    if not first:
                        outputs_turned(i - 1)
                    qk_to_sbuf(i, 0)
                    square(i, 2)
                    square(i, 3)
                    roots(i, 1)
                    for c in range(3):
                        qk_to_sbuf(i, c + 1)
                        state_out(i, c)
                    square_outputs(i, 0)
                    deviation(i, 0)
                    state_out(i, 3)
                    if more:
                        xt_out(b * (TPASS * NQ) + 3 * NQ + i + 1, first=5)

                xt_out(b * (TPASS * NQ) + 3 * NQ, first=5)
                stage_h(0, first=True)
                with act.Fori(1, NQ - 1) as i:
                    stage_h(i)
                stage_h(NQ - 1, more=False)
                def x_out(i):
                    q = b * (TPASS * NQ) + 4 * NQ + i
                    act.wait_ge(S["xh_ready"], 2 * q + 2)
                    A(ch(hx, i, 0, 4), xh[:, :, :], ACT.Copy).then_inc(S["x_kept"], 1)
                    xt_out(q)

                act.wait_ge(dT.sem, dT.value(b * NQ, "keep"))
                deviations(3, aI, slice(0, 4), "sd0")
                square_outputs(NQ - 1, 1)
                deviation(NQ - 1, 1)
                outputs_turned(NQ - 1)
                x_out(0)
                act.wait_ge(dT.sem, dT.value(b * NQ + NQ - 1, "keep"))
                deviations(3, aI, slice(4, NC), "sd")
                act.wait_ge(dI.sem, dI.value(b, "ms"))
                aI.mark(A(rn[:, :], rn[:, :], ACT.Sqrt, bias=eps_rms[0:T]), "rms")

                def logits_out(i):
                    act.wait_ge(S["lt_done"], b * NQ + i + 1)
                    A(lgT[:, :], bank(7, E, 4 * T), ACT.Copy).then_inc(S["lt_out"], 1)

                def logits_kept(i):
                    act.wait_ge(S["lg_done"], b * NQ + i + 1)
                    A(lg[:, :, bass.ds(4 * i, 4)].rearrange("p e c -> p c e"),
                      bank(6, T, 4 * E).rearrange("p (c e) -> p c e", c=4), ACT.Copy).then_inc(S["lg_out"], 1)

                def x_next(i):
                    logits_out(i)
                    x_out(i + 1)
                    logits_kept(i)

                pipelined(act, lambda: hold(act), x_next, lambda i: [logits_out(i), logits_kept(i)])
                act.wait_ge(dR.sem, dR.value(b, "shift"))
                aR.mark(A(rtmp[:, :, :], rtmp[:, :, :], ACT.Exp), "exp")
            conv_stage(0)
            with act.Fori(0, nb - 1) as b:
                image(b)
                conv_stage(b + 1, after=b)
            image(nb - 1)
            with act.Fori(0, NQ) as i:
                residual(nb - 1, i)
            with act.Fori(0, E // 2) as k2:
                for s in range(2):
                    e = 2 * k2 + s
                    act.wait_ge(S["moe_f"], 6 * e + 6)
                    act.wait_ge(S["moe_turned"], e + 2)
                    for p in range(2):
                        m = A(mT[:, :, 256 * p:256 * (p + 1)], bank(p, DH, 512).rearrange("p (k n) -> p k n", k=2),
                              ACT.Copy)
                    m.then_inc(S["moe_xt"], 1)
                    act.wait_ge(S["moe_o"], 2 * e + 3)
                    for f in (0, 2, 4):
                        act.wait_ge(S["moe_f"], 6 * e + f + 7)
                        A(mh[:, f, :], PS[:, 2 + f % 4, :], ACT.Relu).then_inc(S["moe_ra"], 1)

        @block.vector
        def _(dve):
            tt, ts, stt = nc.vector.tensor_tensor, nc.vector.tensor_scalar, nc.vector.scalar_tensor_tensor
            red, cp = nc.vector.tensor_reduce, nc.vector.tensor_copy

            def settle(steps, done, name):
                dve.wait_ge(steps.sem, steps.value(done, name))

            def two_ahead(prepare, body, first=0, last=lambda: None):
                for i in range(first, 2):
                    prepare(i)
                with dve.Fori(0, NQ - 2) as i:
                    body(i, lambda: prepare(i + 2))
                body(NQ - 2, lambda: None)
                body(NQ - 1, last)

            dS.mark(nc.vector.memset(qk[:, :, :, :], 0.0), "pad")
            dS.mark(nc.vector.memset(state[:, :, :, :, :], 0.0), "state")
            dS.mark(nc.vector.memset(csel[:, :, :, :], 0.0), "sel")
            dS.mark(nc.vector.memset(slots[:, :, :], 0.0), "slots")
            dve.wait_ge(S["packed_in"], 16)
            give_leads(dve, conv_out=2, h1_ready=2, h2_ready=2, uprod_done=1, o_out=1, h3_ready=2,
                       image_done=1, res_ready=2, patches_done=2, moe_y=2)
            dS.mark(tt(cprod[:, 0:2, :], gate, gate, ALU.mult), "gsq")
            settle(dS, 0, "gsq")
            dS.mark(red(gss[:, :], cprod[:, 0:2, :], AX.X, ALU.add), "gss")
            dve.wait_ge(aS.sem, aS.value(0, "gnorm"))
            dS.mark(ts(gss[:, :], gss[:, :], 1e-12, None, ALU.max), "nmax")
            settle(dS, 0, "nmax")
            dS.mark(nc.vector.reciprocal(gss[:, :], gss[:, :]), "nrec")
            settle(dS, 0, "nrec")
            dS.mark(tt(gate, gate, spread(gss[:, :], 2, D), ALU.mult), "gate")
            dS.mark(tt(halves["router"], halves["router"], spread(w("lnwT"), 2, E), ALU.mult), "router")
            dS.mark(ts(tau[:, :], w("logtau"), -50.0, 30.0, ALU.max, ALU.min), "tau")
            dve.wait_ge(aS.sem, aS.value(0, "tau"))
            dS.mark(tt(taumu.rearrange("p (h d) -> p h d", h=HL), w("mu").rearrange("p (h d) -> p h d", h=HL),
                       spread(tau[:, :], 2, HD), ALU.mult), "taumu")
            dS.mark(tt(scoef[:, :, :], spread(w("pos"), 2, HL), spread(tau[:, :], 1, NC), ALU.add), "s0")
            settle(dS, 0, "s0")
            dS.mark(nc.vector.reciprocal(scoef[:, :, :], scoef[:, :, :]), "s1")
            settle(dS, 0, "s1")
            dS.mark(ts(scoef[:, :, :], scoef[:, :, :], -1.0 / HD ** 0.5, None, ALU.mult), "s2")
            dS.mark(nc.vector.reciprocal(invt[:, :], w("pos")), "invt")
            settle(dS, 0, "invt")

            def normalise(q, i, n):
                for p in range(2):
                    dve.wait_ge(S["turned"], 2 * q + p + 1)
                    for c in (2 * p, 2 * p + 1):
                        m = ts(xh[:, c, :], one(ch(hx, i, c)), one(ch(mv[n], i, c)[:, :, 0:1]), ch(rs[n], i, c),
                               ALU.subtract, ALU.mult)
                    m.then_inc(S["xh_ready"], 1)

            def stats(steps, done, i, n):
                hold(dve)
                for c in range(4):
                    m = nc.vector.bn_stats(bns[:, c, :], one(ch(hx, i, c)))
                steps.mark(m, "stat")
                settle(steps, done, "stat")
                hold(dve)
                for c in range(4):
                    m = nc.vector.bn_aggr(bnv[:, c, :], bns[:, c, :])
                steps.mark(m, "agg")
                settle(steps, done, "agg")
                hold(dve)
                steps.mark(cp(ch(mv[n], i, 0, 4), bnv[:, :, :]), "keep")

            def add_pair(i, p, bk):
                return tt(ch(hx, i, 2 * p, 2), ch(hx, i, 2 * p, 2), bank(bk, T, 2 * D).rearrange("p (c n) -> p c n", c=2),
                          ALU.add)

            def picks(b, i):
                for c in range(4):
                    dve.wait_ge(S["slots_done"], 4 * (b * NQ + i) + c + 1)
                    ts(pick[:, c, :], w("iota128"), ch(posx, i, c),
                       w("tokid")[:, bass.ds(b * NC + 4 * i + c, 1)], ALU.is_equal, ALU.mult)\
                        .then_inc(S["pick_ready"], 1)

            def unrouted(b, i):
                g = b * NQ + i
                for p in range(2):
                    dve.wait_ge(S["xo_ready"], 2 * g + p + 1)
                    dve.wait_ge(S["xs_ready"], 2 * g + p + 1)
                    if p == 0:
                        dve.wait_ge(S["out_written"], 16 * g + 16)
                    for c in (2 * p, 2 * p + 1):
                        m = stt(ob[:, c, :], xo[:, c, :], ch(prs, i, c), hs[:, c, :], ALU.mult, ALU.add)
                    m.then_inc(S["res_ready"], 1)

            def slots_close(b):
                dve.wait_ge(S["slots_done"], 4 * NQ * b + 4 * NQ + 4)
                pair = slots[:, bass.ds(b // 2, 1), :].rearrange("p a e -> p (a e)")
                tt(pair, pair, bank(3, 128, E), ALU.add).then_inc(S["image_done"], 1)

            def conv_stage(b, after=None):
                def with_bias(i):
                    g = b * NQ + i
                    if after is not None:
                        dve.wait_ge(S["rows_written"], 16 * (after * NQ + i) + 32)
                    for p in range(2):
                        dve.wait_ge(S["conv_done"], 2 * g + p + 3)
                        tt(ch(hx, i, 2 * p, 2), bank(6 + p, T, 2 * D).rearrange("p (c n) -> p c n", c=2),
                           spread(w("tok_b"), 1, 2), ALU.add).then_inc(S["conv_out"], 1)
                    dve.wait_ge(S["conv_out"], 2 * g + 4)
                    stats(dA, g, i, 0)

                def normal_quad(i):
                    g = b * NQ + i
                    dve.wait_ge(aA.sem, aA.value(g, "sd"))
                    dA.mark(nc.vector.reciprocal(ch(rs[0], i, 0, 4), ch(rs[0], i, 0, 4)), "rstd")
                    dve.wait_ge(S["gram_read"], g + 1)
                    settle(dA, g, "rstd")
                    for c in range(4):
                        m = ts(xg[:, c, :], one(ch(hx, i, c)), bnv[:, c, 0:1], ch(rs[0], i, c),
                               ALU.subtract, ALU.mult)
                    m.then_inc(S["xg_ready"], 1)

                def body(i):
                    with_bias(i)
                    if after is not None:
                        picks(after, i + 1)
                    normal_quad(i)
                    if after is not None:
                        unrouted(after, i + 1)

                def lead_in():
                    if after is not None:
                        dve.wait_ge(S["x_kept"], NQ * after + NQ + 1)
                        hold(dve)
                        picks(after, 0)
                        unrouted(after, 0)

                def lead_out(i):
                    with_bias(i)
                    normal_quad(i)
                    if after is not None:
                        slots_close(after)
                        dve.wait_ge(S["out_written"], 16 * NQ * b + 16)
                        hold(dve)

                pipelined(dve, lead_in, body, lead_out)

            def image(b):
                dve.wait_ge(S["gram_read"], NQ * b + NQ + 1)
                dB.mark(cp(gram[:, 0, :], bank(4, DH, D)), "g0")
                dB.mark(cp(gram[:, 1, DH:D], bank(5, DH, DH)), "g1")
                dve.wait_ge(pB.sem, pB.value(b, "mirror"))
                dB.mark(cp(gram[:, 1, 0:DH], bank(2, DH, DH)), "g2")
                dve.wait_ge(pB.sem, pB.value(b, "gw"))
                gw = [bank(k, DH, 2 * D).rearrange("p (k n) -> p k n", k=2) for k in (4, 5)]
                dB.mark(cp(gk[:, :, :], gw[0]), "gk")
                dB.mark(tt(prodk[:, :, :], gw[0], halves["wk0"], ALU.mult), "pk")
                dB.mark(tt(prodq[:, :, :], gw[1], halves["wq0"], ALU.mult), "pq")
                dve.wait_ge(aB.sem, aB.value(b, "norm"))
                dB.mark(nc.vector.reciprocal(norm0[:, :], norm0[:, :]), "rnorm")
                settle(dB, b, "rnorm")
                dB.mark(tt(rsum[:, :], norm0[:, D:D + 2], w("temp"), ALU.mult), "rqt")
                dB.mark(tt(att0[:, :, :], bank(2, DH, D).rearrange("p (k n) -> p k n", k=2),
                           norm0[:, 0:D].rearrange("p (k n) -> p k n", k=2), ALU.mult), "l0")
                settle(dB, b, "l0")
                for n in range(2):
                    dB.mark(stt(att0[:, n, :], att0[:, n, :], rsum[:, n:n + 1], w("offblock"), ALU.mult, ALU.add),
                            f"l{n + 1}")
                settle(dB, b, "l2")
                dB.mark(red(rowm[:, :], att0[:, :, :], AX.X, ALU.max, negate=True), "rowm")
                dve.wait_ge(aB.sem, aB.value(b, "exp"))
                dB.mark(red(rsum[:, :], att0[:, :, :], AX.X, ALU.add), "rsum")
                settle(dB, b, "rsum")
                nc.vector.reciprocal(rsum[:, :], rsum[:, :]).then_inc(S["att_rsum"], 1)
                dve.wait_ge(S["att_rsum"], b + 1)
                dB.mark(tt(att0[:, :, :], att0[:, :, :], spread(rsum[:, :], 2, DH), ALU.mult), "att")
                dve.wait_ge(pB.sem, pB.value(b, "t1"))
                dB.mark(cp(t1sb[:, :, :], bank(2, DH, 2 * D).rearrange("p (k n) -> p k n", k=2)), "t1")
                dve.wait_ge(pB.sem, pB.value(b, "mix"))
                dB.mark(cp(mix[:, :, :], bank(3, DH, 2 * D).rearrange("p (k n) -> p k n", k=2)), "mix")

                def mixed(i, prepare_next):
                    g = b * NQ + i
                    for p in range(2):
                        dve.wait_ge(S["bias_in"], 2 * NQ * b + i + 1)
                        dve.wait_ge(S["mix_done"], 2 * g + p + 3)
                        add_pair(i, p, 6 + p).then_inc(S["h1_ready"], 1)
                    prepare_next()
                    dve.wait_ge(S["h1_ready"], 2 * g + 4)
                    stats(dC, g, i, 1)

                h_class = h[0:NCLS, 0, 0:D]

                def next_quad(i):
                    normalise(b * (TPASS * NQ) + NQ + i + 1, i + 1, 1)

                def first_normal():
                    dve.wait_ge(S["h1_ready"], 2 * NQ * b + 2 * NQ + 2)
                    dve.wait_ge(aR2.sem, aR2.value(b, "sd0"))
                    dR2.mark(nc.vector.reciprocal(rs[1][:, 0:4], rs[1][:, 0:4]), "rstd0")
                    settle(dR2, b, "rstd0")
                    dE.mark(cp(cres[:, :], h_class), "h")
                    dE.mark(ts(xc[:, :], h_class, mv[1][0:NCLS, 0, 0:1], rs[1][0:NCLS, 0:1], ALU.subtract, ALU.mult),
                            "xc")
                    next_quad(-1)

                two_ahead(lambda i: normalise(b * (TPASS * NQ) + i, i, 0), mixed, last=first_normal)
                dve.wait_ge(aR2.sem, aR2.value(b, "sd"))
                dR2.mark(nc.vector.reciprocal(rs[1][:, 4:NC], rs[1][:, 4:NC]), "rstd")
                settle(dR2, b, "rstd")

                def fed(i, amid=lambda: None):
                    g = b * NQ + i
                    for p in range(2):
                        dve.wait_ge(S["bias_in"], 2 * NQ * b + NQ + i + 1)
                        dve.wait_ge(S["patches_done"], 2 * g + p + 3)
                        add_pair(i, p, 6 + p).then_inc(S["h2_ready"], 1)
                    dve.wait_ge(S["h2_ready"], 2 * g + 4)
                    amid()
                    stats(dD, g, i, 2)

                settle(dE, b, "xc")
                dE.mark(tt(cprod[:, 0:2, :], gate, spread(xc[:, :], 1, 2), ALU.mult), "prod")
                dE.mark(tt(cprod[:, 2, :], xc[:, :], xc[:, :], ALU.mult), "sq")
                settle(dE, b, "sq")
                dE.mark(red(csum[:, :], cprod[:, :, :], AX.X, ALU.add), "sum")
                next_quad(0)
                dve.wait_ge(aE.sem, aE.value(b, "norm"))
                dE.mark(ts(csum[:, 2:3], csum[:, 2:3], 1e-12, None, ALU.max), "nmax")
                settle(dE, b, "nmax")
                dE.mark(nc.vector.reciprocal(csum[:, 2:3], csum[:, 2:3]), "nrec")
                settle(dE, b, "nrec")
                dE.mark(stt(clog[:, :], csum[:, 0:2], csum[:, 2:3], w("bal"), ALU.mult, ALU.add), "log")
                settle(dE, b, "log")
                dE.mark(tt(cext[:, 0:1], clog[:, 0:1], clog[:, 1:2], ALU.max), "max")
                dE.mark(tt(cext[:, 1:2], clog[:, 0:1], clog[:, 1:2], ALU.min), "min")
                settle(dE, b, "min")
                dE.mark(tt(cext[:, 1:2], cext[:, 1:2], cext[:, 0:1], ALU.subtract), "diff")
                dE.mark(tt(cflag[:, 0:1], clog[:, 0:1], clog[:, 1:2], ALU.is_ge), "flag0")
                dE.mark(tt(cflag[:, 1:2], clog[:, 0:1], clog[:, 1:2], ALU.is_lt), "flag1")
                dve.wait_ge(aE.sem, aE.value(b, "exp"))
                dE.mark(ts(cext[:, 0:1], cext[:, 1:2], 1.0, None, ALU.add), "p1")
                settle(dE, b, "p1")
                dE.mark(nc.vector.reciprocal(cext[:, 0:1], cext[:, 0:1]), "p")
                for n in range(2):
                    dE.mark(ts(cdiag[:, n, :], ident[0:NCLS, 0:NCLS], cflag[:, n:n + 1], None, ALU.mult), f"diag{n}")
                fed(0)
                dve.wait_ge(pE.sem, pE.value(b, "hidden"))
                dE.mark(tt(cpre[:, :, :], bank(4, 128, NAT * FT * NCLS).rearrange("p (a n) -> p a n", n=NCLS),
                           spread(w("in_b"), 2, NCLS), ALU.add), "pre")
                next_quad(1)
                dve.wait_ge(pE.sem, pE.value(b, "flags"))
                dE.mark(cp(cflagb[:, :], bank(4, 128, 2 * NCLS)), "flags")
                fed(1)
                next_quad(2)
                dve.wait_ge(aE.sem, aE.value(b, "gelu"))
                settle(dE, b, "flags")
                for a in range(3):
                    for t in range(2):
                        n = 2 * a + t
                        ts(csel[:, 3 + t, :, n], chid[:, a, :, n], cflagb[:, n:n + 1], None, ALU.mult)
                        m = ts(csel[:, a, :, n], chid[:, 3 + t, :, n], cflagb[:, NCLS + n:NCLS + n + 1], None, ALU.mult)
                dE.mark(m, "sel")
                out_b = w("out_b").rearrange("p (r n) -> p r n", r=2)
                dE.mark(ts(cbias[:, :], out_b[:, 0, :], cflag[:, 0:1], None, ALU.mult), "bias0")
                settle(dE, b, "bias0")
                dE.mark(stt(cbias[:, :], out_b[:, 1, :], cflag[:, 1:2], cbias[:, :], ALU.mult, ALU.add), "bias")
                fed(2)
                dve.wait_ge(pE.sem, pE.value(b, "out"))
                dE.mark(tt(cbias[:, :], cbias[:, :], bank(5, NCLS, D), ALU.add), "res0")
                settle(dE, b, "res0")
                dE.mark(stt(cres[:, :], cbias[:, :], cext[:, 0:1], cres[:, :], ALU.mult, ALU.add), "res")
                with dve.Fori(3, NQ - 1) as i:
                    next_quad(i)
                    fed(i)
                dve.wait_ge(dE.sem, dE.value(b, "res"))
                dR3.mark(cp(h[0:NCLS, 0, 0:D], cres[:, :]), "class")
                settle(dR3, b, "class")
                dR3.mark(nc.vector.bn_stats(bns[:, 0, :], h[:, 0, 0:D]), "stat")
                settle(dR3, b, "stat")
                hold(dve)
                dR3.mark(nc.vector.bn_aggr(mv[2][:, 0, :], bns[:, 0, :]), "agg")
                settle(dR3, b, "agg")

                def second_normal():
                    dve.wait_ge(aR3.sem, aR3.value(b, "sd0"))
                    dR3.mark(nc.vector.reciprocal(rs[2][:, 0:4], rs[2][:, 0:4]), "rstd0")
                    settle(dR3, b, "rstd0")
                    normalise(b * (TPASS * NQ) + 2 * NQ, 0, 2)

                fed(NQ - 1, second_normal)
                dve.wait_ge(aR3.sem, aR3.value(b, "sd"))
                dR3.mark(nc.vector.reciprocal(rs[2][:, 4:NC], rs[2][:, 4:NC]), "rstd")
                settle(dR3, b, "rstd")
                hold(dve)

                def s_of(i, prepare_next):
                    g = b * NQ + i
                    prepare_next()
                    dve.wait_ge(S["us_done"], 4 * g + 8)
                    tt(uprod[:, :, :], ug[:, :, 0:D], PS[0:T, 4:8, 0:D], ALU.mult).then_inc(S["uprod_done"], 1)
                    dve.wait_ge(S["uprod_done"], g + 2)
                    red(sraw[:, :, :], uprod[:, :, :].rearrange("p c (h d) -> p c h d", h=HL), AX.X, ALU.add)\
                        .then_inc(S["s_kept"], 1)
                    dve.wait_ge(S["s_kept"], 2 * g + 1)
                    tt(es[:, HL:2 * HL, bass.ds(4 * i, 4)].rearrange("p h c -> p c h"), sraw[:, :, :],
                       ch(scoef, i, 0, 4), ALU.mult).then_inc(S["s_kept"], 1)

                two_ahead(lambda i: normalise(b * (TPASS * NQ) + 2 * NQ + i, i, 2), s_of, first=1)

                dve.wait_ge(S["s_kept"], 2 * NQ * b + 2 * NQ)
                dG.mark(red(smax[:, :], es[:, HL:2 * HL, :], AX.X, ALU.max), "max")
                dve.wait_ge(pG.sem, pG.value(b, "maxT"))
                dG.mark(red(smaxT[:, :], bank(2, HL, T), AX.X, ALU.max), "maxT")
                settle(dG, b, "maxT")
                dG.mark(ts(sdiag[:, :], ident[0:HL, 0:HL], smaxT[:, :], None, ALU.mult), "diag")
                dve.wait_ge(pG.sem, pG.value(b, "max"))
                dG.mark(tt(es[:, 0:HL, :], es[:, HL:2 * HL, :], spread(bank(3, T, HL), 2, NC), ALU.subtract), "shift")
                dve.wait_ge(pG.sem, pG.value(b, "sums"))
                cumf = cum[:, :, :].rearrange("p (k h) c -> p k (h c)", k=2)
                for k in range(2):
                    dG.mark(nc.vector.tensor_tensor_scan(cumf[:, k, :], w("reset")[:, 0:HL * NC], bank(6 + k, T, HL * NC),
                                                         0.0, ALU.mult, ALU.add), f"scan{k}")
                settle(dG, b, "scan1")
                dG.mark(tt(cumf, cumf, PS[0:T, 6:8, 0:HL * NC], ALU.subtract), "excl")
                settle(dG, b, "excl")
                dG.mark(tt(cumf, cumf, PS[0:T, 4:6, 0:HL * NC], ALU.add), "sum")
                settle(dG, b, "sum")
                dve.wait_ge(aG.sem, aG.value(b, "gates"))
                gt = gates[:, :, :].rearrange("p c h -> p h c")
                sig1, sigh = gt[:, 0:HL, :], gt[:, HL:2 * HL, :]
                dG.mark(ts(cum[:, 0:HL, :], cum[:, 0:HL, :], 1e-12, None, ALU.add), "eps")
                settle(dG, b, "eps")
                dG.mark(nc.vector.reciprocal(cum[:, 0:HL, :], cum[:, 0:HL, :]), "einv")
                settle(dG, b, "einv")
                dG.mark(tt(coef[:, 0, :, :], cum[:, 0:HL, :], sigh, ALU.mult), "al")
                dG.mark(tt(coef[:, 1, :, :], sig1, sigh, ALU.subtract), "be0")
                settle(dG, b, "be0")
                dG.mark(tt(coef[:, 1, :, :], coef[:, 1, :, :], spread(invt[:, :], 1, HL), ALU.mult), "be")
                settle(dG, b, "be")
                dG.mark(tt(coef[:, 2, :, :], coef[:, 1, :, :], cum[:, HL:2 * HL, :], ALU.mult), "ga0")
                settle(dG, b, "ga0")
                dG.mark(tt(coef[:, 2, :, :], coef[:, 2, :, :], sigh, ALU.add), "ga1")
                settle(dG, b, "ga1")
                dG.mark(stt(coef[:, 2, :, :], coef[:, 2, :, :], -1.0, spread(invt[:, :], 1, HL), ALU.mult, ALU.mult),
                        "ga")

                def rope(i, c):
                    g = b * NQ + i
                    dve.wait_ge(S["qk_done"], 4 * g + c + 1)
                    dve.wait_ge(S["qk_ready"], 4 * g + c + 1)
                    x = bank(2 + c, T, 2 * D).rearrange("p (h d e) -> p h d e", d=HD // 2, e=2)
                    r1, r2 = (r[:, c, :, :].rearrange("p h (d e) -> p h d e", e=2) for r in (rope1, rope2))
                    tt(r1, x, spread(spread(one(ch(cos, i, c)), 1, 2 * HL), 3, 2), ALU.mult)
                    lo, hi = slice(0, HD // 4), slice(HD // 4, HD // 2)
                    for to, frm in ((lo, hi), (hi, lo)):
                        m = tt(r2[:, :, to], x[:, :, frm],
                               spread(spread(one(ch(sin, i, c)[:, :, to]), 1, 2 * HL), 3, 2), ALU.mult)
                    m.then_inc(S["rope_done"], 1)

                def squares_summed(i, p):
                    pair = slice(2 * p, 2 * p + 2)
                    dve.wait_ge(S["squared"], 4 * (b * NQ + i) + 2 * p + 2)
                    dH.mark(red(nrm[:, pair, :], rope1[:, pair, :, :], AX.X, ALU.add), f"ss{p}")

                def norms(i, p):
                    g = b * NQ + i
                    pair = slice(2 * p, 2 * p + 2)
                    dve.wait_ge(S["rn_ready"], 2 * g + p + 1)
                    dN.mark(ts(nrm[:, pair, :], nrm[:, pair, :], 1e-12, None, ALU.max), f"nmax{p}")
                    settle(dN, g, f"nmax{p}")
                    dN.mark(nc.vector.reciprocal(nrm[:, pair, :], nrm[:, pair, :]), f"nrec{p}")

                def masked(i, c):
                    g = b * NQ + i
                    if c >= 2:
                        dve.wait_ge(S["o_done"], 4 * g + c - 1)
                    for k in range(3):
                        dve.wait_ge(S["s_done"], 12 * g + 3 * c + k + 1)
                        tt(att[:, c % 2, k, :, :], bank(2 + k, T, 4 * T).rearrange("p (j t) -> p j t", j=4),
                           spread(tri, 1, 4), ALU.mult).then_inc(S["s_out"], 1)

                def weigh(i, c):
                    g = b * NQ + i
                    dve.wait_ge(S["o_done"], 4 * g + c + 1)
                    if c == 0:
                        dve.wait_ge(S["c_ready"], g + 1)
                    for n, heads_of in enumerate((slice(0, 8), slice(8, HL))):
                        k = heads_of.stop - heads_of.start
                        m = tt(o3[:, c, heads_of, :, :],
                               bank(n, T, k * 3 * HD).rearrange("p (h j d) -> p h j d", h=k, j=3),
                               spread(cq[:, c, heads_of, :], 3, HD), ALU.mult)
                    m.then_inc(S["o_out"], 1)

                def mean(i, p):
                    g = b * NQ + i
                    pair = slice(2 * p, 2 * p + 2)
                    dve.wait_ge(S["osum_ready"], 2 * g + p + 1)
                    dL.mark(red(ost[:, pair, :], osum[:, pair, :].rearrange("p c (h d) -> p c h d", h=HL), AX.X, ALU.add),
                            f"sum{p}")
                    settle(dL, g, f"sum{p}")
                    dL.mark(ts(ost[:, pair, :], ost[:, pair, :], -1.0 / HD, None, ALU.mult), f"mean{p}")

                def variance(i, p):
                    pair = slice(2 * p, 2 * p + 2)
                    dve.wait_ge(S["osq_out"], 2 * (b * NQ + i) + p + 1)
                    red(ost[:, pair, :], osq.rearrange("p c (h d) -> p c h d", h=HL), AX.X, ALU.add)\
                        .then_inc(S["ovar"], 1)

                def deviation(i, p):
                    pair = slice(2 * p, 2 * p + 2)
                    dve.wait_ge(S["osd_out"], 2 * (b * NQ + i) + p + 1)
                    dL.mark(nc.vector.reciprocal(ost[:, pair, :], ost[:, pair, :]), f"rec{p}")

                def projected(i, p):
                    g = b * NQ + i
                    dve.wait_ge(S["wo_done"], 2 * g + p + 1)
                    add_pair(i, p, p).then_inc(S["h3_ready"], 1)

                def h3_stats(i):
                    g = b * NQ + i
                    dve.wait_ge(S["h3_ready"], 2 * g + 4)
                    stats(dT, g, i, 3)

                def stage_h(i, first=False, more=True):
                    rope(i, 0)
                    if not first:
                        mean(i - 1, 1)
                    rope(i, 1)
                    if not first:
                        variance(i - 1, 1)
                    if not first:
                        deviation(i - 1, 1)
                    rope(i, 2)
                    squares_summed(i, 0)
                    rope(i, 3)
                    norms(i, 0)
                    squares_summed(i, 1)
                    if more:
                        normalise(b * (TPASS * NQ) + 3 * NQ + i + 1, i + 1, 2)
                    norms(i, 1)
                    if not first:
                        projected(i - 1, 0)
                    masked(i, 0)
                    if not first:
                        projected(i - 1, 1)
                    masked(i, 1)
                    if not first:
                        h3_stats(i - 1)
                    weigh(i, 0)
                    masked(i, 2)
                    weigh(i, 1)
                    masked(i, 3)
                    mean(i, 0)
                    weigh(i, 2)
                    variance(i, 0)
                    deviation(i, 0)
                    weigh(i, 3)

                normalise(b * (TPASS * NQ) + 3 * NQ, 0, 2)
                stage_h(0, first=True)
                with dve.Fori(1, NQ - 1) as i:
                    stage_h(i)
                stage_h(NQ - 1, more=False)
                mean(NQ - 1, 1)
                variance(NQ - 1, 1)
                deviation(NQ - 1, 1)
                dve.wait_ge(aI.sem, aI.value(b, "sd0"))
                dI.mark(ts(h[:, 0:4, SD], rs[3][:, 0:4], 1.0, None, ALU.add), "one_sd0")
                dI.mark(nc.vector.reciprocal(rs[3][:, 0:4], rs[3][:, 0:4]), "rstd0")
                settle(dI, b, "rstd0")
                normalise(b * (TPASS * NQ) + 4 * NQ, 0, 3)
                projected(NQ - 1, 0)
                projected(NQ - 1, 1)
                h3_stats(NQ - 1)

                dve.wait_ge(aI.sem, aI.value(b, "sd"))
                dI.mark(ts(h[:, 4:NC, SD], rs[3][:, 4:NC], 1.0, None, ALU.add), "one_sd")
                dI.mark(cp(h[:, :, MEAN], mv[3][:, :, 0]), "mean")
                dI.mark(nc.vector.reciprocal(rs[3][:, 4:NC], rs[3][:, 4:NC]), "rstd")
                settle(dI, b, "rstd")
                dI.mark(tt(rn[:, :], rs[3][:, :], rs[3][:, :], ALU.mult), "sq")
                settle(dI, b, "sq")
                dI.mark(tt(rn[:, :], rn[:, :], mv[3][:, :, 1], ALU.mult), "ms")
                dve.wait_ge(aI.sem, aI.value(b, "rms"))
                dI.mark(nc.vector.reciprocal(rn[:, :], rn[:, :]), "rn")
                settle(dI, b, "rn")
                dI.mark(cp(h[:, :, RN], rn[:, :]), "keep")
                with dve.Fori(1, NQ) as i:
                    dve.wait_ge(S["x_kept"], b * NQ + i + 1)
                    normalise(b * (TPASS * NQ) + 4 * NQ + i, i, 3)

                dve.wait_ge(S["lg_out"], NQ * b + NQ + 1)
                by_chunk = lg[:, :, :].rearrange("p e c -> p c e")
                dR.mark(tt(lg[:, :, :], lg[:, :, :], spread(rn[:, :], 1, E), ALU.mult), "scale")
                settle(dR, b, "scale")
                dR.mark(red(rmax[:, :], by_chunk, AX.X, ALU.max), "max")
                settle(dR, b, "max")
                dR.mark(tt(rtmp[:, :, :], lg[:, :, :], spread(rmax[:, :], 1, E), ALU.subtract), "shift")
                dR.mark(tt(prio[:, :, :], lg[:, :, :], spread(rmax[:, :], 1, E), ALU.is_equal), "eq")
                settle(dR, b, "eq")
                dR.mark(stt(prio[:, :, :], prio[:, :, :], -1000.0, spread(w("iotae"), 2, NC), ALU.mult, ALU.add),
                        "first")
                settle(dR, b, "first")
                dR.mark(red(posx[:, :], prio[:, :, :].rearrange("p e c -> p c e"), AX.X, ALU.min), "lowest")
                settle(dR, b, "lowest")
                dR.mark(tt(onehot[:, :, :], prio[:, :, :], spread(posx[:, :], 1, E), ALU.is_equal), "onehot")
                dve.wait_ge(aR.sem, aR.value(b, "exp"))
                dR.mark(red(prob[:, :], rtmp[:, :, :].rearrange("p e c -> p c e"), AX.X, ALU.add), "psum")
                settle(dR, b, "psum")
                dR.mark(nc.vector.reciprocal(prob[:, :], prob[:, :]), "prob")
                settle(dR, b, "prob")
                dR.mark(tt(prs[:, :], prob[:, :], rn[:, :], ALU.mult), "prs")
                dR.mark(cp(h[:, :, PROB], prob[:, :]), "keepp")
                dve.wait_ge(pR.sem, pR.value(b, "sums"))
                flat = [t[:, :, :].rearrange("p e c -> p (e c)") for t in (prio, rtmp, onehot)]
                dR.mark(nc.vector.tensor_tensor_scan(flat[0], w("reset")[:, 0:E * NC], bank(3, T, E * NC), 0.0,
                                                     ALU.mult, ALU.add), "scan")
                settle(dR, b, "scan")
                dR.mark(tt(flat[0], flat[0], bank(3, T, E * NC), ALU.subtract), "excl")
                settle(dR, b, "excl")
                dR.mark(tt(flat[0], flat[0], bank(2, T, E * NC), ALU.add), "prio")
                settle(dR, b, "prio")
                dR.mark(ts(flat[1], flat[0], CAP + 0.5, None, ALU.is_lt), "under")
                settle(dR, b, "under")
                dR.mark(tt(flat[2], flat[2], flat[1], ALU.mult), "keep")
                settle(dR, b, "keep")
                dR.mark(tt(flat[1], flat[0], flat[2], ALU.mult), "pz")
                settle(dR, b, "pz")
                dR.mark(red(posx[:, :], rtmp[:, :, :].rearrange("p e c -> p c e"), AX.X, ALU.add), "pos")
                settle(dR, b, "pos")
                dR.mark(ts(posx[:, :], posx[:, :], w("poff")[:, bass.ds(b, 1)], None, ALU.add), "posx")
                settle(dR, b, "posx")

            conv_stage(0)
            with dve.Fori(0, nb - 1) as b:
                image(b)
                conv_stage(b + 1, after=b)
            image(nb - 1)
            dve.wait_ge(S["x_kept"], NQ * nb + 1)
            with dve.Fori(0, NQ) as i:
                picks(nb - 1, i)
                unrouted(nb - 1, i)
            slots_close(nb - 1)
            dve.wait_ge(S["image_done"], nb + 1)
            dM.mark(nc.vector.memset(gidx[:, :, :], 0), "zero")
            dM.mark(ts(empty[:, :, :], slots[:, :, :], 0.0, FAR, ALU.is_equal, ALU.mult), "empty")
            dve.wait_ge(dM.sem, dM.value(0, "empty"))
            dM.mark(cp(gidx[:, 0:E, :], slots[:, :, :].rearrange("p b e -> p e b")), "gather")
            dM.mark(stt(empty[:, :, :], slots[:, :, :], -1.0, empty[:, :, :], ALU.add, ALU.add), "minus1")
            dve.wait_ge(dM.sem, dM.value(0, "minus1"))
            cp(sidx[:, :, :], empty[:, :, :].rearrange("p b e -> p e b")).then_inc(S["index_ready"], 1)

            def expert(e, k2, s, first=False):
                dve.wait_ge(S["moe_turned"], e + 1)
                dve.wait_ge(S[f"gathered{s}"], 64 * k2 + 64)
                for n in range(4):
                    m = stt(mx[:, n, :], mrow[s][:, n, 0:D], mrow[s][:, n, RN:RN + 1], w("lnw"), ALU.mult, ALU.mult)
                m.then_inc(S["moe_x"], 1)
                dve.wait_ge(S["moe_o"], 2 * e + 3)
                for f in (1, 3, 5):
                    dve.wait_ge(S["moe_f"], 6 * e + f + 7)
                    ts(mh[:, f, :], PS[:, 2 + f % 4, :], 0.0, None, ALU.max).then_inc(S["moe_rd"], 1)
                if not first:
                    dve.wait_ge(S[f"scattered{s}"], 64 * k2)
                for n in range(4):
                    m = ts(my[s][:, n, :], mrow[s][:, n, 0:D], mrow[s][:, n, SD:SD + 1],
                           mrow[s][:, n, MEAN:MEAN + 1], ALU.mult, ALU.add)
                m.then_inc(S["moe_h"], 1)
                dve.wait_ge(S["moe_h"], e + 1)
                for p in range(2):
                    dve.wait_ge(S["moe_o"], 2 * e + p + 4)
                    for n in (2 * p, 2 * p + 1):
                        m = stt(my[s][:, n, :], PS[:, 6 + p, (n % 2) * D:(n % 2 + 1) * D],
                                mrow[s][:, n, PROB:PROB + 1], my[s][:, n, :], ALU.mult, ALU.add)
                    m.then_inc(S["moe_y"], 1)

            for s in range(2):
                expert(s, 0, s, first=True)
            with dve.Fori(0, E // 2 - 1) as k:
                for s in range(2):
                    expert(2 * k + 2 + s, k + 1, s)

        @block.gpsimd
        def _(pool):
            tt, ts, cp = nc.gpsimd.tensor_tensor, nc.gpsimd.tensor_scalar, nc.gpsimd.tensor_copy
            pool.wait_ge(S["packed_in"], 16)
            give_leads(pool, gates_kept=1, v3_ready=4, qk_ready=4, slots_done=4)

            def add_bias(b, i, after, name):
                pool.wait_ge(S["xh_ready"], after)
                tt(ch(hx, i, 0, 4), ch(hx, i, 0, 4), spread(w(name), 1, 4), ALU.add).then_inc(S["bias_in"], 1)

            with pool.Fori(0, nb) as b:
                with pool.Fori(0, NQ) as i:
                    add_bias(b, i, 2 * (b * (TPASS * NQ) + i) + 2, "bproj")
                with pool.Fori(0, NQ) as i:
                    add_bias(b, i, 2 * (b * (TPASS * NQ) + NQ + i) + 2, "fc2_b")
                pool.wait_ge(dR3.sem, dR3.value(b, "agg"))
                hold(pool)
                lF.mark(nc.gpsimd.memset(usum[:, 0, :], 0.0), "zero")
                pool.wait_ge(lF.sem, lF.value(b, "zero"))
                hold(pool)
                cp(usum[0:1, 0, :], taumu[0:1]).then_inc(S["before_kept"], 1)
                with pool.Fori(0, NQ) as i:
                    g = b * NQ + i
                    for c in range(4):
                        if c % 2 == 0:
                            pool.wait_ge(S["ug_out"], 2 * g + c // 2 + 3)
                        pool.wait_ge(S["us_done"], 4 * g + c + 2)
                        pool.wait_ge(S["before_kept"], b + 4 * g + c + 1)
                        tt(usum[:, (c + 1) % 4, :], usum[:, c, :], ug[:, c, 0:D], ALU.add)\
                            .then_inc(S["before_kept"], 1)
                    cp(ch(gates, i, 0, 4), ug[:, :, D:GU]).then_inc(S["gates_kept"], 1)

                nc.gpsimd.memset(qd[:, :, :, :], 0.0).then_inc(S["qd_zero"], 1)

                def rotated(i, c):
                    g = b * NQ + i
                    pool.wait_ge(S["rope_done"], 4 * g + c + 1)
                    pool.wait_ge(S["st_done"], 4 * g + c + 1)
                    tt(qk[:, c, :, 0:HD], rope1[:, c, :, :], rope2[:, c, :, :], ALU.add).then_inc(S["qk_ready"], 1)

                def value_weights(i, p):
                    g = b * NQ + i
                    pair = slice(2 * p, 2 * p + 2)
                    pool.wait_ge(dN.sem, dN.value(g, f"nrec{p}"))
                    at = bass.ds(4 * i + 2 * p, 2)
                    rk = nrm[:, pair, HL:2 * HL]
                    lK.mark(tt(ck[:, pair, :, 0], es[:, 0:HL, at].rearrange("p h c -> p c h"), rk, ALU.mult), f"k0{p}")
                    lK.mark(tt(ck[:, pair, :, 1], es[:, HL:2 * HL, at].rearrange("p h c -> p c h"), rk, ALU.mult),
                            f"k1{p}")
                    lK.mark(cp(ck[:, pair, :, 2], rk), f"k2{p}")

                def weighted(i, p):
                    g = b * NQ + i
                    pool.wait_ge(S["v_out"], 2 * g + p + 1)
                    pool.wait_ge(lK.sem, lK.value(g, f"k2{p}"))
                    for c in (2 * p, 2 * p + 1):
                        tt(v3[:, c, :, :, :], spread(vs[:, c, :].rearrange("p (h d) -> p h d", h=HL), 2, 3),
                           spread(ck[:, c, :, :], 3, HD), ALU.mult).then_inc(S["v3_ready"], 1)

                def output_weights(i):
                    for j in range(3):
                        lK.mark(tt(cq[:, :, :, j], coef[:, j, :, bass.ds(4 * i, 4)].rearrange("p h c -> p c h"),
                                   nrm[:, :, 0:HL], ALU.mult), f"q{j}")
                    pool.wait_ge(lK.sem, lK.value(b * NQ + i, "q2"))
                    pool.sem_inc(S["c_ready"], 1)

                def pair_of(p):
                    return (o3[:, 2 * p:2 * p + 2, :, :, :],
                            osum[:, 2 * p:2 * p + 2, :].rearrange("p c (h d) -> p c h d", h=HL),
                            ost[:, 2 * p:2 * p + 2, :])

                def summed(i, p):
                    g = b * NQ + i
                    o, s, _ = pair_of(p)
                    pool.wait_ge(S["o_out"], 4 * g + 2 * p + 3)
                    for c in range(2):
                        m = tt(s[:, c], o[:, c, :, 0, :], o[:, c, :, 1, :], ALU.add)
                    lA.mark(m, f"a{p}")
                    pool.wait_ge(lA.sem, lA.value(g, f"a{p}"))
                    for c in range(2):
                        m = tt(s[:, c], s[:, c], o[:, c, :, 2, :], ALU.add)
                    m.then_inc(S["osum_ready"], 1)

                def centred(i, p):
                    _, s, mid = pair_of(p)
                    pool.wait_ge(dL.sem, dL.value(b * NQ + i, f"mean{p}"))
                    tt(s, s, spread(mid, 3, HD), ALU.add).then_inc(S["ctr_ready"], 1)

                def normal(i, p):
                    g = b * NQ + i
                    _, s, mid = pair_of(p)
                    pool.wait_ge(dL.sem, dL.value(g, f"rec{p}"))
                    pool.wait_ge(S["ctr_ready"], 2 * g + p + 1)
                    tt(s, s, spread(mid, 3, HD), ALU.mult).then_inc(S["oln_ready"], 1)

                def stage_h(i, first=False):
                    if not first:
                        summed(i - 1, 1)
                    rotated(i, 0)
                    if not first:
                        centred(i - 1, 1)
                    rotated(i, 1)
                    if not first:
                        normal(i - 1, 1)
                    rotated(i, 2)
                    rotated(i, 3)
                    value_weights(i, 0)
                    weighted(i, 0)
                    value_weights(i, 1)
                    output_weights(i)
                    weighted(i, 1)
                    summed(i, 0)
                    centred(i, 0)
                    normal(i, 0)

                stage_h(0, first=True)
                with pool.Fori(1, NQ) as i:
                    stage_h(i)
                summed(NQ - 1, 1)
                centred(NQ - 1, 1)
                normal(NQ - 1, 1)
                pool.wait_ge(S["x_kept"], NQ * b + NQ + 1)
                hold(pool)
                with pool.Fori(0, NQ) as i:
                    for p in range(2):
                        pool.wait_ge(S["res_ready"], 2 * (b * NQ + i) + p + 1)
                        tt(xo[:, 2 * p:2 * p + 2, :], ch(hx, i, 2 * p, 2), spread(w("lnw")[0:T], 1, 2), ALU.mult)\
                            .then_inc(S["xo_ready"], 1)
            pool.wait_ge(S["index_ready"], 1)
            pool.wait_ge(S["rows_written"], 16 * NQ * nb + 16)
            pool.wait_ge(S["out_written"], 16 * NQ * nb + 16)

            def gather(e, s, n):
                cp(gi[s][:, :], gidx[:, bass.ds(e, 1), :].rearrange("p a b -> p (a b)")).then_inc(S["gi_ready"], 1)
                pool.wait_ge(S["gi_ready"], n + 1)
                hold(pool)
                for t in range(B // 2):
                    pool.indirect_dma_start(mrow[s][:, t, :], None, rows,
                                            bass.IndirectOffsetOnAxis(ap=gi[s][:, t:t + 1], axis=0))\
                        .then_inc(S[f"gathered{s}"], 16)

            def scatter(e, k2, s, first=False):
                if not first:
                    pool.wait_ge(S[f"scattered{s}"], 64 * k2)
                cp(si[s][:, :], sidx[:, bass.ds(e, 1), :].rearrange("p a b -> p (a b)")).then_inc(S["si_ready"], 1)
                pool.wait_ge(S["si_ready"], e + 1)
                pool.wait_ge(S["moe_y"], 2 * e + 4)
                hold(pool)
                for t in range(B // 2):
                    pool.indirect_dma_start(out, bass.IndirectOffsetOnAxis(ap=si[s][:, t:t + 1], axis=0),
                                            my[s][:, t, :], None, bounds_check=nb * L - 1, oob_is_err=False)\
                        .then_inc(S[f"scattered{s}"], 16)

            for s in range(2):
                gather(s, s, s)
            for s in range(2):
                scatter(s, 0, s, first=True)
                gather(s + 2, s, s + 2)
            with pool.Fori(0, E // 2 - 1) as k:
                for s in range(2):
                    e = 2 * k + 2 + s
                    scatter(e, k + 1, s)
                    gather(e + 2, s, e + 2)
            for s in range(2):
                pool.wait_ge(S[f"gathered{s}"], 64 * (E // 2 + 1))
                pool.wait_ge(S[f"scattered{s}"], 64 * (E // 2))


def _planes(x):
    n = x.shape[0]
    planes = np.zeros((n, 2, CIN, 3, OUTW + 1, OUTW), x.dtype)
    for parity, rows in ((0, x[:, :, 1::2]), (1, x[:, :, 0::2])):
        at = slice(1, OUTW + 1) if parity == 0 else slice(0, OUTW)
        planes[:, parity, :, 0, at, 1:] = rows[..., 1:-1:2]
        planes[:, parity, :, 1, at] = rows[..., 0::2]
        planes[:, parity, :, 2, at] = rows[..., 1::2]
    return planes.reshape(n, 2 * CIN, 3, (OUTW + 1) * OUTW)


def _ktiles(m, size):
    k, n = m.shape
    return np.transpose(m.reshape(k // size, size, n), (1, 0, 2)).reshape(size, -1)


def _packed(a):
    conv = a["L0_tok_W"].reshape(D, CIN, 3, 3)
    taps = np.transpose(conv, (2, 3, 1, 0))
    qkv = a["L0_attn_W_qkv"].reshape(D, D, 3)
    gate = np.transpose(a["L1_attn_Wg"].reshape(HL, 3, D), (1, 0, 2))
    heads = np.arange(DH) // (D // HA)
    tok = np.arange(T, dtype=np.float32)
    inv = (1.0 / 10000.0 ** (np.arange(0, HD, 2, dtype=np.float32) / np.float32(HD))).astype(np.float32)
    ang = np.arange(L, dtype=np.float32)[:, None] * inv[None, :]
    sign = np.where(np.arange(HD // 2) < HD // 4, -1.0, 1.0).astype(np.float32)

    def table(f, sg):
        t = f(ang).astype(np.float32) * sg
        return np.transpose(t.reshape(NC, T, HD // 2), (1, 0, 2)).reshape(T, -1)

    def lanes(v, n=T):
        return np.broadcast_to(np.asarray(v).reshape(1, -1), (n, np.asarray(v).size))

    src = [(n // 2, 3 + n % 2) for n in range(NCLS)]
    out_b = np.stack([np.concatenate([a["L0_ffn_atom_out_b"][r], a["L0_ffn_atom_out_b"][l]]) for l, r in src])
    reset = np.ones((E, NC), np.float32)
    reset[:, 0] = 0.0
    eps = np.zeros((128, 2), np.float32)
    eps[:, 0], eps[:, 1] = 1e-5, 1e-6
    chunk = np.arange(NC, dtype=np.float32)
    parts = {
        "conv01": np.transpose(taps[0:2], (0, 2, 1, 3)).reshape(128, 3 * D),
        "conv2": np.transpose(taps[2], (1, 0, 2)).reshape(CIN, 3 * D),
        "tok_b": lanes(a["L0_tok_b"]),
        "wq0": _ktiles(qkv[:, :, 0], DH), "wk0": _ktiles(qkv[:, :, 1], DH), "wvT": _ktiles(qkv[:, :, 2].T, DH),
        "wproj": _ktiles(a["L0_attn_W_proj"], DH), "bproj": lanes(a["L0_attn_b_proj"]),
        "temp": np.repeat(a["L0_attn_temp"].reshape(HA), D // HA).reshape(2, DH).T,
        "offblock": np.where(heads[:, None] == heads[None, :], 0.0, NEG).astype(np.float32),
        "fc1": _ktiles(a["L0_ffn_fc1_w"].T, DH), "fc1_b": a["L0_ffn_fc1_b"].reshape(FT, 128).T,
        "fc2": _ktiles(a["L0_ffn_fc2_w"].T, 128), "fc2_b": lanes(a["L0_ffn_fc2_b"]),
        "wqkv": _ktiles(np.concatenate([a["L1_attn_Wq"], a["L1_attn_Wk"], a["L1_attn_Wv"]]).T, DH),
        "wug": _ktiles(np.concatenate([a["L1_attn_Wu"], gate[0], gate[1]]).T, DH),
        "wo": _ktiles(a["L1_attn_Wo"].T, DH),
        "mu": lanes(a["L1_attn_prior_mu"]), "logtau": lanes(a["L1_attn_prior_log_tau"]),
        "lnw": lanes(a["L1_ffn_ln_w"], 128), "lnwT": a["L1_ffn_ln_w"].reshape(2, DH).T,
        "router": _ktiles(a["L1_ffn_w_router"], DH),
        "ident": np.eye(128, dtype=np.float32), "tri": np.triu(np.ones((T, T), np.float32)),
        "ones": np.ones((128, 128), np.float32), "zeros": np.zeros((128, ROW), np.float32),
        "reset": lanes(reset), "cos": table(np.cos, 1.0), "sin": table(np.sin, sign),
        "pos": chunk[None, :] * T + tok[:, None] + 1, "iotae": lanes(np.arange(E, dtype=np.float32)),
        "iota128": lanes(np.arange(128, dtype=np.float32)),
        "tokid": np.arange(B * NC, dtype=np.float32)[None, :] * T + tok[:, None] + 1,
        "poff": lanes(CAP * (np.arange(B) % 2) - 1.0), "eps": eps,
        "gate": a["L0_ffn_gate_pair"].reshape(NCLS, 2 * D), "bal": a["L0_ffn_balance_bias"], "out_b": out_b,
        "in_b": np.transpose(a["L0_ffn_atom_in_b"].reshape(NAT, FT, 128), (2, 0, 1)).reshape(128, -1),
        "atom_in": _ktiles(a["L0_ffn_atom_in_w"].reshape(NAT * F, D).T, DH),
        "atom_out": np.transpose(a["L0_ffn_atom_out_w"].reshape(NAT, D, FT, 128), (3, 0, 2, 1)).reshape(128, -1),
    }
    where, total = pack_columns()
    packed = np.zeros((128, total), np.float32)
    for name, (p, at, n) in where.items():
        assert parts[name].shape == (p, n), (name, parts[name].shape)
        packed[:p, at:at + n] = parts[name]
    return packed


def arrays(inputs):
    a = {k: np.asarray(v) for k, v in inputs.items()}
    wi, wo_e = a["L1_ffn_wi"], a["L1_ffn_wo"]
    return {
        "xin": _planes(a["x"]), "packed": _packed(a),
        "wi": np.ascontiguousarray(np.transpose(wi.reshape(E, 2, DH, F), (0, 2, 1, 3)).reshape(E, DH, 2 * F)),
        "wo_e": np.ascontiguousarray(np.transpose(wo_e.reshape(E, FT, 128, D), (0, 2, 1, 3)).reshape(E, 128, FT * D)),
    }


def kernel(**inputs):
    import concourse.bacc as bacc
    from concourse.bass_utils import run_bass_kernel_spmd

    nc = bacc.Bacc("TRN2", target_bir_lowering=False, num_devices=1)
    data = arrays(inputs)
    args = [nc.dram_tensor(n, data[n].shape, F32, kind="ExternalInput").ap() for n in ("xin", "packed")]
    out = nc.dram_tensor("out", (B * L, D), F32, kind="ExternalOutput").ap()
    rows = nc.dram_tensor("rows", (B * L + 1, ROW), F32).ap()
    weights = [nc.dram_tensor(n, data[n].shape, F32, kind="ExternalInput").ap() for n in ("wi", "wo_e")]
    build_tower(nc, *args, out, rows, *weights)
    r = run_bass_kernel_spmd(nc, [data], core_ids=[0])
    return r.results[0]["out"].reshape(B, L, D)
```
